# Optimizing a Trainium2 kernel written in Bass

```python
import numpy as np
import jax
import jax.numpy as jnp

def _softmax(x, axis=-1):
    return jax.nn.softmax(x, axis=axis)

def _gelu(x):
    return jax.nn.gelu(x, approximate=True)

def _silu(x):
    return jax.nn.silu(x)

def _sigmoid(x):
    return jax.nn.sigmoid(x)

def _layernorm(x, axis=-1, eps=1e-05):
    m = jnp.mean(x, axis=axis, keepdims=True)
    v = jnp.var(x, axis=axis, keepdims=True)
    return (x - m) / jnp.sqrt(v + eps)

def _scatter_add(tgt, idx, src, axis=0):
    return tgt.at[idx].add(src)

def _segment_sum(src, seg, n):
    return jax.ops.segment_sum(src, seg, n)
kernel_name = 'mk_gnn_ffn_d2_gnn_r16_b53278'

def setup_inputs(seed: int=0):
    np.random.seed(seed)
    _w = jnp.asarray

    def _rec_inputs():
        import jax
        import jax.numpy as jnp
        _gk = jax.random.key(seed)
        x = -0.0003713 + 1 * jax.random.normal(jax.random.fold_in(_gk, 1), (3125, 256), jnp.float32)
        _s = jax.random.randint(jax.random.fold_in(_gk, 2), (25000,), 0, 3125, jnp.int32)
        _d = jax.random.randint(jax.random.fold_in(_gk, 3), (25000,), 0, 3125, jnp.int32)
        _loop = jnp.arange(3125, dtype=jnp.int32)
        src = jnp.concatenate([_s, _d, _loop])
        dst = jnp.concatenate([_d, _s, _loop])
        _o = jnp.argsort(dst, stable=True)
        src = src[_o]
        dst = dst[_o]
        edge_type_200 = jax.random.randint(jax.random.fold_in(_gk, 13), (53125,), 0, 200, jnp.int32)
        edge_weight = jax.random.uniform(jax.random.fold_in(_gk, 14), (53125,), jnp.float32, 0.0, 0.999998)
        return (x, src, dst, edge_type_200, edge_weight)
    x, src, dst, edge_type_200, edge_weight = _rec_inputs()

    def _L0_gnn_setup():
        import jax, jax.numpy as jnp
        import numpy as np
        N_NODES = 3125
        N_EDGES = 50000
        H, D_IN, D_OUT = (4, 256, 64)
        key = jax.random.key(seed)
        ks = jax.random.split(key, 7)
        x = jax.random.normal(ks[0], (N_NODES, D_IN), dtype=jnp.float32)
        idx = jax.random.randint(ks[1], (2, N_EDGES), 0, N_NODES, dtype=jnp.int32)
        elem = jax.random.uniform(ks[2], (N_EDGES,), dtype=jnp.float32)
        Ws = jax.random.normal(ks[3], (H, D_IN, D_OUT), dtype=jnp.float32) * 0.05
        bs = jax.random.normal(ks[4], (H, D_OUT), dtype=jnp.float32) * 0.05
        aw = jax.random.normal(ks[5], (H, 2 * D_OUT + 1), dtype=jnp.float32) * 0.05
        ab = jax.random.normal(ks[6], (H,), dtype=jnp.float32) * 0.05
        return {'x': x, 'idx': idx, 'elem': elem, 'Ws': Ws, 'bs': bs, 'aw': aw, 'ab': ab}
    _L0_gnn_all = _L0_gnn_setup()
    _L0_gnn_in = {k: v for k, v in _L0_gnn_all.items() if k in ('Ws', 'bs', 'aw', 'ab')}
    del _L0_gnn_all

    def _L0_ffn_setup():
        import jax, jax.numpy as jnp
        import numpy as np
        D_MODEL = 256
        N_EXPERTS = 16
        HIDDEN = 512
        SCALE = 0.02
        key = jax.random.key(seed)
        ks = jax.random.split(key, 5)
        x = jax.random.normal(ks[0], (4, 512, D_MODEL), dtype=jnp.float32)
        gate_w = jax.random.normal(ks[1], (D_MODEL, N_EXPERTS), dtype=jnp.float32) * SCALE
        gate_b = jnp.zeros((N_EXPERTS,), dtype=jnp.float32)
        w1 = jax.random.normal(ks[2], (N_EXPERTS, D_MODEL, HIDDEN), dtype=jnp.float32) * SCALE
        w2 = jax.random.normal(ks[3], (N_EXPERTS, D_MODEL, HIDDEN), dtype=jnp.float32) * SCALE
        w3 = jax.random.normal(ks[4], (N_EXPERTS, HIDDEN, D_MODEL), dtype=jnp.float32) * SCALE
        return {'x': x, 'gate_w': gate_w, 'gate_b': gate_b, 'w1': w1, 'w2': w2, 'w3': w3}
    _L0_ffn_all = _L0_ffn_setup()
    _L0_ffn_in = {k: v for k, v in _L0_ffn_all.items() if k in ('gate_w', 'gate_b', 'w1', 'w2', 'w3')}
    del _L0_ffn_all

    def _L1_gnn_setup():
        import jax, jax.numpy as jnp
        import numpy as np
        N, D, E, R = (3125, 256, 40000, 200)
        if __name__ == '__main__':
            out = reference(**setup_inputs())
            print(out.shape, out.dtype)
        key = jax.random.key(seed)
        ks = jax.random.split(key, 12)

        def xavier(k, shape, gain=np.sqrt(2.0)):
            fan_in, fan_out = (shape[0], shape[1])
            bound = gain * np.sqrt(6.0 / (fan_in + fan_out))
            return jax.random.uniform(k, shape, jnp.float32, -bound, bound)
        return {'h': jax.random.normal(ks[0], (N, D), jnp.float32), 'rel_emb': jax.random.normal(ks[1], (R, D), jnp.float32) * 0.1, 'weight_neighbor': xavier(ks[2], (D, D)), 'a': xavier(ks[3], (3 * D, 1)), 'W3': xavier(ks[4], (3 * D, 3 * D)), 'loop_weight': xavier(ks[5], (D, D)), 'evolve_loop_weight': xavier(ks[6], (D, D)), 'src': jax.random.randint(ks[7], (E,), 0, N, jnp.int32), 'dst': jax.random.randint(ks[8], (E,), 0, N, jnp.int32), 'etype': jax.random.randint(ks[9], (E,), 0, R, jnp.int32)}
    _L1_gnn_all = _L1_gnn_setup()
    _L1_gnn_in = {k: v for k, v in _L1_gnn_all.items() if k in ('rel_emb', 'weight_neighbor', 'a', 'W3', 'loop_weight', 'evolve_loop_weight')}
    del _L1_gnn_all

    def _L1_ffn_setup():
        import jax, jax.numpy as jnp
        import numpy as np
        B, S, D = (8, 256, 256)
        H = 4 * D
        CAPACITY = 0.5
        key = jax.random.key(seed)
        ks = jax.random.split(key, 6)
        x = jax.random.normal(ks[0], (B, S, D), dtype=jnp.float32)
        attention_mask = jnp.zeros((B, 1, 1, S), dtype=jnp.float32)
        wr = jax.random.normal(ks[1], (D, 1), dtype=jnp.float32) * 0.02
        br = jnp.zeros((1,), dtype=jnp.float32)
        w1 = jax.random.normal(ks[2], (D, H), dtype=jnp.float32) * 0.02
        b1 = jnp.zeros((H,), dtype=jnp.float32)
        w2 = jax.random.normal(ks[3], (H, D), dtype=jnp.float32) * 0.02
        b2 = jnp.zeros((D,), dtype=jnp.float32)
        return {'x': x, 'attention_mask': attention_mask, 'wr': wr, 'br': br, 'w1': w1, 'b1': b1, 'w2': w2, 'b2': b2}
    _L1_ffn_all = _L1_ffn_setup()
    _L1_ffn_in = {k: v for k, v in _L1_ffn_all.items() if k in ('attention_mask', 'wr', 'br', 'w1', 'b1', 'w2', 'b2')}
    del _L1_ffn_all
    return {'x': x, 'src': src, 'dst': dst, 'edge_type_200': edge_type_200, 'edge_weight': edge_weight, 'L0_gnn_Ws': _L0_gnn_in['Ws'], 'L0_gnn_bs': _L0_gnn_in['bs'], 'L0_gnn_aw': _L0_gnn_in['aw'], 'L0_gnn_ab': _L0_gnn_in['ab'], 'L0_ffn_gate_w': _L0_ffn_in['gate_w'], 'L0_ffn_gate_b': _L0_ffn_in['gate_b'], 'L0_ffn_w1': _L0_ffn_in['w1'], 'L0_ffn_w2': _L0_ffn_in['w2'], 'L0_ffn_w3': _L0_ffn_in['w3'], 'L1_gnn_rel_emb': _L1_gnn_in['rel_emb'], 'L1_gnn_weight_neighbor': _L1_gnn_in['weight_neighbor'], 'L1_gnn_a': _L1_gnn_in['a'], 'L1_gnn_W3': _L1_gnn_in['W3'], 'L1_gnn_loop_weight': _L1_gnn_in['loop_weight'], 'L1_gnn_evolve_loop_weight': _L1_gnn_in['evolve_loop_weight'], 'L1_ffn_attention_mask': _L1_ffn_in['attention_mask'], 'L1_ffn_wr': _L1_ffn_in['wr'], 'L1_ffn_br': _L1_ffn_in['br'], 'L1_ffn_w1': _L1_ffn_in['w1'], 'L1_ffn_b1': _L1_ffn_in['b1'], 'L1_ffn_w2': _L1_ffn_in['w2'], 'L1_ffn_b2': _L1_ffn_in['b2']}

def reference(x, src, dst, edge_type_200, edge_weight, L0_gnn_Ws, L0_gnn_bs, L0_gnn_aw, L0_gnn_ab, L0_ffn_gate_w, L0_ffn_gate_b, L0_ffn_w1, L0_ffn_w2, L0_ffn_w3, L1_gnn_rel_emb, L1_gnn_weight_neighbor, L1_gnn_a, L1_gnn_W3, L1_gnn_loop_weight, L1_gnn_evolve_loop_weight, L1_ffn_attention_mask, L1_ffn_wr, L1_ffn_br, L1_ffn_w1, L1_ffn_b1, L1_ffn_w2, L1_ffn_b2):
    import jax
    import jax.numpy as jnp

    def _L0_gnn_ref(x, idx, elem, Ws, bs, aw, ab):
        import jax, jax.numpy as jnp
        import numpy as np
        N_NODES = 3125
        N_EDGES = 50000
        H, D_IN, D_OUT = (4, 256, 64)
        N = x.shape[0]
        O = Ws.shape[-1]
        feats = jnp.einsum('nd,hdo->hno', x, Ws) + bs[:, None, :]
        aw_src, aw_dst, aw_e = (aw[:, :O], aw[:, O:2 * O], aw[:, 2 * O])
        a_s = jnp.einsum('hno,ho->hn', feats, aw_src)
        a_d = jnp.einsum('hno,ho->hn', feats, aw_dst)
        src, dst = (idx[0], idx[1])
        score = a_s[:, src] + a_d[:, dst] + aw_e[:, None] * elem[None, :] + ab[:, None]
        w = jnp.exp(-jax.nn.relu(score / 20.0))
        dst_f = feats[:, dst]
        seg = lambda vals: jax.ops.segment_sum(vals, src, num_segments=N)
        pooled = jax.vmap(lambda wi, fi: seg(wi[:, None] * fi))(w, dst_f)
        row_sum = jax.vmap(lambda wi: seg(wi))(w)
        out = pooled / row_sum[:, :, None]
        return jnp.transpose(out, (1, 0, 2)).reshape(N, H * O)

    def _L0_ffn_ref(x, gate_w, gate_b, w1, w2, w3):
        import jax, jax.numpy as jnp
        import numpy as np
        D_MODEL = 256
        N_EXPERTS = 16
        HIDDEN = 512
        SCALE = 0.02
        n_experts = w1.shape[0]
        logits = jnp.einsum('bsd,de->bse', x, gate_w) + gate_b
        probs = jax.nn.softmax(logits, axis=-1)
        top_probs, top_idx = jax.lax.top_k(probs, 2)
        top_probs = top_probs / jnp.sum(top_probs, axis=-1, keepdims=True)
        dispatch = jnp.sum(jax.nn.one_hot(top_idx, n_experts, dtype=x.dtype) * top_probs[..., None], axis=-2)
        h1 = jnp.einsum('bsd,edh->bseh', x, w1)
        h2 = jnp.einsum('bsd,edh->bseh', x, w2)
        hidden = jax.nn.silu(h1) * h2
        expert_out = jnp.einsum('bseh,eho->bseo', hidden, w3)
        return jnp.einsum('bseo,bse->bso', expert_out, dispatch)

    def _L1_gnn_ref(h, rel_emb, weight_neighbor, a, W3, loop_weight, evolve_loop_weight, src, dst, etype):
        import jax, jax.numpy as jnp
        import numpy as np
        N, D, E, R = (3125, 256, 40000, 200)
        if __name__ == '__main__':
            out = reference(**setup_inputs())
            print(out.shape, out.dtype)
        n, d = h.shape
        e = src.shape[0]
        in_deg = jax.ops.segment_sum(jnp.ones((e,), h.dtype), dst, num_segments=n)
        loop_message = jnp.where((in_deg > 0)[:, None], h @ loop_weight, h @ evolve_loop_weight)
        W = (W3 @ a)[:, 0]
        w_src, w_dst, w_rel = (W[:d], W[d:2 * d], W[2 * d:])
        rel_e = rel_emb[etype]
        score = h[src] @ w_src + h[dst] @ w_dst + rel_e @ w_rel
        alpha = jnp.exp(jax.nn.leaky_relu(score))[:, None]
        alpha = alpha / jnp.sum(alpha, axis=1, keepdims=True)
        msg = (h[src] + rel_e) @ weight_neighbor * alpha
        agg = jax.ops.segment_sum(msg, dst, num_segments=n)
        node_repr = jax.nn.relu(agg) + loop_message
        return node_repr

    def _L1_ffn_ref(x, attention_mask, wr, br, w1, b1, w2, b2):
        import jax, jax.numpy as jnp
        import numpy as np
        B, S, D = (8, 256, 256)
        H = 4 * D
        CAPACITY = 0.5
        b, s, d = x.shape
        weights = (jnp.einsum('bsd,do->bso', x, wr) + br)[..., 0]
        k = max(1, int(CAPACITY * s))
        kk = k - 1 if k > 1 else 1
        _, idx = jax.lax.top_k(weights, k)
        sel_idx = idx[:, :kk]
        sel = jnp.take_along_axis(x, sel_idx[:, :, None], axis=1)
        h = jax.nn.gelu(jnp.einsum('bkd,dh->bkh', sel, w1) + b1)
        y = jnp.einsum('bkh,hd->bkd', h, w2) + b2
        w_sel = jnp.take_along_axis(weights, sel_idx, axis=1)
        y = y * w_sel[..., None]
        batch_idx = jnp.arange(b)[:, None]
        processed = jnp.zeros_like(x).at[batch_idx, sel_idx].set(y)
        return processed + x
    edge_index = jnp.stack([src, dst])
    x = x + _L0_gnn_ref(_layernorm(x, axis=-1), edge_index, edge_weight, L0_gnn_Ws, L0_gnn_bs, L0_gnn_aw, L0_gnn_ab)
    x = x + _L0_ffn_ref(_layernorm(x, axis=-1)[None], L0_ffn_gate_w, L0_ffn_gate_b, L0_ffn_w1, L0_ffn_w2, L0_ffn_w3)[0]
    x = x + _L1_gnn_ref(_layernorm(x, axis=-1), L1_gnn_rel_emb, L1_gnn_weight_neighbor, L1_gnn_a, L1_gnn_W3, L1_gnn_loop_weight, L1_gnn_evolve_loop_weight, src, dst, edge_type_200)
    x = x + _L1_ffn_ref(_layernorm(x, axis=-1)[None], L1_ffn_attention_mask, L1_ffn_wr, L1_ffn_br, L1_ffn_w1, L1_ffn_b1, L1_ffn_w2, L1_ffn_b2)[0]
    return x

_drawn_inputs = setup_inputs


def setup_inputs(seed=0):
    import zlib

    import numpy as np

    out = dict(_drawn_inputs(seed))
    spreads = {'L0_ffn_gate_b': (0.0, 0.711), 'L1_ffn_b1': (0.0, 0.8), 'L1_ffn_b2': (0.0, 0.8)}
    factors = {'edge_weight': 8.0,
     'L0_gnn_aw': 8.0,
     'L0_gnn_ab': 8.0,
     'L0_ffn_gate_w': 3.64,
     'L0_ffn_w1': 3.353,
     'L0_ffn_w2': 3.306,
     'L0_ffn_w3': 3.303,
     'L1_ffn_wr': 8.0,
     'L1_ffn_w1': 8.0,
     'L1_ffn_w2': 8.0}
    for name, (base, spread) in spreads.items():
        noise = np.random.default_rng([zlib.crc32(name.encode()), seed]).standard_normal(out[name].shape)
        drawn = base * np.exp(spread * noise) if base else spread * noise
        out[name] = jnp.asarray(drawn.astype(out[name].dtype))
    for name, factor in factors.items():
        out[name] = (out[name] * factor).astype(out[name].dtype)
    return out
```

```python
from contextlib import ExitStack

import concourse.bass as bass
from concourse import mybir

F32 = mybir.dt.float32
I32 = mybir.dt.int32
ALU = mybir.AluOpType
ACT = mybir.ActivationFunctionType
AX = mybir.AxisListType

P = 128
DEPTH = 4
TPG = 4
TPU = 2


class Chain:

    def __init__(self, eng, sem):
        self.eng, self.sem, self.n, self.i, self.per = eng, sem, 0, None, 0

    def value(self):
        return self.n if self.i is None else self.i * self.per + (self.n - self.start * self.per)

    def link(self, ins):
        ins.then_inc(self.sem, 1)
        self.n += 1
        self.eng.wait_ge(self.sem, self.value())

    def enter(self, i, per, start=0):
        self.i, self.per, self.at, self.start = i, per, self.n, start

    def leave(self, end):
        assert self.n - self.at == self.per, (self.n - self.at, self.per)
        self.n, self.i = self.at + self.per * (end - self.start), None


def build(nc, a, out, debug=None):
    N, D = a["x"].shape
    E = a["src"].shape[0]
    NT = -(-N // P)
    LAST = N - (NT - 1) * P
    EP = next(p for p in range(P, 0, -1) if E % p == 0)
    EC = E // EP
    H, _, O = a["L0_gnn_Ws"].shape
    R = a["L1_gnn_rel_emb"].shape[0]
    NE, _, FH = a["L0_ffn_w1"].shape
    FF = a["L1_ffn_w1"].shape[1]
    KD = D // P
    UNIT = TPU * P
    UNITS = (E + NT * (UNIT - 1)) // UNIT
    GROUPS = -(-UNITS * TPU // TPG)
    GROUPS = -(-GROUPS // DEPTH) * DEPTH
    ST = GROUPS * TPG
    UNITS = ST // TPU
    MT = (2 * N + NE * (P - 1)) // P
    MT += MT % 2
    W0 = D + 2 * H
    A0 = D + H
    W1 = D + 2
    A1 = W1 + R
    CH = 5
    NCH = NT // CH
    SELECTED = max(1, N // 2) - 1
    assert NT % CH == 0 and D == 2 * P and H * O == D and R > P

    ctx = ExitStack()

    def dram(name, shape, dt):
        if debug and name in debug:
            return nc.dram_tensor(name, shape, dt, kind="ExternalOutput").ap()
        return nc.dram_tensor(name, shape, dt).ap()

    rec_d = [dram(f"records{l}", (P * ST, 4), I32) for l in range(2)]
    table0 = dram("table0", (NT * P, W0), F32)
    table1 = dram("table1", (NT * P, W1), F32)
    expert_in = dram("expert_in", (MT * P, D), F32)
    expert_out = dram("expert_out", (MT * P, D), F32)
    score_d = dram("score_d", (NT * P, 1), F32)
    dbg = dram("dbg", (P, NT * D), F32) if debug else None

    def sb(name, shape, dt=F32, c=ctx):
        return c.enter_context(nc.sbuf_tensor(name, shape, dt))

    def ps(name, shape, c):
        return c.enter_context(nc.psum_tensor(name, shape, F32))

    phase_sems = []

    def sem(name):
        phase_sems.append(nc.alloc_semaphore(name=name))
        return phase_sems[-1]

    def end_phase():
        nc.clear_and_free_semaphores(list(phase_sems))
        phase_sems.clear()
        nc.all_engine_barrier()

    X = sb("X", [P, NT, D])
    rec_s = [sb(f"rec_s{l}", [EP, EC, 4], I32) for l in range(2)]
    slot = [sb(f"slot{l}", [EP, EC], I32) for l in range(2)]
    unit_tile = [sb(f"unit_tile{l}", [P, UNITS], I32) for l in range(2)]
    ident = sb("ident", [P, P])
    iota = sb("iota", [P, R])
    ones = sb("ones", [P, P])
    before = sb("before", [P, P])
    padrow = sb("padrow", [P, NT])
    eps = sb("eps", [P, 1])
    turn = {e: ctx.enter_context(nc.semaphore(f"turn_{e}")) for e in ("pool", "dve", "act", "sp")}

    def hold(eng, name):
        eng.sem_inc(turn[name], 1)

    class Dense:

        def __init__(self, tag, c, width):
            self.width = width
            self.xc = sb(tag + "_xc", [P, CH, D], c=c)
            self.xn = sb(tag + "_xn", [P, CH, D], c=c)
            self.junk = sb(tag + "_junk", [P, D], c=c)
            self.st = sb(tag + "_st", [P, 5, CH], c=c)
            self.xT = sb(tag + "_xT", [P, CH, KD, P], c=c)
            self.psT = ps(tag + "_psT", [P, 2, 512], c)
            self.psF = ps(tag + "_psF", [P, 2, 512], c)
            (self.centred, self.squared, self.std, self.normed, self.turned, self.turned_free, self.copied,
             self.product, self.product_free, self.xn_free, self.xT_free) = (
                sem(tag + "_" + n) for n in ("centred", "squared", "std", "normed", "turned", "turned_free", "copied",
                                             "product", "product_free", "xn_free", "xT_free"))

        def vector(self, dve, ch, c):
            x = X[:, bass.ds(c * CH, CH), :]
            st = self.st
            hold(dve, "dve")
            ch.link(dve.tensor_reduce(st[:, 0, :], x, AX.X, ALU.add))
            ch.link(dve.tensor_scalar(st[:, 1, :], st[:, 0, :], -1.0 / D, None, ALU.mult))
            dve.tensor_tensor(self.xc[:, :, :], x, st[:, 1, :].unsqueeze(2).to_broadcast([P, CH, D]),
                              ALU.add).then_inc(self.centred, 1)
            dve.wait_ge(self.std, c + 1)
            ch.link(dve.reciprocal(st[:, 4, :], st[:, 3, :]))
            dve.wait_ge(self.xn_free, c + 1)
            dve.tensor_tensor(self.xn[:, :, :], self.xc[:, :, :],
                              st[:, 4, :].unsqueeze(2).to_broadcast([P, CH, D]), ALU.mult)\
               .then_inc(self.normed, 1)

        LINKS = 3

        def scalar_std(self, act, c):
            act.wait_ge(self.centred, c + 1)
            for k in range(CH):
                if k:
                    act.wait_ge(self.squared, c * CH + k)
                nc.scalar.activation(self.junk[:, :], self.xc[:, k, :], ACT.Square,
                                     accum_out=self.st[:, 2, k:k + 1]).then_inc(self.squared, 1)
            act.wait_ge(self.squared, c * CH + CH)
            nc.scalar.activation(self.st[:, 3, :], self.st[:, 2, :], ACT.Sqrt, bias=eps[:, :],
                                 scale=1.0 / D).then_inc(self.std, 1)

        def scalar_copy(self, act, c, k):
            act.wait_ge(self.turned, c * CH + k + 1)
            act.wait_ge(self.xT_free, c + 1)
            nc.scalar.activation(self.xT[:, k, :, :],
                                 self.psT[:, k % 2, 0:D].rearrange("p (a b) -> p a b", a=KD),
                                 ACT.Copy).then_inc(self.copied, 1)

        def free_at(self, c, k):
            return c * CH + (k if k < 1 else k - 1) + 1

        def transposes(self, pe, c, k):
            if k == 0:
                pe.wait_ge(self.normed, c + 1)
            pe.wait_ge(self.turned_free, self.free_at(c, k))
            for j in range(KD):
                ins = pe.transpose(self.psT[:, k % 2, j * P:(j + 1) * P], self.xn[:, k, j * P:(j + 1) * P],
                                   ident[:, :])
            ins.then_inc(self.turned, 1)
            if k == CH - 1:
                pe.wait_ge(self.turned, c * CH + CH)
                pe.sem_inc(self.xn_free, 1)

        def products(self, pe, c, k, weight):
            pe.wait_ge(self.copied, c * CH + k + 1)
            pe.wait_ge(self.product_free, self.free_at(c, k))
            for j in range(KD):
                ins = pe.matmul(self.psF[:, k % 2, 0:self.width], self.xT[:, k, j, :],
                                weight[:, j, 0:self.width], start=(j == 0), stop=(j == KD - 1))
            ins.then_inc(self.product, 1)
            if k == CH - 1:
                pe.wait_ge(self.product, c * CH + CH)
                pe.sem_inc(self.xT_free, 1)

        def credits_pe(self, pe):
            pe.sem_inc(self.xn_free, 1)
            pe.sem_inc(self.xT_free, 1)

        def credit_act(self, act):
            act.sem_inc(self.turned_free, 1)

        def credit_dve(self, dve):
            dve.sem_inc(self.product_free, 1)

        def run_pe(self, pe, weight, extra=None):
            self.credits_pe(pe)
            with pe.Fori(0, NCH) as c:
                for k in range(CH):
                    self.transposes(pe, c, k)
                    if k:
                        self.products(pe, c, k - 1, weight)
                        if extra:
                            extra(c, k - 1)
                self.products(pe, c, CH - 1, weight)
                if extra:
                    extra(c, CH - 1)

        def run_act(self, act, extra=None, tail=None):
            self.credit_act(act)
            with act.Fori(0, NCH) as c:
                self.scalar_std(act, c)
                if extra:
                    extra(c)
                for k in range(CH):
                    self.scalar_copy(act, c, k)
                    act.wait_ge(self.copied, c * CH + k + 1)
                    act.sem_inc(self.turned_free, 1)
                    if tail:
                        tail(c, k)

    class Sort:

        def __init__(self, tag, c, rows, cols, buckets, unit, units, oh=None, run=None):
            self.rows, self.cols, self.B, self.unit, self.units = rows, cols, buckets, unit, units
            self.oh = oh if oh is not None else sb(tag + "_oh", [rows, buckets, cols + 1], c=c)
            self.run = run if run is not None else sb(tag + "_run", [rows, buckets, cols + 1], c=c)
            self.tot = sb(tag + "_tot", [rows, buckets], c=c)
            self.small = sb(tag + "_small", [P, 8, buckets], c=c)
            self.smalli = sb(tag + "_smalli", [P, 2, buckets], I32, c=c)
            self.ucount = sb(tag + "_ucount", [P, units], c=c)
            self.psum = ps(tag + "_ps", [P, 512], c)
            self.totals, self.sums = sem(tag + "_totals"), sem(tag + "_sums")

        def tensor(self, pe):
            pe.wait_ge(self.totals, 1)
            pe.matmul(self.psum[0:P, 0:self.B], before[0:self.rows, :], self.tot[:, :], start=True, stop=True)
            pe.matmul(self.psum[0:P, self.B:2 * self.B], ones[0:self.rows, :], self.tot[:, :], start=True,
                      stop=True).then_inc(self.sums, 1)

        def vector(self, dve, link, bucket, tile_of_unit, where):
            B, rows, cols = self.B, self.rows, self.cols
            oh, run, s, si = self.oh, self.run, self.small, self.smalli
            full = [rows, B, cols]
            link(dve.tensor_tensor(oh[:, :, 1:], bucket.unsqueeze(1).to_broadcast(full),
                                   iota[0:rows, 0:B].unsqueeze(2).to_broadcast(full), ALU.is_equal))
            dve.tensor_reduce(self.tot[:, :], oh[:, :, 1:], AX.X, ALU.add).then_inc(self.totals, 1)
            dve.wait_ge(self.sums, 1)
            link(dve.tensor_scalar(si[:, 0, :], self.psum[:, B:2 * B], float(self.unit - 1), None, ALU.add))
            link(dve.tensor_scalar(si[:, 1, :], si[:, 0, :], self.unit.bit_length() - 1, None,
                                   ALU.arith_shift_right))
            link(dve.tensor_copy(s[:, 0, :], si[:, 1, :]))
            link(dve.tensor_tensor_scan(s[:, 1, :], s[:, 0, :], s[:, 0, :], 0.0, ALU.add, ALU.max))
            link(dve.tensor_tensor(s[:, 2, :], s[:, 1, :], s[:, 0, :], ALU.subtract))
            link(dve.scalar_tensor_tensor(s[:, 3, :], s[:, 2, :], float(self.unit), self.psum[:, 0:B],
                                          ALU.mult, ALU.add))
            link(dve.tensor_tensor(s[0:rows, 4, :], s[0:rows, 3, :], self.tot[:, :], ALU.add))
            link(dve.tensor_copy(oh[:, 0, 0:1], s[0:rows, 3, 0:1]))
            link(dve.tensor_tensor(oh[:, 1:, 0], s[0:rows, 3, 1:], s[0:rows, 4, 0:B - 1], ALU.subtract))
            flat = "p b c -> p (b c)"
            link(dve.tensor_tensor_scan(run[:, :, :].rearrange(flat), oh[:, :, :].rearrange(flat),
                                        oh[:, :, :].rearrange(flat), 0.0, ALU.add, ALU.max))
            link(dve.tensor_tensor(run[:, :, 1:], run[:, :, 1:], oh[:, :, 1:], ALU.mult))
            link(dve.tensor_reduce(where, run[:, :, 1:].rearrange("p b c -> p c b"), AX.X, ALU.max))
            link(dve.tensor_scalar(where, where, -1.0, 0.0, ALU.add, ALU.max))
            view = run[:, :, :].rearrange(flat)[:, 0:B * min(self.units, cols)]
            n = min(self.units, cols)
            for u in range(0, self.units, n):
                m = min(n, self.units - u)
                v = view[:, 0:B * m].rearrange("p (u b) -> p u b", b=B)
                link(dve.tensor_tensor(v, self.unumber[0:rows, u:u + m].unsqueeze(2).to_broadcast([rows, m, B]),
                                       s[0:rows, 2, :].unsqueeze(1).to_broadcast([rows, m, B]), ALU.is_ge))
                link(dve.tensor_reduce(self.ucount[0:rows, u:u + m], v, AX.X, ALU.add))
            link(dve.tensor_scalar(tile_of_unit, self.ucount[0:rows, :], -1.0, None, ALU.add))

    with ExitStack() as c:
        big = [sb(f"sort_{n}", [EP, NT, EC + 1], c=c) for n in ("oh", "run")]
        unumber = sb("unumber", [P, UNITS], c=c)
        sort = [Sort(f"sort{l}", c, EP, EC, NT, UNIT, UNITS, *big) for l in range(2)]
        for s in sort:
            s.unumber = unumber
        raw = sb("raw", [EP, 3, EC], I32, c=c)
        elem = sb("elem", [EP, EC], c=c)
        keyi = sb("keyi", [EP, EC], I32, c=c)
        keyf = sb("keyf", [EP, EC], c=c)
        wheref = sb("wheref", [EP, EC], c=c)
        slot_t = sb("slot_t", [EP, 3, EC], I32, c=c)
        ts = slot_t[:, :, :]
        blank = sb("blank", [P, ST, 4], I32, c=c)
        stage_slot = sb("stage_slot", [EP, 5, 17], I32, c=c)
        stage_rec = sb("stage_rec", [EP, 5, 17, 4], I32, c=c)

        loaded, xloaded, consts, zeroed = sem("edges_loaded"), sem("x_loaded"), sem("consts"), sem("x_zeroed")
        blanked, blank_ready, ready = sem("blanked"), sem("blank_ready"), [sem("slots0_ready"), sem("slots1_ready")]
        chain = sem("chain1")
        staged, landed = sem("staged"), [sem(f"rec_landed{b}") for b in range(5)]

        def scatter_records(pool, l, times_before):
            cols = EC // 25
            assert EC == 25 * cols and cols == 17
            base = 5 * times_before

            def turn(i, first):
                for b in range(5):
                    if not first:
                        pool.wait_ge(landed[b], (i + base) * (16 * cols))
                        hold(pool, "pool")
                    at = (i * 5 + b) * cols
                    nc.gpsimd.tensor_copy(stage_slot[:, b, :], slot[l][:, bass.ds(at, cols)]).then_inc(staged, 1)
                    nc.gpsimd.tensor_copy(stage_rec[:, b, :, :], rec_s[l][:, bass.ds(at, cols), :])\
                        .then_inc(staged, 1)
                    pool.wait_ge(staged, (i + base) * 10 + 2 * b + 2)
                    hold(pool, "pool")
                    for k in range(cols):
                        pool.indirect_dma_start(
                            out=rec_d[l], out_offset=bass.IndirectOffsetOnAxis(ap=stage_slot[:, b, k:k + 1], axis=0),
                            in_=stage_rec[:, b, k, :], in_offset=None).then_inc(landed[b], 16)
            if base == 0:
                turn(0, True)
            with pool.Fori(0 if base else 1, 5) as i:
                turn(i, False)
            for b in range(5):
                pool.wait_ge(landed[b], 16 * cols * (base + 5))

        dn = Dense("ln0", c, W0)
        wcat = sb("wcat", [P, KD, W0], c=c)
        awb = sb("awb", [P, H, 2 * O + 1], c=c)
        biasrow = sb("biasrow", [P, W0], c=c)
        awprod = sb("awprod", [P, H, O], c=c)
        frow = sb("frow", [P, 2, W0], c=c)
        wloaded, wready, fready, fstored = sem("wloaded"), sem("wready"), sem("fready"), [sem("fst0"), sem("fst1")]

        with nc.Block() as block:
            @block.sync
            def _(sp):
                flat = "(p c) -> p c"
                sp.dma_start(raw[:, 0, :], a["src"].rearrange(flat, p=EP)).then_inc(loaded, 16)
                sp.dma_start(raw[:, 1, :], a["dst"].rearrange(flat, p=EP)).then_inc(loaded, 16)
                sp.dma_start(raw[:, 2, :], a["edge_type_200"].rearrange(flat, p=EP)).then_inc(loaded, 16)
                sp.dma_start(elem[:, :], a["edge_weight"].rearrange(flat, p=EP)).then_inc(loaded, 16)
                sp.dma_start(X[:, 0:NT - 1, :], a["x"][0:(NT - 1) * P, :].rearrange("(t p) d -> p t d", p=P))\
                    .then_inc(xloaded, 16)
                sp.wait_ge(zeroed, 1)
                sp.dma_start(X[0:LAST, NT - 1, :], a["x"][(NT - 1) * P:N, :]).then_inc(xloaded, 16)
                for j in range(KD):
                    sp.dma_start(wcat[:, j, 0:D].rearrange("p (h o) -> p h o", h=H),
                                 a["L0_gnn_Ws"][:, j * P:(j + 1) * P, :].rearrange("h p o -> p h o"))\
                        .then_inc(wloaded, 16)
                sp.dma_start(awb[:, :, :].rearrange("p h o -> p (h o)"),
                             a["L0_gnn_aw"].rearrange("h o -> (h o)").partition_broadcast(P)).then_inc(wloaded, 16)
                sp.dma_start(biasrow[:, 0:D],
                             a["L0_gnn_bs"].rearrange("h o -> (h o)").partition_broadcast(P)).then_inc(wloaded, 16)
                sp.wait_ge(blank_ready, 1)
                for l in range(2):
                    sp.dma_start(rec_d[l].rearrange("(p t) w -> p (t w)", p=P),
                                 blank[:, :, :].rearrange("p t w -> p (t w)")).then_inc(blanked, 16)
                with sp.Fori(0, NCH) as i:
                    for k in range(CH):
                        sp.wait_ge(fready, i * CH + k + 1)
                        sp.dma_start(table0[bass.ds((i * CH + k) * P, P), :], frow[:, k % 2, :])\
                            .then_inc(fstored[k % 2], 16)
                sp.wait_ge(fstored[0], 16 * 3 * NCH)
                sp.wait_ge(fstored[1], 16 * 2 * NCH)

            @block.gpsimd
            def _(pool):
                g = nc.gpsimd
                g.memset(ident[:, :], 0.0).then_inc(consts, 1)
                g.memset(before[:, :], 1.0).then_inc(consts, 1)
                g.memset(ones[:, :], 1.0).then_inc(consts, 1)
                g.memset(eps[:, :], 1e-5).then_inc(consts, 1)
                g.memset(padrow[:, :], 0.0).then_inc(consts, 1)
                g.memset(blank[:, :, :], 0).then_inc(consts, 1)
                g.iota(iota[:, :], [[1, R]], base=0, channel_multiplier=0,
                       allow_small_or_imprecise_dtypes=True).then_inc(consts, 1)
                g.iota(unumber[:, :], [[1, UNITS]], base=0, channel_multiplier=0,
                       allow_small_or_imprecise_dtypes=True).then_inc(consts, 1)
                pool.wait_ge(consts, 8)
                g.affine_select(out=ident[:, :], in_=ident[:, :], compare_op=ALU.not_equal, fill=1.0, base=0,
                                pattern=[[-1, P]], channel_multiplier=1).then_inc(consts, 1)
                g.affine_select(out=before[:, :], in_=before[:, :], compare_op=ALU.is_gt, fill=0.0, base=0,
                                pattern=[[1, P]], channel_multiplier=-1).then_inc(consts, 1)
                g.affine_select(out=padrow[:, NT - 1:NT], in_=padrow[:, NT - 1:NT], compare_op=ALU.is_gt, fill=1.0,
                                base=LAST, pattern=[[0, 1]], channel_multiplier=-1).then_inc(consts, 1)
                g.memset(blank[:, :, 0:1], 4 * P).then_inc(blank_ready, 1)
                pool.wait_ge(blanked, 32)
                pool.wait_ge(ready[0], 1)
                scatter_records(pool, 0, 0)
                pool.wait_ge(ready[1], 1)
                scatter_records(pool, 1, 1)

            @block.vector
            def _(dve):
                ch = Chain(dve, chain)
                link = ch.link
                v = nc.vector
                v.memset(X[:, NT - 1, :], 0.0).then_inc(zeroed, 1)
                dve.sem_inc(dn.product_free, 1)
                dve.wait_ge(consts, 11)
                dve.wait_ge(loaded, 64)

                def place(l):
                    key, other = (0, 1) if l == 0 else (1, 0)
                    link(v.tensor_scalar(rec_s[l][:, :, 0], raw[:, key, :], P - 1, None, ALU.bitwise_and))
                    link(v.tensor_copy(rec_s[l][:, :, 1], raw[:, other, :]))
                    if l == 0:
                        link(v.tensor_copy(rec_s[l][:, :, 2:3].bitcast(F32), elem[:, :].unsqueeze(2)))
                    else:
                        link(v.tensor_copy(rec_s[l][:, :, 2], raw[:, 2, :]))
                    link(v.memset(rec_s[l][:, :, 3], 0))
                    link(v.tensor_scalar(keyi[:, :], raw[:, key, :], 7, None, ALU.arith_shift_right))
                    link(v.tensor_copy(keyf[:, :], keyi[:, :]))
                    sort[l].vector(dve, link, keyf[:, :], unit_tile[l][0:EP, :], wheref[:, :])
                    link(v.tensor_copy(ts[:, 0, :], wheref[:, :]))
                    link(v.tensor_scalar(ts[:, 1, :], ts[:, 0, :], P - 1, None, ALU.bitwise_and))
                    link(v.tensor_scalar(ts[:, 2, :], ts[:, 0, :], 7, None, ALU.arith_shift_right))
                    v.scalar_tensor_tensor(slot[l][:, :], ts[:, 1, :], float(ST), ts[:, 2, :], ALU.mult,
                                           ALU.add).then_inc(ready[l], 1)
                    dve.wait_ge(ready[l], 1)

                place(0)
                dve.wait_ge(wloaded, 16 * (KD + 2))
                for part, off in ((1, 0), (0, H)):
                    aw = awb[:, :, part * O:(part + 1) * O]
                    for j in range(KD):
                        link(v.tensor_tensor(awprod[:, :, :], wcat[:, j, 0:D].rearrange("p (h o) -> p h o", h=H),
                                             aw, ALU.mult))
                        link(v.tensor_reduce(wcat[:, j, D + off:D + off + H], awprod[:, :, :], AX.X, ALU.add))
                    link(v.tensor_tensor(awprod[:, :, :], biasrow[:, 0:D].rearrange("p (h o) -> p h o", h=H),
                                         aw, ALU.mult))
                    link(v.tensor_reduce(biasrow[:, D + off:D + off + H], awprod[:, :, :], AX.X, ALU.add))
                dve.sem_inc(wready, 1)
                dve.wait_ge(xloaded, 32)

                def features(i):
                    dn.vector(dve, ch, i)
                    for k in range(CH):
                        dve.wait_ge(dn.product, i * CH + k + 1)
                        if not (isinstance(i, int) and k < 2):
                            dve.wait_ge(fstored[k % 2], (i * (3 - k % 2) + k // 2) * 16)
                        v.tensor_tensor(frow[:, k % 2, :], dn.psF[:, k % 2, 0:W0], biasrow[:, :], ALU.add)\
                            .then_inc(fready, 1)
                        dve.wait_ge(fready, i * CH + k + 1)
                        dve.sem_inc(dn.product_free, 1)
                features(0)
                with dve.Fori(1, NCH) as i:
                    ch.enter(i, dn.LINKS, 1)
                    features(i)
                ch.leave(NCH)
                place(1)

            @block.scalar
            def _(act):
                dn.run_act(act)

            @block.tensor
            def _(pe):
                pe.wait_ge(consts, 11)
                sort[0].tensor(pe)
                pe.wait_ge(wready, 1)
                dn.run_pe(pe, wcat)
                sort[1].tensor(pe)

    end_phase()

    def edge_phase(l, c, table, width, accw, acc, rec, own_off, own_n, heads, post):
        tag = f"e{l}_"
        rows = sb(tag + "rows", [P, DEPTH, TPG, accw if l else width], c=c)
        gidx = sb(tag + "gidx", [P, DEPTH, TPG], I32, c=c)
        oh = sb(tag + "oh", [P, DEPTH, TPG, P], c=c)
        ohT = sb(tag + "ohT", [P, 2, TPG, P], c=c)
        ownv = sb(tag + "ownv", [P, DEPTH, 2, own_n], c=c)
        sc = sb(tag + "sc", [P, 2, TPG, heads], c=c)
        psT = ps(tag + "psT", [P, 2, 512], c)
        psA = ps(tag + "psA", [P, 2, 512], c)
        psO = ps(tag + "psO", [P, 4, 512], c)
        names = ("oh_ready", "turned", "ohT_ready", "own_e", "own_used", "score", "weight", "payload",
                 "summed", "added", "gidx_ready", "rec_loaded", "table_done", "acc_zero", "bulk")
        S = {n: sem(tag + n) for n in names}
        fetched = [sem(tag + f"rows_landed{r}") for r in range(DEPTH)]
        ownland = [sem(tag + f"own_landed{r}") for r in range(DEPTH)]
        chain = sem(tag + "chain")
        G = GROUPS

        def pipeline(eng, ahead, behind, step):
            for s in range(-ahead, DEPTH):
                step(s, None)
            with eng.Fori(1, G // DEPTH - 1) as q:
                for r in range(DEPTH):
                    step(None, (q, r))
            for s in range(G - DEPTH, G + behind):
                step(s, None)

        def locate(s, dyn, shift):
            if dyn is None:
                g = s + shift
                return None if g < 0 or g >= G else (g, g // DEPTH, g % DEPTH)
            q, r = dyn
            return q * DEPTH + (r + shift), q + (r + shift) // DEPTH, (r + shift) % DEPTH

        def known(g):
            return isinstance(g, int)

        def back(eng, s, g, n, per=1, extra=0):
            if not known(g):
                eng.wait_ge(s, (g - n + 1) * per + extra)
            elif g - n >= 0:
                eng.wait_ge(s, (g - n + 1) * per + extra)

        with nc.Block() as block:
            @block.sync
            def _(sp):
                sp.dma_start(rec[:, :, :].rearrange("p t w -> p (t w)"),
                             rec_d[l].rearrange("(p t) w -> p (t w)", p=P)).then_inc(S["rec_loaded"], 16)
                if post.get("sync"):
                    post["sync"](sp, S)

                def step(s, dyn):
                    at = locate(s, dyn, 0)
                    if at is None:
                        return
                    g, q, r = at
                    back(sp, S["own_e"], g, DEPTH)
                    hold(sp, "sp")
                    for j in range(2):
                        t = sp.value_load(unit_tile[l][0:1, bass.ds(g * 2 + j, 1)], min_val=0, max_val=NT - 1)
                        sp.dma_start(ownv[:, r, j, :], table[bass.ds(t * P, P), own_off:own_off + own_n])\
                            .then_inc(ownland[r], 16)
                pipeline(sp, 0, 0, step)

            @block.gpsimd
            def _(pool):
                pool.wait_ge(S["rec_loaded"], 16)

                def step(s, dyn):
                    at = locate(s, dyn, 0)
                    if at is None:
                        return
                    g, q, r = at
                    back(pool, S["summed"], g, DEPTH)
                    hold(pool, "pool")
                    nc.gpsimd.tensor_copy(gidx[:, r, :], rec[:, bass.ds(g * TPG, TPG), 1]).then_inc(S["gidx_ready"], 1)
                    pool.wait_ge(S["gidx_ready"], g + 1)
                    hold(pool, "pool")
                    for t in range(TPG):
                        pool.indirect_dma_start(
                            out=rows[:, r, t, 0:width], out_offset=None, in_=table,
                            in_offset=bass.IndirectOffsetOnAxis(ap=gidx[:, r, t:t + 1], axis=0))\
                            .then_inc(fetched[r], 16)
                pipeline(pool, 0, 0, step)

            @block.vector
            def _(dve):
                v = nc.vector
                v.memset(acc[:, :, :], 0.0).then_inc(S["acc_zero"], 1)
                dve.wait_ge(S["acc_zero"], 1)
                dve.wait_ge(S["rec_loaded"], 16)
                if post.get("bulk"):
                    post["bulk"](dve, S, chain)

                def onehots(at):
                    g, q, r = at
                    back(dve, S["summed"], g, DEPTH)
                    v.tensor_tensor(oh[:, r, :, :], rec[:, bass.ds(g * TPG, TPG), 0:1].to_broadcast([P, TPG, P]),
                                    iota[:, 0:P].unsqueeze(1).to_broadcast([P, TPG, P]), ALU.is_equal)\
                        .then_inc(S["oh_ready"], 1)
                    if post.get("onehots"):
                        post["onehots"](dve, v, at, rows, oh, S)

                def add(at):
                    g, q, r = at
                    tiles = []
                    hold(dve, "dve")
                    for j in range(2):
                        tiles.append(dve.value_load(unit_tile[l][0:1, bass.ds(g * 2 + j, 1)], min_val=0,
                                                    max_val=NT - 1))
                    dve.wait_ge(S["summed"], g + 1)
                    for j in range(2):
                        if not (known(g) and g == 0 and j == 0):
                            dve.wait_ge(S["added"], g * 2 + j)
                        d = acc[:, bass.ds(tiles[j], 1), :].rearrange("p a w -> p (a w)")
                        v.tensor_tensor(d, d, psO[:, 2 * (r % 2) + j, 0:accw], ALU.add).then_inc(S["added"], 1)

                def step(s, dyn):
                    nxt, now, last = (locate(s, dyn, d) for d in (1, 0, -1))
                    if nxt is not None:
                        onehots(nxt)
                    if now is not None:
                        post["score"](dve, v, now, rows, psA, sc, S, fetched)
                    if last is not None:
                        add(last)
                    if now is not None:
                        post["payload"](dve, v, now, rows, oh, sc, S)
                pipeline(dve, 1, 1, step)

            @block.scalar
            def _(act):
                def step(s, dyn):
                    nxt, now = (locate(s, dyn, d) for d in (1, 0))
                    if now is not None:
                        post["exp"](act, now, rows, sc, S)
                    if nxt is not None:
                        g, q, r = nxt
                        act.wait_ge(S["turned"], g + 1)
                        back(act, S["own_e"], g, 2)
                        nc.scalar.activation(ohT[:, r % 2, :, :].rearrange("p t n -> p (t n)"), psT[:, r % 2, :],
                                             ACT.Copy).then_inc(S["ohT_ready"], 1)
                pipeline(act, 1, 0, step)

            @block.tensor
            def _(pe):
                def step(s, dyn):
                    nxt, now, last = (locate(s, dyn, d) for d in (1, 0, -1))
                    if now is not None:
                        g, q, r = now
                        pe.wait_ge(S["ohT_ready"], g + 1)
                        pe.wait_ge(ownland[r], q * 32 + 32)
                        back(pe, S["own_used"], g, 2)
                        for t in range(TPG):
                            ins = pe.matmul(psA[:, r % 2, t * heads:(t + 1) * heads], ohT[:, r % 2, t, :],
                                            ownv[:, r, t // TPU, own_n - heads:], start=True, stop=True)
                        ins.then_inc(S["own_e"], 1)
                    if last is not None:
                        g, q, r = last
                        pe.wait_ge(S["payload"], g + 1)
                        back(pe, S["added"], g, 2, per=2)
                        for t in range(TPG):
                            ins = pe.matmul(psO[:, 2 * (r % 2) + t // TPU, 0:accw], oh[:, r, t, :],
                                            rows[:, r, t, 0:accw], start=(t % TPU == 0), stop=(t % TPU == TPU - 1))
                        ins.then_inc(S["summed"], 1)
                    if nxt is not None:
                        g, q, r = nxt
                        pe.wait_ge(S["oh_ready"], g + 1)
                        back(pe, S["ohT_ready"], g, 2)
                        for t in range(TPG):
                            ins = pe.transpose(psT[:, r % 2, t * P:(t + 1) * P], oh[:, r, t, :], ident[:, :])
                        ins.then_inc(S["turned"], 1)
                pipeline(pe, 1, 1, step)

        end_phase()

    with ExitStack() as c2:
        acc0 = sb("acc0", [P, NT, A0], c=c2)
        with ExitStack() as c:
            rec = sb("rec0", [P, ST, 4], I32, c=c)
            edge_term = sb("edge_term", [P, ST, H], c=c)
            awe = sb("awe", [P, H, 2 * O + 1], c=c)
            abb = sb("abb", [P, H], c=c)
            s_score = sem("l0_score_steps")

            def l0_sync(sp, S):
                sp.dma_start(awe[:, :, :].rearrange("p h o -> p (h o)"),
                             a["L0_gnn_aw"].rearrange("h o -> (h o)").partition_broadcast(P)).then_inc(S["table_done"], 16)
                sp.dma_start(abb[:, :], a["L0_gnn_ab"].partition_broadcast(P)).then_inc(S["table_done"], 16)

            def l0_bulk(dve, S, chain):
                v = nc.vector
                link = Chain(dve, chain).link
                dve.wait_ge(S["table_done"], 32)
                full = [P, ST, H]
                el = rec[:, :, 2:3].bitcast(F32).to_broadcast(full)
                link(v.tensor_tensor(edge_term[:, :, :], el,
                                     awe[:, :, 2 * O:2 * O + 1].rearrange("p h o -> p o h").to_broadcast(full),
                                     ALU.mult))
                link(v.tensor_tensor(edge_term[:, :, :], edge_term[:, :, :],
                                     abb[:, :].unsqueeze(1).to_broadcast(full), ALU.add))

            def l0_score(dve, v, at, rows, psA, sc, S, fetched):
                g, q, r = at
                dve.wait_ge(S["own_e"], g + 1)
                dve.wait_ge(fetched[r], q * (16 * TPG) + 16 * TPG)
                s = sc[:, r % 2, :, :]
                v.tensor_tensor(s, psA[:, r % 2, 0:TPG * H].rearrange("p (t h) -> p t h", t=TPG),
                                rows[:, r, :, D:D + H], ALU.add).then_inc(S["own_used"], 1)
                dve.wait_ge(S["own_used"], g + 1)
                v.tensor_tensor(s, s, edge_term[:, bass.ds(g * TPG, TPG), :], ALU.add).then_inc(s_score, 1)
                dve.wait_ge(s_score, g + 1)
                v.tensor_scalar(s, s, -1.0 / 20.0, 0.0, ALU.mult, ALU.min).then_inc(S["score"], 1)

            def l0_exp(act, at, rows, sc, S):
                g, q, r = at
                act.wait_ge(S["score"], g + 1)
                nc.scalar.activation(rows[:, r, :, D:D + H], sc[:, r % 2, :, :], ACT.Exp).then_inc(S["weight"], 1)

            def l0_payload(dve, v, at, rows, oh, sc, S):
                g, q, r = at
                dve.wait_ge(S["weight"], g + 1)
                f = rows[:, r, :, 0:D].rearrange("p t (h o) -> p t h o", h=H)
                v.tensor_tensor(f, f, rows[:, r, :, D:D + H].unsqueeze(3).to_broadcast([P, TPG, H, O]), ALU.mult)\
                    .then_inc(S["payload"], 1)

            edge_phase(0, c, table0, W0, A0, acc0, rec, D + H, H, H,
                       dict(sync=l0_sync, bulk=l0_bulk, score=l0_score, exp=l0_exp, payload=l0_payload))

        with ExitStack() as c:
            dn = Dense("ln1", c, NE)
            XN = sb("XN", [P, NT, D], c=c)
            gw = sb("gw", [P, KD, NE], c=c)
            gb = sb("gb", [P, NE], c=c)
            prob = sb("prob", [P, NT, NE], c=c)
            pick = sb("pick", [P, NT, NE], c=c)
            col = sb("col", [P, 8, NT], c=c)
            keys = sb("keys", [P, 2, NT], c=c)
            wts = sb("wts", [P, 2, NT], c=c)
            wheref = sb("where2", [P, 2 * NT], c=c)
            tokslot = sb("tokslot", [P, 2 * NT], I32, c=c)
            texp = sb("tile_expert", [P, MT], I32, c=c)
            srt = Sort("sort2", c, P, 2 * NT, NE, P, MT)
            srt.unumber = sb("unumber2", [P, MT], c=c)
            zero = sb("zero", [P, 8, D], c=c)
            chain = sem("chain3")
            gloaded, zfilled, zset, xncopied = sem("gloaded"), sem("zfilled"), sem("zset"), sem("xncopied")
            xn_copy_free, logits = sem("xn_copy_free"), sem("logits")
            shifted, exped, tok_ready, dispatched = sem("shifted"), sem("exped"), sem("tok_ready"), sem("dispatched")
            x1d = sem("x1_done")

            with nc.Block() as block:
                @block.sync
                def _(sp):
                    sp.dma_start(gw[:, :, :], a["L0_ffn_gate_w"].rearrange("(j p) e -> p j e", p=P)).then_inc(gloaded, 16)
                    sp.dma_start(gb[:, :], a["L0_ffn_gate_b"].partition_broadcast(P)).then_inc(gloaded, 16)
                    sp.wait_ge(zset, 1)
                    rest = expert_in.rearrange("(p s) d -> p s d", p=P)
                    for s0 in range(0, MT, 8):
                        n = min(8, MT - s0)
                        sp.dma_start(rest[:, s0:s0 + n, :], zero[:, 0:n, :]).then_inc(zfilled, 16)

                @block.gpsimd
                def _(pool):
                    nc.gpsimd.memset(zero[:, :, :], 0.0).then_inc(zset, 1)
                    nc.gpsimd.iota(srt.unumber[:, :], [[1, MT]], base=0, channel_multiplier=0,
                                   allow_small_or_imprecise_dtypes=True).then_inc(zset, 1)
                    pool.wait_ge(zfilled, 16 * -(-MT // 8))
                    pool.wait_ge(tok_ready, 1)
                    for j in range(2):
                        for t in range(NT):
                            n = LAST if t == NT - 1 else P
                            at = j * NT + t
                            pool.indirect_dma_start(
                                out=expert_in,
                                out_offset=bass.IndirectOffsetOnAxis(ap=tokslot[0:n, at:at + 1], axis=0),
                                in_=XN[0:n, t, :], in_offset=None).then_inc(dispatched, 16)
                    pool.wait_ge(dispatched, 16 * 2 * NT)

                @block.vector
                def _(dve):
                    v = nc.vector
                    ch = Chain(dve, chain)
                    link = ch.link
                    dve.sem_inc(dn.product_free, 1)
                    w = acc0[:, :, D:D + H]
                    link(v.tensor_tensor(w, w, padrow[:, :].unsqueeze(2).to_broadcast([P, NT, H]), ALU.add))
                    link(v.reciprocal(w, w))
                    for h in range(H):
                        f = acc0[:, :, h * O:(h + 1) * O]
                        link(v.tensor_tensor(f, f, acc0[:, :, D + h:D + h + 1].to_broadcast([P, NT, O]), ALU.mult))
                    link(v.tensor_tensor(X[:, :, :], X[:, :, :], acc0[:, :, 0:D], ALU.add))
                    dve.wait_ge(gloaded, 32)
                    with dve.Fori(0, NCH) as i:
                        ch.enter(i, dn.LINKS)
                        dve.wait_ge(xn_copy_free, i + 1)
                        dn.vector(dve, ch, i)
                        for k in range(CH):
                            dve.wait_ge(dn.product, i * CH + k + 1)
                            v.tensor_tensor(prob[:, bass.ds(i * CH + k, 1), :].rearrange("p a e -> p (a e)"),
                                            dn.psF[:, k % 2, 0:NE], gb[:, :], ALU.add).then_inc(logits, 1)
                            dve.wait_ge(logits, i * CH + k + 1)
                            dve.sem_inc(dn.product_free, 1)
                    ch.leave(NCH)
                    full = [P, NT, NE]

                    def over(x):
                        return x.unsqueeze(2).to_broadcast(full)

                    number = iota[:, 0:NE].unsqueeze(1).to_broadcast(full)
                    link(v.tensor_reduce(col[:, 0, :], prob[:, :, :], AX.X, ALU.max))
                    v.tensor_tensor(prob[:, :, :], prob[:, :, :], over(col[:, 0, :]), ALU.subtract).then_inc(shifted, 1)
                    dve.wait_ge(exped, 1)
                    link(v.tensor_reduce(col[:, 1, :], prob[:, :, :], AX.X, ALU.add))
                    link(v.reciprocal(col[:, 2, :], col[:, 1, :]))
                    link(v.tensor_tensor(prob[:, :, :], prob[:, :, :], over(col[:, 2, :]), ALU.mult))
                    for j in range(2):
                        link(v.tensor_reduce(col[:, 3 + j, :], prob[:, :, :], AX.X, ALU.max))
                        link(v.tensor_tensor(pick[:, :, :], prob[:, :, :], over(col[:, 3 + j, :]), ALU.is_equal))
                        link(v.tensor_tensor(pick[:, :, :], pick[:, :, :],
                                             srt.small[:, 7, 0:NE].unsqueeze(1).to_broadcast(full), ALU.mult)
                             if j else v.tensor_scalar(srt.small[:, 7, 0:NE], iota[:, 0:NE], -1.0, float(NE),
                                                       ALU.mult, ALU.add))
                        if j == 0:
                            link(v.tensor_tensor(pick[:, :, :], pick[:, :, :],
                                                 srt.small[:, 7, 0:NE].unsqueeze(1).to_broadcast(full), ALU.mult))
                        link(v.tensor_reduce(keys[:, j, :], pick[:, :, :], AX.X, ALU.max))
                        link(v.tensor_scalar(keys[:, j, :], keys[:, j, :], -1.0, float(NE), ALU.mult, ALU.add))
                        if j == 0:
                            link(v.tensor_tensor(pick[:, :, :], number, over(keys[:, 0, :]), ALU.is_equal))
                            link(v.scalar_tensor_tensor(prob[:, :, :], pick[:, :, :], -2.0, prob[:, :, :],
                                                        ALU.mult, ALU.add))
                    link(v.tensor_tensor(col[:, 5, :], col[:, 3, :], col[:, 4, :], ALU.add))
                    link(v.reciprocal(col[:, 6, :], col[:, 5, :]))
                    for j in range(2):
                        link(v.tensor_tensor(wts[:, j, :], col[:, 3 + j, :], col[:, 6, :], ALU.mult))
                        link(v.scalar_tensor_tensor(keys[:, j, :], padrow[:, :], float(2 * NE), keys[:, j, :],
                                                    ALU.mult, ALU.add))
                    dve.wait_ge(zset, 2)
                    srt.vector(dve, link, keys[:, :, :].rearrange("p j t -> p (j t)"), texp[:, :], wheref[:, :])
                    v.tensor_copy(tokslot[:, :], wheref[:, :]).then_inc(tok_ready, 1)

                @block.scalar
                def _(act):
                    act.sem_inc(xn_copy_free, 1)

                    def keep(i):
                        act.wait_ge(dn.normed, i + 1)
                        hold(act, "act")
                        nc.scalar.activation(XN[:, bass.ds(i * CH, CH), :], dn.xn[:, :, :], ACT.Copy).then_inc(xncopied, 1)
                        act.wait_ge(xncopied, i + 1)
                        act.sem_inc(xn_copy_free, 1)
                    dn.run_act(act, extra=keep)
                    act.wait_ge(shifted, 1)
                    nc.scalar.activation(prob[:, :, :], prob[:, :, :], ACT.Exp).then_inc(exped, 1)

                @block.tensor
                def _(pe):
                    pe.wait_ge(gloaded, 32)
                    dn.run_pe(pe, gw)
                    srt.tensor(pe)

            end_phase()

            with ExitStack() as cc:
                xs = sb("xs", [P, 2, D], c=cc)
                xsT = sb("xsT", [P, 2, KD, P], c=cc)
                w1s = sb("w1s", [P, 2, KD, FH], c=cc)
                w2s = sb("w2s", [P, 2, KD, FH], c=cc)
                w3s = sb("w3s", [P, 2, FH // P, D], c=cc)
                gate = sb("gate", [P, 2, FH], c=cc)
                hid = sb("hid", [P, 2, FH], c=cc)
                ys = sb("ys", [P, 2, D], c=cc)
                cidx = sb("cidx", [P, 2, CH], I32, c=cc)
                crow = sb("crow", [P, 2, CH, D], c=cc)
                names = ("turned", "xsT_ready", "h1", "h2", "gated", "hidden", "y", "y_copied", "cstaged", "cused",
                         "mixed")
                S = {n: sem("m_" + n) for n in names}
                xland = [sem(f"m_xland{r}") for r in range(2)]
                wland = [sem(f"m_wland{r}") for r in range(2)]
                ystored = [sem(f"m_ystored{r}") for r in range(2)]
                cland = sem("m_cland")

                psX, psH1 = dn.psT, dn.psF
                psH2, psY = ps("psH2", [P, 2, 512], cc), (srt.psum, ps("psY2", [P, 512], cc))

                def both(eng, ahead, behind, step):
                    for s in range(-ahead, 4):
                        step(s, None)
                    with eng.Fori(2, MT // 2 - 1) as q:
                        for r in range(2):
                            step(None, (q, r))
                    for s in range(MT - 2, MT + behind):
                        step(s, None)

                def tile_at(s, dyn, shift):
                    if dyn is None:
                        t = s + shift
                        return None if t < 0 or t >= MT else (t, t // 2, t % 2)
                    q, r = dyn
                    return q * 2 + (r + shift), q + (r + shift) // 2, (r + shift) % 2

                def back(eng, s, t, n):
                    if not isinstance(t, int) or t - n >= 0:
                        eng.wait_ge(s, t - n + 1)

                with nc.Block() as block:
                    @block.sync
                    def _(sp):
                        def step(s, dyn):
                            t, q, r = tile_at(s, dyn, 0)
                            back(sp, S["turned"], t, 2)
                            sp.dma_start(xs[:, r, :], expert_in[bass.ds(t * P, P), :]).then_inc(xland[r], 16)
                            back(sp, S["y"], t, 2)
                            hold(sp, "sp")
                            e = sp.value_load(texp[0:1, bass.ds(t, 1)], min_val=0, max_val=NE - 1)
                            for w, d in ((w1s, a["L0_ffn_w1"]), (w2s, a["L0_ffn_w2"]), (w3s, a["L0_ffn_w3"])):
                                sp.dma_start(w[:, r, :, :], d[bass.ds(e, 1), :, :]
                                             .rearrange("e (j p) n -> p (e j) n", p=P)).then_inc(wland[r], 16)
                        both(sp, 0, 0, step)

                    @block.gpsimd
                    def _(pool):
                        for r in range(2):
                            pool.wait_ge(ystored[r], 16 * (MT // 2))
                        with pool.Fori(0, NCH) as i:
                            pool.wait_ge(S["cused"], i + 1)
                            hold(pool, "pool")
                            for j in range(2):
                                nc.gpsimd.tensor_copy(cidx[:, j, :], tokslot[:, bass.ds(i * CH + j * NT, CH)])\
                                    .then_inc(S["cstaged"], 1)
                            pool.wait_ge(S["cstaged"], i * 2 + 2)
                            hold(pool, "pool")
                            for j in range(2):
                                for k in range(CH):
                                    pool.indirect_dma_start(
                                        out=crow[:, j, k, :], out_offset=None, in_=expert_out,
                                        in_offset=bass.IndirectOffsetOnAxis(ap=cidx[:, j, k:k + 1], axis=0))\
                                        .then_inc(cland, 16)

                    @block.vector
                    def _(dve):
                        v = nc.vector

                        def step(s, dyn):
                            now, last = tile_at(s, dyn, 0), tile_at(s, dyn, -1)
                            if now is not None:
                                t, q, r = now
                                dve.wait_ge(S["gated"], t + 1)
                                dve.wait_ge(S["h2"], t + 1)
                                back(dve, S["y"], t, 2)
                                v.tensor_tensor(hid[:, r, :], gate[:, r, :], psH2[:, r, :], ALU.mult)\
                                    .then_inc(S["hidden"], 1)
                            if last is not None:
                                t, q, r = last
                                dve.wait_ge(S["y"], t + 1)
                                if not isinstance(t, int) or t >= 2:
                                    dve.wait_ge(ystored[r], q * 16)
                                v.tensor_copy(ys[:, r, :], psY[r][:, 0:D]).then_inc(S["y_copied"], 1)
                        both(dve, 0, 1, step)
                        dve.sem_inc(S["cused"], 1)
                        with dve.Fori(0, NCH) as i:
                            dve.wait_ge(cland, i * (32 * CH) + 32 * CH)
                            for j in range(2):
                                wt = wts[:, j, bass.ds(i * CH, CH)].unsqueeze(2).to_broadcast([P, CH, D])
                                v.tensor_tensor(crow[:, j, :, :], crow[:, j, :, :], wt, ALU.mult).then_inc(S["mixed"], 1)
                            for j in range(2):
                                dve.wait_ge(S["mixed"], i * 4 + (2 + j))
                                xc = X[:, bass.ds(i * CH, CH), :]
                                v.tensor_tensor(xc, xc, crow[:, j, :, :], ALU.add).then_inc(S["mixed"], 1)
                            dve.wait_ge(S["mixed"], i * 4 + 4)
                            dve.sem_inc(S["cused"], 1)

                    @block.scalar
                    def _(act):
                        def step(s, dyn):
                            nxt, now, last = (tile_at(s, dyn, d) for d in (1, 0, -1))
                            if nxt is not None:
                                t, q, r = nxt
                                act.wait_ge(S["turned"], t + 1)
                                back(act, S["h2"], t, 2)
                                nc.scalar.activation(xsT[:, r, :, :], psX[:, r, 0:D].rearrange("p (a b) -> p a b", a=KD),
                                                     ACT.Copy).then_inc(S["xsT_ready"], 1)
                            if now is not None:
                                t, q, r = now
                                act.wait_ge(S["h1"], t + 1)
                                back(act, S["hidden"], t, 2)
                                nc.scalar.activation(gate[:, r, :], psH1[:, r, :], ACT.Silu).then_inc(S["gated"], 1)
                            if last is not None:
                                t, q, r = last
                                act.wait_ge(S["y_copied"], t + 1)
                                act.dma_start(expert_out[bass.ds(t * P, P), :], ys[:, r, :]).then_inc(ystored[r], 16)
                        both(act, 1, 1, step)

                    @block.tensor
                    def _(pe):
                        def step(s, dyn):
                            nxt, now, last = (tile_at(s, dyn, d) for d in (1, 0, -1))
                            if nxt is not None:
                                t, q, r = nxt
                                pe.wait_ge(xland[r], q * 16 + 16)
                                back(pe, S["xsT_ready"], t, 2)
                                for j in range(KD):
                                    ins = pe.transpose(psX[:, r, j * P:(j + 1) * P], xs[:, r, j * P:(j + 1) * P],
                                                       ident[:, :])
                                ins.then_inc(S["turned"], 1)
                            if now is not None:
                                t, q, r = now
                                pe.wait_ge(S["xsT_ready"], t + 1)
                                pe.wait_ge(wland[r], q * 48 + 48)
                                for w, p_, name, freed in ((w1s, psH1, "h1", "gated"), (w2s, psH2, "h2", "hidden")):
                                    back(pe, S[freed], t, 2)
                                    for m in range(FH // P):
                                        for j in range(KD):
                                            ins = pe.matmul(p_[:, r, m * P:(m + 1) * P], w[:, r, j, m * P:(m + 1) * P],
                                                            xsT[:, r, j, :], start=(j == 0), stop=(j == KD - 1))
                                    ins.then_inc(S[name], 1)
                            if last is not None:
                                t, q, r = last
                                pe.wait_ge(S["hidden"], t + 1)
                                back(pe, S["y_copied"], t, 2)
                                for m in range(FH // P):
                                    ins = pe.matmul(psY[r][:, 0:D], hid[:, r, m * P:(m + 1) * P],
                                                    w3s[:, r, m, :], start=(m == 0), stop=(m == FH // P - 1))
                                ins.then_inc(S["y"], 1)
                        both(pe, 1, 1, step)

                end_phase()

    with ExitStack() as c4:
        acc1 = sb("acc1", [P, NT, A1], c=c4)
        relW = sb("relW", [P, 2, D], c=c4)
        with ExitStack() as c:
            rec = sb("rec1", [P, ST, 4], I32, c=c)
            relrow = sb("relrow", [P, R], c=c)
            with ExitStack() as cc:
                dn = Dense("ln2", cc, W1)
                wn = sb("wn", [P, KD, W1], c=cc)
                w3r = sb("w3r", [P, 3 * KD, 3 * D], c=cc)
                arow = sb("arow", [P, 3 * D], c=cc)
                wcol = sb("wcol", [P, 3 * KD], c=cc)
                rel = sb("rel", [P, 2, D], c=cc)
                relT = sb("relT", [P, KD, R], c=cc)
                relwb = sb("relwb", [P, KD, P], c=cc)
                frow = sb("frow1", [P, 2, W1], c=cc)
                psR = ps("psR", [P, 2, 512], cc)
                wloaded, wready, chain = sem("w4_loaded"), sem("w4_ready"), sem("chain4")
                rel_t, rel_c, rel_p = sem("rel_turned"), sem("rel_copied"), sem("rel_product")
                fready, fstored = sem("f4_ready"), [sem("f4st0"), sem("f4st1")]

                with nc.Block() as block:
                    @block.sync
                    def _(sp):
                        sp.dma_start(arow[:, :], a["L1_gnn_a"].rearrange("n o -> (n o)").partition_broadcast(P))\
                            .then_inc(wloaded, 16)
                        sp.dma_start(w3r[:, :, :], a["L1_gnn_W3"].rearrange("(j p) n -> p j n", p=P)).then_inc(wloaded, 16)
                        sp.dma_start(wn[:, :, 0:D], a["L1_gnn_weight_neighbor"].rearrange("(j p) n -> p j n", p=P))\
                            .then_inc(wloaded, 16)
                        sp.dma_start(rel[:, 0, :], a["L1_gnn_rel_emb"][0:P, :]).then_inc(wloaded, 16)
                        sp.dma_start(rel[0:R - P, 1, :], a["L1_gnn_rel_emb"][P:R, :]).then_inc(wloaded, 16)
                        with sp.Fori(0, NCH) as i:
                            for k in range(CH):
                                sp.wait_ge(fready, i * CH + k + 1)
                                sp.dma_start(table1[bass.ds((i * CH + k) * P, P), :], frow[:, k % 2, :])\
                                    .then_inc(fstored[k % 2], 16)
                        sp.wait_ge(fstored[0], 16 * 3 * NCH)
                        sp.wait_ge(fstored[1], 16 * 2 * NCH)

                    @block.vector
                    def _(dve):
                        v = nc.vector
                        ch = Chain(dve, chain)
                        link = ch.link
                        dve.sem_inc(dn.product_free, 1)
                        dve.wait_ge(wloaded, 80)
                        link(v.tensor_tensor(w3r[:, :, :], w3r[:, :, :],
                                             arow[:, :].unsqueeze(1).to_broadcast([P, 3 * KD, 3 * D]), ALU.mult))
                        link(v.tensor_reduce(wcol[:, :], w3r[:, :, :], AX.X, ALU.add))
                        for j in range(KD):
                            for e in range(2):
                                link(v.tensor_copy(wn[:, j, D + e:D + e + 1], wcol[:, e * KD + j:e * KD + j + 1]))
                            link(v.tensor_scalar(relwb[:, j, :], ones[:, :], wcol[:, 2 * KD + j:2 * KD + j + 1], None,
                                                 ALU.mult))
                        dve.wait_ge(rel_t, 1)
                        v.tensor_copy(relT[:, :, :], psR[:, 0, 0:KD * R].rearrange("p (j r) -> p j r", j=KD))\
                            .then_inc(rel_c, 1)
                        dve.sem_inc(wready, 1)
                        dve.wait_ge(rel_p, 1)
                        link(v.tensor_copy(relW[:, 0, :], psR[:, 1, 0:D]))
                        link(v.tensor_copy(relW[0:R - P, 1, :], psR[0:R - P, 1, D:2 * D]))
                        link(v.tensor_copy(relrow[:, :], psR[:, 0, 0:R]))

                        def projections(i):
                            dn.vector(dve, ch, i)
                            for k in range(CH):
                                dve.wait_ge(dn.product, i * CH + k + 1)
                                if not (isinstance(i, int) and k < 2):
                                    dve.wait_ge(fstored[k % 2], (i * (3 - k % 2) + k // 2) * 16)
                                v.tensor_copy(frow[:, k % 2, :], dn.psF[:, k % 2, 0:W1]).then_inc(fready, 1)
                                dve.wait_ge(fready, i * CH + k + 1)
                                dve.sem_inc(dn.product_free, 1)
                        projections(0)
                        with dve.Fori(1, NCH) as i:
                            ch.enter(i, dn.LINKS, 1)
                            projections(i)
                        ch.leave(NCH)

                    @block.scalar
                    def _(act):
                        dn.run_act(act)

                    @block.tensor
                    def _(pe):
                        pe.wait_ge(wloaded, 80)
                        for j in range(KD):
                            pe.transpose(psR[:, 0, j * R:j * R + P], rel[:, 0, j * P:(j + 1) * P], ident[:, :])
                            ins = pe.transpose(psR[:, 0, j * R + P:(j + 1) * R], rel[0:R - P, 1, j * P:(j + 1) * P],
                                               ident[0:R - P, 0:R - P])
                        ins.then_inc(rel_t, 1)
                        pe.wait_ge(rel_c, 1)
                        pe.wait_ge(wready, 1)
                        for b, n in ((0, P), (1, R - P)):
                            for j in range(KD):
                                pe.matmul(psR[0:n, 1, b * D:(b + 1) * D], relT[:, j, b * P:b * P + n], wn[:, j, 0:D],
                                          start=(j == 0), stop=(j == KD - 1))
                        for j in range(KD):
                            ins = pe.matmul(psR[:, 0, 0:R], relwb[:, j, :], relT[:, j, :], start=(j == 0),
                                            stop=(j == KD - 1))
                        ins.then_inc(rel_p, 1)
                        dn.run_pe(pe, wn)

                end_phase()

            rsc = sb("rsc", [P, 2, TPG], c=c)
            rjunk = sb("rjunk", [P, R], c=c)
            steps = sem("l1_steps")
            relsum = sem("l1_relsum")
            tail = sem("l1_tail")

            def l1_onehots(dve, v, at, rows, oh, S):
                g, q, r = at
                for_t = rows[:, r, :, W1:A1]
                v.tensor_tensor(for_t, rec[:, bass.ds(g * TPG, TPG), 2:3].to_broadcast([P, TPG, R]),
                                iota[:, :].unsqueeze(1).to_broadcast([P, TPG, R]), ALU.is_equal).then_inc(relsum, 1)
                dve.wait_ge(relsum, g * 5 + 1)
                for t in range(TPG):
                    v.tensor_tensor_reduce(rjunk[:, :], rows[:, r, t, W1:A1], relrow[:, :], 1.0, 0.0, ALU.mult,
                                           ALU.add, rsc[:, r % 2, t:t + 1]).then_inc(relsum, 1)
                    dve.wait_ge(relsum, g * 5 + (2 + t))

            def l1_score(dve, v, at, rows, psA, sc, S, fetched):
                g, q, r = at
                dve.wait_ge(S["own_e"], g + 1)
                dve.wait_ge(fetched[r], q * (16 * TPG) + 16 * TPG)
                s = sc[:, r % 2, :, 0]
                v.tensor_tensor(s, psA[:, r % 2, 0:TPG], rows[:, r, :, D], ALU.add).then_inc(S["own_used"], 1)
                dve.wait_ge(S["own_used"], g + 1)
                v.tensor_tensor(s, s, rsc[:, r % 2, :], ALU.add).then_inc(steps, 1)
                dve.wait_ge(steps, g + 1)
                v.scalar_tensor_tensor(s, s, 0.01, s, ALU.mult, ALU.max).then_inc(S["score"], 1)

            def l1_exp(act, at, rows, sc, S):
                g, q, r = at
                act.wait_ge(S["score"], g + 1)
                nc.scalar.activation(sc[:, r % 2, :, :], sc[:, r % 2, :, :], ACT.Exp).then_inc(S["weight"], 1)

            def l1_payload(dve, v, at, rows, oh, sc, S):
                g, q, r = at
                dve.wait_ge(S["weight"], g + 1)
                v.reciprocal(rsc[:, r % 2, :], sc[:, r % 2, :, 0]).then_inc(tail, 1)
                dve.wait_ge(tail, g * 2 + 1)
                v.tensor_tensor(sc[:, r % 2, :, 0], sc[:, r % 2, :, 0], rsc[:, r % 2, :], ALU.mult).then_inc(tail, 1)
                dve.wait_ge(tail, g * 2 + 2)
                dve.wait_ge(S["turned"], g + 1)
                v.tensor_tensor(oh[:, r, :, :], oh[:, r, :, :], sc[:, r % 2, :, :].to_broadcast([P, TPG, P]), ALU.mult)\
                    .then_inc(S["payload"], 1)

            edge_phase(1, c, table1, W1, A1, acc1, rec, D, 2, 1,
                       dict(onehots=l1_onehots, score=l1_score, exp=l1_exp, payload=l1_payload))

        with ExitStack() as c:
            dn = Dense("ln3", c, 2 * D)
            wl = sb("wl", [P, KD, 2 * D], c=c)
            cnt = sb("cnt", [P, 2, R], c=c)
            cntT = sb("cntT", [P, 2, 2, P], c=c)
            deg = sb("deg", [P, 2, 2], c=c)
            upd = sb("upd", [P, 2, D], c=c)
            sel = sb("sel", [P, 2, D], c=c)
            psC = ps("psC", [P, 2, 512], c)
            psG = ps("psG", [P, 2, 512], c)
            wloaded, chain = sem("w5_loaded"), sem("chain5")
            cready, cturned, ccopied, gsum = sem("c_ready"), sem("c_turned"), sem("c_copied"), sem("g_sum")
            tdone = sem("t_done")

            def ago(c_, k, n=0):
                return c_ * CH + (k if k < 1 else k - 1) + 1

            with nc.Block() as block:
                @block.sync
                def _(sp):
                    sp.dma_start(wl[:, :, 0:D], a["L1_gnn_loop_weight"].rearrange("(j p) n -> p j n", p=P))\
                        .then_inc(wloaded, 16)
                    sp.dma_start(wl[:, :, D:2 * D], a["L1_gnn_evolve_loop_weight"].rearrange("(j p) n -> p j n", p=P))\
                        .then_inc(wloaded, 16)

                @block.vector
                def _(dve):
                    v = nc.vector
                    ch = Chain(dve, chain)
                    link = ch.link
                    dve.sem_inc(dn.product_free, 1)
                    dve.sem_inc(tdone, 1)

                    with dve.Fori(0, NCH) as i:
                        ch.enter(i, dn.LINKS + 8 * CH)
                        dn.vector(dve, ch, i)
                        for k in range(CH):
                            t = i * CH + k
                            b = k % 2
                            row = acc1[:, bass.ds(t, 1), :].rearrange("p a w -> p (a w)")
                            link(v.tensor_scalar(cnt[:, b, :], row[:, W1:A1], 1.0, None, ALU.mult))
                            dve.sem_inc(cready, 1)
                            link(v.tensor_reduce(deg[:, b, 0:1], cnt[:, b, :], AX.X, ALU.add))
                            link(v.tensor_scalar(deg[:, b, 0:1], deg[:, b, 0:1], 0.0, None, ALU.is_gt))
                            link(v.tensor_scalar(deg[:, b, 1:2], deg[:, b, 0:1], -1.0, 1.0, ALU.mult, ALU.add))
                            dve.wait_ge(gsum, t + 1)
                            link(v.tensor_tensor(upd[:, b, :], psG[:, b, 0:D], row[:, 0:D], ALU.add))
                            xt = X[:, bass.ds(t, 1), :].rearrange("p a d -> p (a d)")
                            link(v.scalar_tensor_tensor(xt, upd[:, b, :], 0.0, xt, ALU.max, ALU.add))
                            dve.wait_ge(dn.product, t + 1)
                            link(v.scalar_tensor_tensor(xt, dn.psF[:, b, 0:D], deg[:, b, 0:1], xt, ALU.mult, ALU.add))
                            link(v.scalar_tensor_tensor(xt, dn.psF[:, b, D:2 * D], deg[:, b, 1:2], xt, ALU.mult,
                                                        ALU.add))
                            dve.sem_inc(dn.product_free, 1)
                            dve.sem_inc(tdone, 1)
                    ch.leave(NCH)

                @block.scalar
                def _(act):
                    def counts(i, k):
                        t = i * CH + k
                        act.wait_ge(cturned, t + 1)
                        act.wait_ge(tdone, ago(i, k))
                        nc.scalar.activation(cntT[:, k % 2, 0, :], psC[:, k % 2, 0:P], ACT.Copy).then_inc(ccopied, 1)
                        nc.scalar.activation(cntT[0:R - P, k % 2, 1, :], psC[0:R - P, k % 2, P:2 * P],
                                             ACT.Copy).then_inc(ccopied, 1)
                    dn.run_act(act, tail=counts)

                @block.tensor
                def _(pe):
                    def counts(i, k):
                        t = i * CH + k
                        b = k % 2
                        pe.wait_ge(cready, t + 1)
                        pe.transpose(psC[:, b, 0:P], cnt[:, b, 0:P], ident[:, :])
                        pe.transpose(psC[0:R - P, b, P:2 * P], cnt[:, b, P:R], ident[:, :]).then_inc(cturned, 1)
                        pe.wait_ge(ccopied, t * 2 + 2)
                        pe.matmul(psG[:, b, 0:D], cntT[:, b, 0, :], relW[:, 0, :], start=True, stop=False)
                        pe.matmul(psG[:, b, 0:D], cntT[0:R - P, b, 1, :], relW[0:R - P, 1, :], start=False,
                                  stop=True).then_inc(gsum, 1)
                    pe.wait_ge(wloaded, 32)
                    dn.run_pe(pe, wl, extra=counts)

            end_phase()

    with ExitStack() as c:
        dn = Dense("ln4", c, 1)
        Z = sb("Z", [P, NT, D], c=c)
        zT = sb("zT", [P, KD, NT * P], c=c)
        wrc = sb("wrc", [P, KD, 1], c=c)
        brc = sb("brc", [P, 1], c=c)
        w1 = sb("f_w1", [P, KD, FF], c=c)
        w2 = sb("f_w2", [P, FF // P, D], c=c)
        b1 = sb("f_b1", [P, FF // P], c=c)
        b2 = sb("f_b2", [P, D], c=c)
        score = sb("score", [P, NT], c=c)
        srow = sb("srow", [P, NT * P], c=c)
        above = sb("above", [P, NT * P], mybir.dt.bfloat16, c=c)
        tie = sb("tie", [P, 3, P], c=c)
        rank = sb("rank", [P, 4, NT], c=c)
        HALF = CH * P // 2
        hid = sb("f_hid", [P, FF // P, 2 * HALF], c=c)
        psHid = ps("f_psH", [P, 2, 512], c)
        psY = ps("f_psY", [P, 2, 512], c)
        xland, wloaded, chain, scored, rowland = (sem(n) for n in ("w6_xl", "w6_loaded", "chain6", "scored", "rowland"))
        stored_s, zcopied, zfree, zTc = sem("stored_s"), sem("zcopied"), sem("zfree"), sem("zTc")
        hidp, gelu, yp, yd, hfree = sem("hidp"), sem("gelu"), sem("yp"), sem("yd"), sem("hfree")
        final, outd, ranked = sem("final"), sem("outd"), sem("ranked")
        YF = sb("YF", [P, NT, D], c=c)

        with nc.Block() as block:
            @block.sync
            def _(sp):
                with nc.allow_non_contiguous_dma(reason="one small vector, row j * 128 + p to partition p"):
                    sp.dma_start(wrc[:, :, :], a["L1_ffn_wr"].rearrange("(j p) o -> p j o", p=P)).then_inc(wloaded, 16)
                sp.dma_start(brc[:, :], a["L1_ffn_br"].partition_broadcast(P)).then_inc(wloaded, 16)
                sp.dma_start(w1[:, :, :], a["L1_ffn_w1"].rearrange("(j p) n -> p j n", p=P)).then_inc(xland, 16)
                sp.dma_start(w2[:, :, :], a["L1_ffn_w2"].rearrange("(j p) n -> p j n", p=P)).then_inc(xland, 16)
                with nc.allow_non_contiguous_dma(reason="one small vector, hidden unit j * 128 + p to partition p"):
                    sp.dma_start(b1[:, :], a["L1_ffn_b1"].rearrange("(j p) -> p j", p=P)).then_inc(xland, 16)
                sp.dma_start(b2[:, :], a["L1_ffn_b2"].partition_broadcast(P)).then_inc(xland, 16)
                sp.wait_ge(scored, NT)
                with nc.allow_non_contiguous_dma(reason="the scores, turned once"):
                    sp.dma_start(score_d.rearrange("(t p) o -> p (t o)", p=P), score[:, :]).then_inc(stored_s, 16)
                sp.wait_ge(stored_s, 16)
                sp.dma_start(srow[:, :], score_d.rearrange("n o -> (n o)").partition_broadcast(P)).then_inc(rowland, 16)
                with sp.Fori(0, NCH - 1) as i:
                    sp.wait_ge(final, i + 1)
                    sp.dma_start(out[bass.ds(i * (CH * P), CH * P), :].rearrange("(t p) d -> p t d", p=P),
                                 X[:, bass.ds(i * CH, CH), :]).then_inc(outd, 16)
                sp.wait_ge(final, NCH)
                t0 = (NCH - 1) * CH
                sp.dma_start(out[t0 * P:(NT - 1) * P, :].rearrange("(t p) d -> p t d", p=P), X[:, t0:NT - 1, :])\
                    .then_inc(outd, 16)
                sp.dma_start(out[(NT - 1) * P:N, :], X[0:LAST, NT - 1, :]).then_inc(outd, 16)
                sp.wait_ge(outd, 16 * (NCH + 1))

            @block.vector
            def _(dve):
                v = nc.vector
                ch = Chain(dve, chain)
                link = ch.link
                dve.sem_inc(dn.product_free, 1)
                dve.wait_ge(wloaded, 32)
                with dve.Fori(0, NCH) as i:
                    ch.enter(i, dn.LINKS)
                    dve.wait_ge(zfree, i + 1)
                    dn.vector(dve, ch, i)
                    for k in range(CH):
                        dve.wait_ge(dn.product, i * CH + k + 1)
                        v.tensor_tensor(score[:, bass.ds(i * CH + k, 1)], dn.psF[:, k % 2, 0:1], brc[:, :], ALU.add)\
                            .then_inc(scored, 1)
                        dve.wait_ge(scored, i * CH + k + 1)
                        dve.sem_inc(dn.product_free, 1)
                ch.leave(NCH)
                dve.wait_ge(rowland, 16)
                link(v.memset(rank[:, :, :], 0.0))
                for t in range(NT):
                    own = score[:, t:t + 1]
                    if t:
                        link(v.tensor_scalar(above[:, 0:t * P], srow[:, 0:t * P], own, 0.0, ALU.is_ge, ALU.add,
                                             accum_out=rank[:, 0, t:t + 1]))
                    n = min(P, N - t * P)
                    if t < NT - 1:
                        link(v.tensor_scalar(above[:, (t + 1) * P:N], srow[:, (t + 1) * P:N], own, 0.0, ALU.is_gt,
                                             ALU.add, accum_out=rank[:, 1, t:t + 1]))
                    blk = srow[:, t * P:t * P + n]
                    link(v.tensor_scalar(tie[:, 0, 0:n], blk, own, 0.0, ALU.is_gt, ALU.add,
                                         accum_out=rank[:, 2, t:t + 1]))
                    link(v.tensor_scalar(tie[:, 1, 0:n], blk, own, None, ALU.is_equal))
                    link(v.tensor_tensor(tie[:, 2, 0:n], ones[:, 0:n], before[:, 0:n], ALU.subtract))
                    link(v.tensor_tensor(tie[:, 2, 0:n], tie[:, 2, 0:n], ident[:, 0:n], ALU.subtract))
                    link(v.tensor_tensor_reduce(tie[:, 0, 0:n], tie[:, 1, 0:n], tie[:, 2, 0:n], 1.0, 0.0, ALU.mult,
                                                ALU.add, rank[:, 3, t:t + 1]))
                for j in range(1, 4):
                    link(v.tensor_tensor(rank[:, 0, :], rank[:, 0, :], rank[:, j, :], ALU.add))
                link(v.scalar_tensor_tensor(rank[:, 1, :], rank[:, 0, :], float(SELECTED), score[:, :], ALU.is_lt,
                                            ALU.mult))
                dve.wait_ge(xland, 64)
                with dve.Fori(0, NCH) as i:
                    ch.enter(i, 4)
                    dve.wait_ge(yd, i * CH + CH)
                    full = [P, CH, D]
                    y, xc, z = (m[:, bass.ds(i * CH, CH), :] for m in (YF, X, Z))
                    link(v.tensor_tensor(y, y, b2[:, :].unsqueeze(1).to_broadcast(full), ALU.add))
                    link(v.tensor_tensor(y, y, rank[:, 1, bass.ds(i * CH, CH)].unsqueeze(2).to_broadcast(full),
                                         ALU.mult))
                    link(v.tensor_tensor(z, z, y, ALU.add))
                    link(v.tensor_tensor(xc, xc, z, ALU.add))
                    dve.sem_inc(final, 1)
                ch.leave(NCH)

            @block.scalar
            def _(act):
                act.sem_inc(zfree, 1)

                def keep(i):
                    act.wait_ge(dn.normed, i + 1)
                    hold(act, "act")
                    nc.scalar.activation(Z[:, bass.ds(i * CH, CH), :], dn.xn[:, :, :], ACT.Copy).then_inc(zcopied, 1)
                    act.wait_ge(zcopied, i + 1)
                    act.sem_inc(zfree, 1)

                def keepT(i, k):
                    act.wait_ge(dn.copied, i * CH + k + 1)
                    hold(act, "act")
                    nc.scalar.activation(zT[:, :, bass.ds((i * CH + k) * P, P)], dn.xT[:, k, :, :], ACT.Copy)\
                        .then_inc(zTc, 1)
                dn.run_act(act, extra=keep, tail=keepT)
                act.wait_ge(xland, 64)
                with act.Fori(0, NCH) as i:
                    for m in range(FF // P):
                        for h in range(2):
                            act.wait_ge(hidp, i * (2 * FF // P) + 2 * m + h + 1)
                            if m == 0 and h == 0:
                                act.wait_ge(hfree, i + 1)
                            nc.scalar.activation(hid[:, m, h * HALF:(h + 1) * HALF], psHid[:, h, 0:HALF],
                                                 ACT.Gelu_apprx_tanh, bias=b1[:, m:m + 1]).then_inc(gelu, 1)
                    for k in range(CH):
                        act.wait_ge(yp, i * CH + k + 1)
                        hold(act, "act")
                        nc.scalar.activation(YF[:, bass.ds(i * CH + k, 1), :].rearrange("p a d -> p (a d)"),
                                             psY[:, k % 2, 0:D], ACT.Copy).then_inc(yd, 1)

            @block.tensor
            def _(pe):
                pe.wait_ge(wloaded, 32)
                dn.run_pe(pe, wrc)
                pe.wait_ge(zTc, NT)
                pe.wait_ge(xland, 64)
                pe.sem_inc(hfree, 1)
                NH = 2 * FF // P
                with pe.Fori(0, NCH) as i:
                    for m in range(FF // P):
                        for h in range(2):
                            n = 2 * m + h
                            if n < 2:
                                pe.wait_ge(ranked, i + 1)
                            else:
                                pe.wait_ge(gelu, i * NH + n - 1)
                            for j in range(KD):
                                ins = pe.matmul(psHid[:, h, 0:HALF], w1[:, j, m * P:(m + 1) * P],
                                                zT[:, j, bass.ds(i * (2 * HALF) + h * HALF, HALF)],
                                                start=(j == 0), stop=(j == KD - 1))
                            ins.then_inc(hidp, 1)
                    pe.wait_ge(gelu, i * NH + NH)
                    pe.sem_inc(ranked, 1)
                    for k in range(CH):
                        if k < 2:
                            pass
                        else:
                            pe.wait_ge(yd, i * CH + k - 1)
                        for m in range(FF // P):
                            ins = pe.matmul(psY[:, k % 2, 0:D], hid[:, m, k * P:(k + 1) * P],
                                            w2[:, m, :], start=(m == 0), stop=(m == FF // P - 1))
                        ins.then_inc(yp, 1)
                    pe.wait_ge(yd, i * CH + CH)
                    pe.sem_inc(hfree, 1)

            @block.gpsimd
            def _(pool):
                pool.sem_inc(ranked, 1)
    ctx.close()


_INS = ["x", "src", "dst", "edge_type_200", "edge_weight", "L0_gnn_Ws", "L0_gnn_bs", "L0_gnn_aw", "L0_gnn_ab",
        "L0_ffn_gate_w", "L0_ffn_gate_b", "L0_ffn_w1", "L0_ffn_w2", "L0_ffn_w3", "L1_gnn_rel_emb",
        "L1_gnn_weight_neighbor", "L1_gnn_a", "L1_gnn_W3", "L1_gnn_loop_weight", "L1_gnn_evolve_loop_weight",
        "L1_ffn_attention_mask", "L1_ffn_wr", "L1_ffn_br", "L1_ffn_w1", "L1_ffn_b1", "L1_ffn_w2", "L1_ffn_b2"]
DEBUG = ()


def kernel(**inputs):
    import numpy as _np
    import concourse.bacc as _bacc
    from concourse import mybir as _mybir
    from concourse.bass_utils import run_bass_kernel_spmd as _run

    nc = _bacc.Bacc("TRN2", target_bir_lowering=False, num_devices=1)
    arrays, args = {}, {}
    for name in _INS:
        v = _np.ascontiguousarray(inputs[name])
        arrays[f"in_{name}_dram"] = v
        args[name] = nc.dram_tensor(f"in_{name}_dram", v.shape, _mybir.dt.from_np(v.dtype), kind="ExternalInput").ap()
    out = nc.dram_tensor("out_0_dram", (args["x"].shape[0], args["x"].shape[1]), F32, kind="ExternalOutput").ap()
    build(nc, args, out, DEBUG)
    r = _run(nc, [arrays], core_ids=[0])
    return r.results[0]["out_0_dram"]
```

```python
from contextlib import ExitStack

import concourse.bass as bass
from concourse import mybir

F32 = mybir.dt.float32
I32 = mybir.dt.int32
ALU = mybir.AluOpType
ACT = mybir.ActivationFunctionType
AX = mybir.AxisListType

P = 128
DEPTH = 4
TPG = 4
TPU = 2


class Chain:

    def __init__(self, eng, sem):
        self.eng, self.sem, self.n, self.i, self.per = eng, sem, 0, None, 0

    def value(self):
        return self.n if self.i is None else self.i * self.per + (self.n - self.start * self.per)

    def link(self, ins):
        ins.then_inc(self.sem, 1)
        self.n += 1
        self.eng.wait_ge(self.sem, self.value())

    def enter(self, i, per, start=0):
        self.i, self.per, self.at, self.start = i, per, self.n, start

    def leave(self, end):
        assert self.n - self.at == self.per, (self.n - self.at, self.per)
        self.n, self.i = self.at + self.per * (end - self.start), None


def build(nc, a, out):
    N, D = a["x"].shape
    E = a["src"].shape[0]
    NT = -(-N // P)
    LAST = N - (NT - 1) * P
    EP = next(p for p in range(P, 0, -1) if E % p == 0)
    EC = E // EP
    H, _, O = a["L0_gnn_Ws"].shape
    R = a["L1_gnn_rel_emb"].shape[0]
    NE, _, FH = a["L0_ffn_w1"].shape
    FF = a["L1_ffn_w1"].shape[1]
    KD = D // P
    UNIT = TPU * P
    UNITS = (E + NT * (UNIT - 1)) // UNIT
    GROUPS = -(-UNITS * TPU // TPG)
    GROUPS = -(-GROUPS // DEPTH) * DEPTH
    ST = GROUPS * TPG
    UNITS = ST // TPU
    MT = (2 * N + NE * (P - 1)) // P
    MT += -MT % DEPTH
    W0 = D + 2 * H
    A0 = D + H
    W1 = D + 2
    A1 = W1 + R
    CH = 5
    NCH = NT // CH
    SELECTED = max(1, N // 2) - 1
    assert NT % CH == 0 and D == 2 * P and H * O == D and R > P

    ctx = ExitStack()

    def dram(name, shape, dt):
        return nc.dram_tensor(name, shape, dt).ap()

    rec_d = [dram(f"records{l}", (P * ST, 4), I32) for l in range(2)]
    table0 = dram("table0", (NT * P, W0), F32)
    table1 = dram("table1", (NT * P, W1), F32)
    expert_in = dram("expert_in", (MT * P, D), F32)
    expert_out = dram("expert_out", (MT * P, D), F32)
    score_d = dram("score_d", (NT * P, 1), F32)

    def sb(name, shape, dt=F32, c=ctx):
        return c.enter_context(nc.sbuf_tensor(name, shape, dt))

    def ps(name, shape, c):
        return c.enter_context(nc.psum_tensor(name, shape, F32))

    phase_sems = []

    def sem(name):
        phase_sems.append(nc.alloc_semaphore(name=name))
        return phase_sems[-1]

    def end_phase():
        nc.clear_and_free_semaphores(list(phase_sems))
        phase_sems.clear()
        nc.all_engine_barrier()

    X = sb("X", [P, NT, D])
    wcol = sb("wcol", [P, 3 * KD])
    relT = sb("relT", [P, KD, R])
    rec_s = [sb(f"rec_s{l}", [EP, EC, 4], I32) for l in range(2)]
    slot = [sb(f"slot{l}", [EP, EC], I32) for l in range(2)]
    wts = sb("wts", [P, 2, NT])
    tokslot = sb("tokslot", [P, 2 * NT], I32)
    unit_tile = [sb(f"unit_tile{l}", [P, UNITS], I32) for l in range(2)]
    ident = sb("ident", [P, P])
    iota = sb("iota", [P, R])
    ones = sb("ones", [P, P])
    before = sb("before", [P, P])
    padrow = sb("padrow", [P, NT])
    eps = sb("eps", [P, 1])
    turn = {e: ctx.enter_context(nc.semaphore(f"turn_{e}")) for e in ("pool", "dve", "act", "sp")}

    def hold(eng, name):
        eng.sem_inc(turn[name], 1)

    class Dense:

        def __init__(self, tag, c, width):
            self.width = width
            self.xc = sb(tag + "_xc", [P, CH, D], c=c)
            self.xn = sb(tag + "_xn", [P, CH, D], c=c)
            self.junk = sb(tag + "_junk", [P, D], c=c)
            self.st = sb(tag + "_st", [P, 5, CH], c=c)
            self.xT = sb(tag + "_xT", [P, CH, KD, P], c=c)
            self.psT = ps(tag + "_psT", [P, 2, 512], c)
            self.psF = ps(tag + "_psF", [P, 2, 512], c)
            (self.centred, self.squared, self.std, self.normed, self.turned, self.turned_free, self.copied,
             self.product, self.product_free, self.xn_free, self.xT_free) = (
                sem(tag + "_" + n) for n in ("centred", "squared", "std", "normed", "turned", "turned_free", "copied",
                                             "product", "product_free", "xn_free", "xT_free"))

        def vector(self, dve, ch, c):
            x = X[:, bass.ds(c * CH, CH), :]
            st = self.st
            hold(dve, "dve")
            ch.link(dve.tensor_reduce(st[:, 0, :], x, AX.X, ALU.add))
            ch.link(dve.tensor_scalar(st[:, 1, :], st[:, 0, :], -1.0 / D, None, ALU.mult))
            dve.tensor_tensor(self.xc[:, :, :], x, st[:, 1, :].unsqueeze(2).to_broadcast([P, CH, D]),
                              ALU.add).then_inc(self.centred, 1)
            dve.wait_ge(self.std, c + 1)
            ch.link(dve.reciprocal(st[:, 4, :], st[:, 3, :]))
            dve.wait_ge(self.xn_free, c + 1)
            dve.tensor_tensor(self.xn[:, :, :], self.xc[:, :, :],
                              st[:, 4, :].unsqueeze(2).to_broadcast([P, CH, D]), ALU.mult)\
               .then_inc(self.normed, 1)

        LINKS = 3

        def scalar_std(self, act, c):
            act.wait_ge(self.centred, c + 1)
            for k in range(CH):
                if k:
                    act.wait_ge(self.squared, c * CH + k)
                nc.scalar.activation(self.junk[:, :], self.xc[:, k, :], ACT.Square,
                                     accum_out=self.st[:, 2, k:k + 1]).then_inc(self.squared, 1)
            act.wait_ge(self.squared, c * CH + CH)
            nc.scalar.activation(self.st[:, 3, :], self.st[:, 2, :], ACT.Sqrt, bias=eps[:, :],
                                 scale=1.0 / D).then_inc(self.std, 1)

        def scalar_copy(self, act, c, k):
            act.wait_ge(self.turned, c * CH + k + 1)
            act.wait_ge(self.xT_free, c + 1)
            nc.scalar.activation(self.xT[:, k, :, :],
                                 self.psT[:, k % 2, 0:D].rearrange("p (a b) -> p a b", a=KD),
                                 ACT.Copy).then_inc(self.copied, 1)

        def free_at(self, c, k):
            return c * CH + (k if k < 1 else k - 1) + 1

        def transposes(self, pe, c, k):
            if k == 0:
                pe.wait_ge(self.normed, c + 1)
            pe.wait_ge(self.turned_free, self.free_at(c, k))
            for j in range(KD):
                ins = pe.transpose(self.psT[:, k % 2, j * P:(j + 1) * P], self.xn[:, k, j * P:(j + 1) * P],
                                   ident[:, :])
            ins.then_inc(self.turned, 1)
            if k == CH - 1:
                pe.wait_ge(self.turned, c * CH + CH)
                pe.sem_inc(self.xn_free, 1)

        def products(self, pe, c, k, weight):
            pe.wait_ge(self.copied, c * CH + k + 1)
            pe.wait_ge(self.product_free, self.free_at(c, k))
            for j in range(KD):
                ins = pe.matmul(self.psF[:, k % 2, 0:self.width], self.xT[:, k, j, :],
                                weight[:, j, 0:self.width], start=(j == 0), stop=(j == KD - 1))
            ins.then_inc(self.product, 1)
            if k == CH - 1:
                pe.wait_ge(self.product, c * CH + CH)
                pe.sem_inc(self.xT_free, 1)

        def credits_pe(self, pe):
            pe.sem_inc(self.xn_free, 1)
            pe.sem_inc(self.xT_free, 1)

        def credit_act(self, act):
            act.sem_inc(self.turned_free, 1)

        def credit_dve(self, dve):
            dve.sem_inc(self.product_free, 1)

        def run_pe(self, pe, weight, extra=None):
            self.credits_pe(pe)
            with pe.Fori(0, NCH) as c:
                for k in range(CH):
                    self.transposes(pe, c, k)
                    if k:
                        self.products(pe, c, k - 1, weight)
                        if extra:
                            extra(c, k - 1)
                self.products(pe, c, CH - 1, weight)
                if extra:
                    extra(c, CH - 1)

        def run_act(self, act, extra=None, tail=None):
            self.credit_act(act)
            with act.Fori(0, NCH) as c:
                self.scalar_std(act, c)
                if extra:
                    extra(c)
                for k in range(CH):
                    self.scalar_copy(act, c, k)
                    act.wait_ge(self.copied, c * CH + k + 1)
                    act.sem_inc(self.turned_free, 1)
                    if tail:
                        tail(c, k)

    class Sort:

        def __init__(self, tag, c, rows, cols, buckets, unit, units, oh=None, run=None):
            self.rows, self.cols, self.B, self.unit, self.units = rows, cols, buckets, unit, units
            self.oh = oh if oh is not None else sb(tag + "_oh", [rows, buckets, cols + 1], c=c)
            self.run = run if run is not None else sb(tag + "_run", [rows, buckets, cols + 1], c=c)
            self.tot = sb(tag + "_tot", [rows, buckets], c=c)
            self.small = sb(tag + "_small", [P, 8, buckets], c=c)
            self.smalli = sb(tag + "_smalli", [P, 2, buckets], I32, c=c)
            self.ucount = sb(tag + "_ucount", [P, units], c=c)
            self.psum = ps(tag + "_ps", [P, 512], c)
            self.totals, self.sums = sem(tag + "_totals"), sem(tag + "_sums")

        def tensor(self, pe):
            pe.wait_ge(self.totals, 1)
            pe.matmul(self.psum[0:P, 0:self.B], before[0:self.rows, :], self.tot[:, :], start=True, stop=True)
            pe.matmul(self.psum[0:P, self.B:2 * self.B], ones[0:self.rows, :], self.tot[:, :], start=True,
                      stop=True).then_inc(self.sums, 1)

        def vector(self, dve, link, bucket, tile_of_unit, where):
            B, rows, cols = self.B, self.rows, self.cols
            oh, run, s, si = self.oh, self.run, self.small, self.smalli
            full = [rows, B, cols]
            link(dve.tensor_tensor(oh[:, :, 1:], bucket.unsqueeze(1).to_broadcast(full),
                                   iota[0:rows, 0:B].unsqueeze(2).to_broadcast(full), ALU.is_equal))
            dve.tensor_reduce(self.tot[:, :], oh[:, :, 1:], AX.X, ALU.add).then_inc(self.totals, 1)
            dve.wait_ge(self.sums, 1)
            link(dve.tensor_scalar(si[:, 0, :], self.psum[:, B:2 * B], float(self.unit - 1), None, ALU.add))
            link(dve.tensor_scalar(si[:, 1, :], si[:, 0, :], self.unit.bit_length() - 1, None,
                                   ALU.arith_shift_right))
            link(dve.tensor_copy(s[:, 0, :], si[:, 1, :]))
            link(dve.tensor_tensor_scan(s[:, 1, :], s[:, 0, :], s[:, 0, :], 0.0, ALU.add, ALU.max))
            link(dve.tensor_tensor(s[:, 2, :], s[:, 1, :], s[:, 0, :], ALU.subtract))
            link(dve.scalar_tensor_tensor(s[:, 3, :], s[:, 2, :], float(self.unit), self.psum[:, 0:B],
                                          ALU.mult, ALU.add))
            link(dve.tensor_tensor(s[0:rows, 4, :], s[0:rows, 3, :], self.tot[:, :], ALU.add))
            link(dve.tensor_copy(oh[:, 0, 0:1], s[0:rows, 3, 0:1]))
            link(dve.tensor_tensor(oh[:, 1:, 0], s[0:rows, 3, 1:], s[0:rows, 4, 0:B - 1], ALU.subtract))
            flat = "p b c -> p (b c)"
            link(dve.tensor_tensor_scan(run[:, :, :].rearrange(flat), oh[:, :, :].rearrange(flat),
                                        oh[:, :, :].rearrange(flat), 0.0, ALU.add, ALU.max))
            link(dve.tensor_tensor(run[:, :, 1:], run[:, :, 1:], oh[:, :, 1:], ALU.mult))
            link(dve.tensor_reduce(where, run[:, :, 1:].rearrange("p b c -> p c b"), AX.X, ALU.max))
            link(dve.tensor_scalar(where, where, -1.0, 0.0, ALU.add, ALU.max))
            view = run[:, :, :].rearrange(flat)[:, 0:B * min(self.units, cols)]
            n = min(self.units, cols)
            for u in range(0, self.units, n):
                m = min(n, self.units - u)
                v = view[:, 0:B * m].rearrange("p (u b) -> p u b", b=B)
                link(dve.tensor_tensor(v, self.unumber[0:rows, u:u + m].unsqueeze(2).to_broadcast([rows, m, B]),
                                       s[0:rows, 2, :].unsqueeze(1).to_broadcast([rows, m, B]), ALU.is_ge))
                link(dve.tensor_reduce(self.ucount[0:rows, u:u + m], v, AX.X, ALU.add))
            link(dve.tensor_scalar(tile_of_unit, self.ucount[0:rows, :], -1.0, None, ALU.add))

    BUFS = 5
    COLS = next(n for n in range(20, 0, -1) if EC % (BUFS * n) == 0)
    TURNS = EC // (BUFS * COLS)
    RCOLS = COLS
    stage_slot = sb("stage_slot", [EP, BUFS, COLS], I32)
    stage_rec = sb("stage_rec", [EP, BUFS, COLS, 4], I32)

    def scatter_sems(tag):
        return sem(tag + "_staged"), [sem(f"{tag}_landed{b}") for b in range(BUFS)]

    def scatter_records(pool, l, sems, begin, end):
        staged, landed = sems

        def turn(i, first):
            for b in range(BUFS):
                if not first:
                    pool.wait_ge(landed[b], (i - begin) * (16 * COLS))
                    hold(pool, "pool")
                at = (i * BUFS + b) * COLS
                nc.gpsimd.tensor_copy(stage_slot[:, b, :], slot[l][:, bass.ds(at, COLS)]).then_inc(staged, 1)
                nc.gpsimd.tensor_copy(stage_rec[:, b, :, :], rec_s[l][:, bass.ds(at, COLS), :]).then_inc(staged, 1)
                pool.wait_ge(staged, (i - begin) * (2 * BUFS) + 2 * b + 2)
                hold(pool, "pool")
                for k in range(COLS):
                    pool.indirect_dma_start(
                        out=rec_d[l], out_offset=bass.IndirectOffsetOnAxis(ap=stage_slot[:, b, k:k + 1], axis=0),
                        in_=stage_rec[:, b, k, :], in_offset=None).then_inc(landed[b], 16)
        turn(begin, True)
        if end - begin > 1:
            with pool.Fori(begin + 1, end) as i:
                turn(i, False)
        for b in range(BUFS):
            pool.wait_ge(landed[b], 16 * COLS * (end - begin))

    with ExitStack() as c:
        big = [sb(f"sort_{n}", [P, NT, EC + 1], c=c) for n in ("oh", "run")]
        unumber = sb("unumber", [P, UNITS], c=c)
        sort = [Sort(f"sort{l}", c, EP, EC, NT, UNIT, UNITS, *(b[0:EP, :, :] for b in big)) for l in range(2)]
        for s in sort:
            s.unumber = unumber
        raw = sb("raw", [EP, 3, EC], I32, c=c)
        elem = sb("elem", [EP, EC], c=c)
        keyi = sb("keyi", [EP, EC], I32, c=c)
        keyf = sb("keyf", [EP, EC], c=c)
        wheref = sb("wheref", [EP, EC], c=c)
        slot_t = sb("slot_t", [EP, 3, EC], I32, c=c)
        ts = slot_t[:, :, :]
        blank = sb("blank", [P, ST, 4], I32, c=c)

        loaded, xloaded, consts, zeroed = sem("edges_loaded"), sem("x_loaded"), sem("consts"), sem("x_zeroed")
        blanked, blank_ready, ready = sem("blanked"), sem("blank_ready"), [sem("slots0_ready"), sem("slots1_ready")]
        chain = sem("chain1")
        records0 = scatter_sems("rec0")

        dn = Dense("ln0", c, W0)
        after = big[0][:, :, :].rearrange("p t e -> p (t e)")
        w3r = after[:, 0:9 * KD * D].rearrange("p (j n) -> p j n", j=3 * KD)
        arow = after[:, 9 * KD * D:9 * KD * D + 3 * D]
        rel = sb("rel", [P, 2, D], c=c)
        relwb = sb("relwb", [P, KD, P], c=c)
        relrow = sb("relrow", [P, R], c=c)
        relation = sb("relation", [EP, EC], c=c)
        relpick = big[1][0:EP, :, :].rearrange("p t e -> p (t e)")[:, 0:RCOLS * R].rearrange("p (k r) -> p k r", k=RCOLS)
        psR = ps("psR1", [P, 2, 512], c)
        rel_loaded, rel_t, rel_c = sem("rel_loaded"), sem("rel_turned"), sem("rel_copied")
        rel_p, rel_scored = sem("rel_product1"), sem("rel_scored")
        wcat = sb("wcat", [P, KD, W0], c=c)
        awb = sb("awb", [P, H, 2 * O + 1], c=c)
        biasrow = sb("biasrow", [P, W0], c=c)
        awprod = sb("awprod", [P, H, O], c=c)
        frow = sb("frow", [P, 2, W0], c=c)
        wloaded, wready, fready, fstored = sem("wloaded"), sem("wready"), sem("fready"), [sem("fst0"), sem("fst1")]

        with nc.Block() as block:
            @block.sync
            def _(sp):
                flat = "(p c) -> p c"
                sp.dma_start(raw[:, 0, :], a["src"].rearrange(flat, p=EP)).then_inc(loaded, 16)
                sp.dma_start(raw[:, 1, :], a["dst"].rearrange(flat, p=EP)).then_inc(loaded, 16)
                sp.dma_start(raw[:, 2, :], a["edge_type_200"].rearrange(flat, p=EP)).then_inc(loaded, 16)
                sp.dma_start(elem[:, :], a["edge_weight"].rearrange(flat, p=EP)).then_inc(loaded, 16)
                sp.dma_start(X[:, 0:NT - 1, :], a["x"][0:(NT - 1) * P, :].rearrange("(t p) d -> p t d", p=P))\
                    .then_inc(xloaded, 16)
                sp.wait_ge(zeroed, 1)
                sp.dma_start(X[0:LAST, NT - 1, :], a["x"][(NT - 1) * P:N, :]).then_inc(xloaded, 16)
                for j in range(KD):
                    sp.dma_start(wcat[:, j, 0:D].rearrange("p (h o) -> p h o", h=H),
                                 a["L0_gnn_Ws"][:, j * P:(j + 1) * P, :].rearrange("h p o -> p h o"))\
                        .then_inc(wloaded, 16)
                sp.dma_start(awb[:, :, :].rearrange("p h o -> p (h o)"),
                             a["L0_gnn_aw"].rearrange("h o -> (h o)").partition_broadcast(P)).then_inc(wloaded, 16)
                sp.dma_start(biasrow[:, 0:D],
                             a["L0_gnn_bs"].rearrange("h o -> (h o)").partition_broadcast(P)).then_inc(wloaded, 16)
                sp.dma_start(rel[:, 0, :], a["L1_gnn_rel_emb"][0:P, :]).then_inc(rel_loaded, 16)
                sp.dma_start(rel[0:R - P, 1, :], a["L1_gnn_rel_emb"][P:R, :]).then_inc(rel_loaded, 16)
                sp.wait_ge(blank_ready, 1)
                for l in range(2):
                    sp.dma_start(rec_d[l].rearrange("(p t) w -> p (t w)", p=P),
                                 blank[:, :, :].rearrange("p t w -> p (t w)")).then_inc(blanked, 16)
                with sp.Fori(0, NCH) as i:
                    for k in range(CH):
                        sp.wait_ge(fready, i * CH + k + 1)
                        sp.dma_start(table0[bass.ds((i * CH + k) * P, P), :], frow[:, k % 2, :])\
                            .then_inc(fstored[k % 2], 16)
                sp.wait_ge(ready[1], 1)
                sp.dma_start(arow, a["L1_gnn_a"].rearrange("n o -> (n o)").partition_broadcast(P))\
                    .then_inc(rel_loaded, 16)
                sp.dma_start(w3r[:, :, :], a["L1_gnn_W3"].rearrange("(j p) n -> p j n", p=P)).then_inc(rel_loaded, 16)
                sp.wait_ge(fstored[0], 16 * 3 * NCH)
                sp.wait_ge(fstored[1], 16 * 2 * NCH)

            @block.gpsimd
            def _(pool):
                g = nc.gpsimd
                g.memset(ident[:, :], 0.0).then_inc(consts, 1)
                g.memset(before[:, :], 1.0).then_inc(consts, 1)
                g.memset(ones[:, :], 1.0).then_inc(consts, 1)
                g.memset(eps[:, :], 1e-5).then_inc(consts, 1)
                g.memset(padrow[:, :], 0.0).then_inc(consts, 1)
                g.memset(blank[:, :, :], 0).then_inc(consts, 1)
                g.iota(iota[:, :], [[1, R]], base=0, channel_multiplier=0,
                       allow_small_or_imprecise_dtypes=True).then_inc(consts, 1)
                g.iota(unumber[:, :], [[1, UNITS]], base=0, channel_multiplier=0,
                       allow_small_or_imprecise_dtypes=True).then_inc(consts, 1)
                pool.wait_ge(consts, 8)
                g.affine_select(out=ident[:, :], in_=ident[:, :], compare_op=ALU.not_equal, fill=1.0, base=0,
                                pattern=[[-1, P]], channel_multiplier=1).then_inc(consts, 1)
                g.affine_select(out=before[:, :], in_=before[:, :], compare_op=ALU.is_gt, fill=0.0, base=0,
                                pattern=[[1, P]], channel_multiplier=-1).then_inc(consts, 1)
                g.affine_select(out=padrow[:, NT - 1:NT], in_=padrow[:, NT - 1:NT], compare_op=ALU.is_gt, fill=1.0,
                                base=LAST, pattern=[[0, 1]], channel_multiplier=-1).then_inc(consts, 1)
                g.memset(blank[:, :, 0:1], 4 * P).then_inc(blank_ready, 1)
                pool.wait_ge(blanked, 32)
                pool.wait_ge(ready[0], 1)
                scatter_records(pool, 0, records0, 0, TURNS)

            @block.vector
            def _(dve):
                ch = Chain(dve, chain)
                link = ch.link
                v = nc.vector
                v.memset(X[:, NT - 1, :], 0.0).then_inc(zeroed, 1)
                dve.sem_inc(dn.product_free, 1)
                dve.wait_ge(consts, 11)
                dve.wait_ge(loaded, 64)

                def place(l):
                    key, other = (0, 1) if l == 0 else (1, 0)
                    link(v.tensor_scalar(rec_s[l][:, :, 0], raw[:, key, :], P - 1, None, ALU.bitwise_and))
                    link(v.tensor_copy(rec_s[l][:, :, 1], raw[:, other, :]))
                    if l == 0:
                        link(v.tensor_copy(rec_s[l][:, :, 2:3].bitcast(F32), elem[:, :].unsqueeze(2)))
                    else:
                        link(v.tensor_copy(rec_s[l][:, :, 2], raw[:, 2, :]))
                    if l == 0:
                        link(v.memset(rec_s[l][:, :, 3], 0))
                    link(v.tensor_scalar(keyi[:, :], raw[:, key, :], 7, None, ALU.arith_shift_right))
                    link(v.tensor_copy(keyf[:, :], keyi[:, :]))
                    sort[l].vector(dve, link, keyf[:, :], unit_tile[l][0:EP, :], wheref[:, :])
                    link(v.tensor_copy(ts[:, 0, :], wheref[:, :]))
                    link(v.tensor_scalar(ts[:, 1, :], ts[:, 0, :], P - 1, None, ALU.bitwise_and))
                    link(v.tensor_scalar(ts[:, 2, :], ts[:, 0, :], 7, None, ALU.arith_shift_right))
                    v.scalar_tensor_tensor(slot[l][:, :], ts[:, 1, :], float(ST), ts[:, 2, :], ALU.mult,
                                           ALU.add).then_inc(ready[l], 1)
                    dve.wait_ge(ready[l], 1)

                place(0)
                dve.wait_ge(wloaded, 16 * (KD + 2))
                for part, off in ((1, 0), (0, H)):
                    aw = awb[:, :, part * O:(part + 1) * O]
                    for j in range(KD):
                        link(v.tensor_tensor(awprod[:, :, :], wcat[:, j, 0:D].rearrange("p (h o) -> p h o", h=H),
                                             aw, ALU.mult))
                        link(v.tensor_reduce(wcat[:, j, D + off:D + off + H], awprod[:, :, :], AX.X, ALU.add))
                    link(v.tensor_tensor(awprod[:, :, :], biasrow[:, 0:D].rearrange("p (h o) -> p h o", h=H),
                                         aw, ALU.mult))
                    link(v.tensor_reduce(biasrow[:, D + off:D + off + H], awprod[:, :, :], AX.X, ALU.add))
                dve.sem_inc(wready, 1)
                dve.wait_ge(xloaded, 32)

                def features(i):
                    dn.vector(dve, ch, i)
                    for k in range(CH):
                        dve.wait_ge(dn.product, i * CH + k + 1)
                        if not (isinstance(i, int) and k < 2):
                            dve.wait_ge(fstored[k % 2], (i * (3 - k % 2) + k // 2) * 16)
                        v.tensor_tensor(frow[:, k % 2, :], dn.psF[:, k % 2, 0:W0], biasrow[:, :], ALU.add)\
                            .then_inc(fready, 1)
                        dve.wait_ge(fready, i * CH + k + 1)
                        dve.sem_inc(dn.product_free, 1)
                features(0)
                with dve.Fori(1, NCH) as i:
                    ch.enter(i, dn.LINKS, 1)
                    features(i)
                ch.leave(NCH)
                place(1)
                dve.wait_ge(rel_loaded, 64)
                link(v.tensor_tensor(w3r[:, :, :], w3r[:, :, :],
                                     arow.unsqueeze(1).to_broadcast([P, 3 * KD, 3 * D]), ALU.mult))
                link(v.tensor_reduce(wcol[:, :], w3r[:, :, :], AX.X, ALU.add))
                for j in range(KD):
                    link(v.tensor_scalar(relwb[:, j, :], ones[:, :], wcol[:, 2 * KD + j:2 * KD + j + 1], None,
                                         ALU.mult))
                dve.wait_ge(rel_t, 1)
                v.tensor_copy(relT[:, :, :], psR[:, 0, 0:KD * R].rearrange("p (j r) -> p j r", j=KD))\
                    .then_inc(rel_c, 1)
                dve.wait_ge(rel_p, 1)
                link(v.tensor_copy(relrow[:, :], psR[:, 1, 0:R]))
                link(v.tensor_copy(relation[:, :], raw[:, 2, :]))
                dve.sem_inc(rel_scored, 1)
                with dve.Fori(0, EC // RCOLS) as i:
                    dve.wait_ge(rel_scored, i * RCOLS + 1)
                    for k in range(RCOLS):
                        at = i * RCOLS + k
                        v.scalar_tensor_tensor(relpick[:, k, :], iota[0:EP, :], relation[:, bass.ds(at, 1)],
                                               relrow[0:EP, :], ALU.is_equal, ALU.mult,
                                               accum_out=rec_s[1][:, bass.ds(at, 1), 3].bitcast(F32))\
                            .then_inc(rel_scored, 1)
                dve.wait_ge(rel_scored, EC + 1)

            @block.scalar
            def _(act):
                dn.run_act(act)

            @block.tensor
            def _(pe):
                pe.wait_ge(consts, 11)
                sort[0].tensor(pe)
                pe.wait_ge(wready, 1)
                dn.run_pe(pe, wcat)
                sort[1].tensor(pe)
                pe.wait_ge(rel_loaded, 64)
                for j in range(KD):
                    pe.transpose(psR[:, 0, j * R:j * R + P], rel[:, 0, j * P:(j + 1) * P], ident[:, :])
                    ins = pe.transpose(psR[:, 0, j * R + P:(j + 1) * R], rel[0:R - P, 1, j * P:(j + 1) * P],
                                       ident[0:R - P, 0:R - P])
                ins.then_inc(rel_t, 1)
                pe.wait_ge(rel_c, 1)
                for j in range(KD):
                    ins = pe.matmul(psR[:, 1, 0:R], relwb[:, j, :], relT[:, j, :], start=(j == 0),
                                    stop=(j == KD - 1))
                ins.then_inc(rel_p, 1)

    end_phase()

    def ring(G):
        assert G % DEPTH == 0

        def pipeline(eng, ahead, behind, step):
            for s in range(-ahead, DEPTH):
                step(s, None)
            with eng.Fori(1, G // DEPTH - 1) as q:
                for r in range(DEPTH):
                    step(None, (q, r))
            for s in range(G - DEPTH, G + behind):
                step(s, None)

        def locate(s, dyn, shift):
            if dyn is None:
                g = s + shift
                return None if g < 0 or g >= G else (g, g // DEPTH, g % DEPTH)
            q, r = dyn
            return q * DEPTH + (r + shift), q + (r + shift) // DEPTH, (r + shift) % DEPTH

        def back(eng, s, g, n, per=1, extra=0):
            if not isinstance(g, int) or g - n >= 0:
                eng.wait_ge(s, (g - n + 1) * per + extra)
        return pipeline, locate, back

    def edge_phase(l, c, table, width, accw, acc, rec, own_off, own_n, heads, post):
        tag = f"e{l}_"
        rows = sb(tag + "rows", [P, DEPTH, TPG, accw if l else width], c=c)
        gidx = sb(tag + "gidx", [P, DEPTH, TPG], I32, c=c)
        oh = sb(tag + "oh", [P, DEPTH, TPG, P], c=c)
        ohT = sb(tag + "ohT", [P, 2, TPG, P], c=c)
        ownv = sb(tag + "ownv", [P, DEPTH, 2, own_n], c=c)
        sc = sb(tag + "sc", [P, 2, TPG, heads], c=c)
        psT = ps(tag + "psT", [P, 2, 512], c)
        psA = ps(tag + "psA", [P, 2, 512], c)
        psO = ps(tag + "psO", [P, 4, 512], c)
        names = ("oh_ready", "turned", "ohT_ready", "own_e", "own_used", "score", "weight", "payload",
                 "summed", "added", "gidx_ready", "counted", "rec_loaded", "table_done", "acc_zero")
        S = {n: sem(tag + n) for n in names}
        fetched = [sem(tag + f"rows_landed{r}") for r in range(DEPTH)]
        ownland = [sem(tag + f"own_landed{r}") for r in range(DEPTH)]
        chain = sem(tag + "chain")
        pipeline, locate, back = ring(GROUPS)

        with nc.Block() as block:
            @block.sync
            def _(sp):
                sp.dma_start(rec[:, :, :].rearrange("p t w -> p (t w)"),
                             rec_d[l].rearrange("(p t) w -> p (t w)", p=P)).then_inc(S["rec_loaded"], 16)
                if post.get("sync"):
                    post["sync"](sp, S)

                def step(s, dyn):
                    at = locate(s, dyn, 0)
                    if at is None:
                        return
                    g, q, r = at
                    back(sp, S["own_e"], g, DEPTH)
                    hold(sp, "sp")
                    for j in range(2):
                        t = sp.value_load(unit_tile[l][0:1, bass.ds(g * 2 + j, 1)], min_val=0, max_val=NT - 1)
                        sp.dma_start(ownv[:, r, j, :], table[bass.ds(t * P, P), own_off:own_off + own_n])\
                            .then_inc(ownland[r], 16)
                pipeline(sp, 0, 0, step)

            @block.gpsimd
            def _(pool):
                def step(s, dyn):
                    at = locate(s, dyn, 0)
                    if at is None:
                        return
                    g, q, r = at
                    back(pool, S["summed"], g, DEPTH)
                    pool.wait_ge(S["gidx_ready"], g + 1)
                    hold(pool, "pool")
                    for t in range(TPG):
                        pool.indirect_dma_start(
                            out=rows[:, r, t, 0:width], out_offset=None, in_=table,
                            in_offset=bass.IndirectOffsetOnAxis(ap=gidx[:, r, t:t + 1], axis=0))\
                            .then_inc(fetched[r], 16)
                pipeline(pool, 0, 0, step)

            @block.vector
            def _(dve):
                v = nc.vector
                v.memset(acc[:, :, :], 0.0).then_inc(S["acc_zero"], 1)
                dve.wait_ge(S["acc_zero"], 1)
                dve.wait_ge(S["rec_loaded"], 16)
                if post.get("bulk"):
                    post["bulk"](dve, S, chain)

                def onehots(at):
                    g, q, r = at
                    back(dve, S["summed"], g, DEPTH)
                    v.tensor_tensor(oh[:, r, :, :], rec[:, bass.ds(g * TPG, TPG), 0:1].to_broadcast([P, TPG, P]),
                                    iota[:, 0:P].unsqueeze(1).to_broadcast([P, TPG, P]), ALU.is_equal)\
                        .then_inc(S["oh_ready"], 1)

                def tiles_of(at):
                    g, q, r = at
                    hold(dve, "dve")
                    return [dve.value_load(unit_tile[l][0:1, bass.ds(g * 2 + j, 1)], min_val=0, max_val=NT - 1)
                            for j in range(2)]

                def add(at, tiles, j):
                    g, q, r = at
                    if j == 0:
                        dve.wait_ge(S["summed"], g + 1)
                    if not (isinstance(g, int) and g == 0 and j == 0):
                        dve.wait_ge(S["added"], g * 2 + j)
                    d = acc[:, bass.ds(tiles[j], 1), :].rearrange("p a w -> p (a w)")
                    v.tensor_tensor(d, d, psO[:, 2 * (r % 2) + j, 0:accw], ALU.add).then_inc(S["added"], 1)

                def step(s, dyn):
                    nxt, now, last = (locate(s, dyn, d) for d in (2, 0, -2))
                    if last is not None:
                        tiles = tiles_of(last)
                    for j in range(3):
                        if now is not None:
                            post["score"][j](dve, v, now, rows, psA, sc, S, fetched)
                        if last is not None and j < 2:
                            add(last, tiles, j)
                    if nxt is not None:
                        onehots(nxt)
                    if now is not None:
                        post["payload"][0](dve, v, now, rows, sc, S)
                    if nxt is not None and post.get("onehots"):
                        post["onehots"](v, nxt, rows, S)
                    if now is not None and len(post["payload"]) > 1:
                        post["payload"][1](dve, v, now, rows, sc, S)
                pipeline(dve, 2, 2, step)

            @block.scalar
            def _(act):
                def indices(at):
                    g, q, r = at
                    if not isinstance(g, int) or g >= DEPTH:
                        act.wait_ge(fetched[r], q * (16 * TPG))
                        hold(act, "act")
                    nc.scalar.activation(gidx[:, r, :], rec[:, bass.ds(g * TPG, TPG), 1], ACT.Copy)\
                        .then_inc(S["gidx_ready"], 1)

                act.wait_ge(S["rec_loaded"], 16)

                def step(s, dyn):
                    soon, nxt, now = (locate(s, dyn, d) for d in (3, 1, 0))
                    if now is not None:
                        post["exp"](act, now, rows, sc, S)
                    if nxt is not None:
                        g, q, r = nxt
                        act.wait_ge(S["turned"], g + 1)
                        back(act, S["own_e"], g, 2)
                        nc.scalar.activation(ohT[:, r % 2, :, :].rearrange("p t n -> p (t n)"), psT[:, r % 2, :],
                                             ACT.Copy).then_inc(S["ohT_ready"], 1)
                    if soon is not None:
                        indices(soon)
                    if now is not None and post.get("scale"):
                        post["scale"](act, now, oh, S)
                pipeline(act, 3, 0, step)

            @block.tensor
            def _(pe):
                def step(s, dyn):
                    nxt, now, last = (locate(s, dyn, d) for d in (1, 0, -1))
                    if now is not None:
                        g, q, r = now
                        pe.wait_ge(S["ohT_ready"], g + 1)
                        pe.wait_ge(ownland[r], q * 32 + 32)
                        back(pe, S["own_used"], g, 2)
                        for t in range(TPG):
                            ins = pe.matmul(psA[:, r % 2, t * heads:(t + 1) * heads], ohT[:, r % 2, t, :],
                                            ownv[:, r, t // TPU, own_n - heads:], start=True, stop=True)
                        ins.then_inc(S["own_e"], 1)
                    if nxt is not None:
                        g, q, r = nxt
                        pe.wait_ge(S["oh_ready"], g + 1)
                        back(pe, S["ohT_ready"], g, 2)
                        for t in range(TPG):
                            ins = pe.transpose(psT[:, r % 2, t * P:(t + 1) * P], oh[:, r, t, :], ident[:, :])
                        ins.then_inc(S["turned"], 1)
                    if last is not None:
                        g, q, r = last
                        pe.wait_ge(S["payload"], g + 1)
                        back(pe, S["added"], g, 2, per=2)
                        for t in range(TPG):
                            ins = pe.matmul(psO[:, 2 * (r % 2) + t // TPU, 0:accw], oh[:, r, t, :],
                                            rows[:, r, t, 0:accw], start=(t % TPU == 0), stop=(t % TPU == TPU - 1))
                        ins.then_inc(S["summed"], 1)
                pipeline(pe, 1, 1, step)

        end_phase()

    with ExitStack() as c2:
        acc0 = sb("acc0", [P, NT, A0], c=c2)
        with ExitStack() as c:
            rec = sb("rec0", [P, ST, 4], I32, c=c)
            edge_term = sb("edge_term", [P, ST, H], c=c)
            awe = sb("awe", [P, H, 2 * O + 1], c=c)
            abb = sb("abb", [P, H], c=c)
            s_score = sem("l0_score_steps")

            def l0_sync(sp, S):
                sp.dma_start(awe[:, :, :].rearrange("p h o -> p (h o)"),
                             a["L0_gnn_aw"].rearrange("h o -> (h o)").partition_broadcast(P)).then_inc(S["table_done"], 16)
                sp.dma_start(abb[:, :], a["L0_gnn_ab"].partition_broadcast(P)).then_inc(S["table_done"], 16)

            def l0_bulk(dve, S, chain):
                v = nc.vector
                link = Chain(dve, chain).link
                dve.wait_ge(S["table_done"], 32)
                full = [P, ST, H]
                el = rec[:, :, 2:3].bitcast(F32).to_broadcast(full)
                link(v.tensor_tensor(edge_term[:, :, :], el,
                                     awe[:, :, 2 * O:2 * O + 1].rearrange("p h o -> p o h").to_broadcast(full),
                                     ALU.mult))
                link(v.tensor_tensor(edge_term[:, :, :], edge_term[:, :, :],
                                     abb[:, :].unsqueeze(1).to_broadcast(full), ALU.add))

            def l0_pair(dve, v, at, rows, psA, sc, S, fetched):
                g, q, r = at
                dve.wait_ge(S["own_e"], g + 1)
                dve.wait_ge(fetched[r], q * (16 * TPG) + 16 * TPG)
                v.tensor_tensor(sc[:, r % 2, :, :], psA[:, r % 2, 0:TPG * H].rearrange("p (t h) -> p t h", t=TPG),
                                rows[:, r, :, D:D + H], ALU.add).then_inc(S["own_used"], 1)

            def l0_edge(dve, v, at, rows, psA, sc, S, fetched):
                g, q, r = at
                s = sc[:, r % 2, :, :]
                dve.wait_ge(S["own_used"], g + 1)
                v.tensor_tensor(s, s, edge_term[:, bass.ds(g * TPG, TPG), :], ALU.add).then_inc(s_score, 1)

            def l0_clamp(dve, v, at, rows, psA, sc, S, fetched):
                g, q, r = at
                s = sc[:, r % 2, :, :]
                dve.wait_ge(s_score, g + 1)
                v.tensor_scalar(s, s, -1.0 / 20.0, 0.0, ALU.mult, ALU.min).then_inc(S["score"], 1)

            def l0_exp(act, at, rows, sc, S):
                g, q, r = at
                act.wait_ge(S["score"], g + 1)
                nc.scalar.activation(rows[:, r, :, D:D + H], sc[:, r % 2, :, :], ACT.Exp).then_inc(S["weight"], 1)

            def l0_payload(dve, v, at, rows, sc, S):
                g, q, r = at
                dve.wait_ge(S["weight"], g + 1)
                f = rows[:, r, :, 0:D].rearrange("p t (h o) -> p t h o", h=H)
                v.tensor_tensor(f, f, rows[:, r, :, D:D + H].unsqueeze(3).to_broadcast([P, TPG, H, O]), ALU.mult)\
                    .then_inc(S["payload"], 1)

            edge_phase(0, c, table0, W0, A0, acc0, rec, D + H, H, H,
                       dict(sync=l0_sync, bulk=l0_bulk, score=(l0_pair, l0_edge, l0_clamp), exp=l0_exp,
                            payload=(l0_payload,)))

        with ExitStack() as c:
            dn = Dense("ln1", c, NE)
            XN = sb("XN", [P, NT, D], c=c)
            gw = sb("gw", [P, KD, NE], c=c)
            gb = sb("gb", [P, NE], c=c)
            prob = sb("prob", [P, NT, NE], c=c)
            pick = sb("pick", [P, NT, NE], c=c)
            col = sb("col", [P, 8, NT], c=c)
            keys = sb("keys", [P, 2, NT], c=c)
            wheref = sb("where2", [P, 2 * NT], c=c)
            texp = sb("tile_expert", [P, MT], I32, c=c)
            srt = Sort("sort2", c, P, 2 * NT, NE, P, MT)
            srt.unumber = sb("unumber2", [P, MT], c=c)
            zero = sb("zero", [P, 8, D], c=c)
            chain = sem("chain3")
            gloaded, zfilled, zset, xncopied = sem("gloaded"), sem("zfilled"), sem("zset"), sem("xncopied")
            xn_copy_free, logits = sem("xn_copy_free"), sem("logits")
            shifted, exped, tok_ready, dispatched = sem("shifted"), sem("exped"), sem("tok_ready"), sem("dispatched")
            records1 = scatter_sems("rec1a")

            with nc.Block() as block:
                @block.sync
                def _(sp):
                    sp.dma_start(gw[:, :, :], a["L0_ffn_gate_w"].rearrange("(j p) e -> p j e", p=P)).then_inc(gloaded, 16)
                    sp.dma_start(gb[:, :], a["L0_ffn_gate_b"].partition_broadcast(P)).then_inc(gloaded, 16)
                    sp.wait_ge(zset, 1)
                    rest = expert_in.rearrange("(p s) d -> p s d", p=P)
                    for s0 in range(0, MT, 8):
                        n = min(8, MT - s0)
                        sp.dma_start(rest[:, s0:s0 + n, :], zero[:, 0:n, :]).then_inc(zfilled, 16)

                @block.gpsimd
                def _(pool):
                    nc.gpsimd.memset(zero[:, :, :], 0.0).then_inc(zset, 1)
                    nc.gpsimd.iota(srt.unumber[:, :], [[1, MT]], base=0, channel_multiplier=0,
                                   allow_small_or_imprecise_dtypes=True).then_inc(zset, 1)
                    scatter_records(pool, 1, records1, 0, 1)
                    pool.wait_ge(zfilled, 16 * -(-MT // 8))
                    pool.wait_ge(tok_ready, 1)
                    for j in range(2):
                        for t in range(NT):
                            n = LAST if t == NT - 1 else P
                            at = j * NT + t
                            pool.indirect_dma_start(
                                out=expert_in,
                                out_offset=bass.IndirectOffsetOnAxis(ap=tokslot[0:n, at:at + 1], axis=0),
                                in_=XN[0:n, t, :], in_offset=None).then_inc(dispatched, 16)
                    pool.wait_ge(dispatched, 16 * 2 * NT)

                @block.vector
                def _(dve):
                    v = nc.vector
                    ch = Chain(dve, chain)
                    link = ch.link
                    dve.sem_inc(dn.product_free, 1)
                    w = acc0[:, :, D:D + H]
                    link(v.tensor_tensor(w, w, padrow[:, :].unsqueeze(2).to_broadcast([P, NT, H]), ALU.add))
                    link(v.reciprocal(w, w))
                    for h in range(H):
                        f = acc0[:, :, h * O:(h + 1) * O]
                        link(v.tensor_tensor(f, f, acc0[:, :, D + h:D + h + 1].to_broadcast([P, NT, O]), ALU.mult))
                    link(v.tensor_tensor(X[:, :, :], X[:, :, :], acc0[:, :, 0:D], ALU.add))
                    dve.wait_ge(gloaded, 32)
                    with dve.Fori(0, NCH) as i:
                        ch.enter(i, dn.LINKS)
                        dve.wait_ge(xn_copy_free, i + 1)
                        dn.vector(dve, ch, i)
                        for k in range(CH):
                            dve.wait_ge(dn.product, i * CH + k + 1)
                            v.tensor_tensor(prob[:, bass.ds(i * CH + k, 1), :].rearrange("p a e -> p (a e)"),
                                            dn.psF[:, k % 2, 0:NE], gb[:, :], ALU.add).then_inc(logits, 1)
                            dve.wait_ge(logits, i * CH + k + 1)
                            dve.sem_inc(dn.product_free, 1)
                    ch.leave(NCH)
                    full = [P, NT, NE]

                    def over(x):
                        return x.unsqueeze(2).to_broadcast(full)

                    number = iota[:, 0:NE].unsqueeze(1).to_broadcast(full)
                    link(v.tensor_reduce(col[:, 0, :], prob[:, :, :], AX.X, ALU.max))
                    v.tensor_tensor(prob[:, :, :], prob[:, :, :], over(col[:, 0, :]), ALU.subtract).then_inc(shifted, 1)
                    dve.wait_ge(exped, 1)
                    link(v.tensor_reduce(col[:, 1, :], prob[:, :, :], AX.X, ALU.add))
                    link(v.reciprocal(col[:, 2, :], col[:, 1, :]))
                    link(v.tensor_tensor(prob[:, :, :], prob[:, :, :], over(col[:, 2, :]), ALU.mult))
                    for j in range(2):
                        link(v.tensor_reduce(col[:, 3 + j, :], prob[:, :, :], AX.X, ALU.max))
                        link(v.tensor_tensor(pick[:, :, :], prob[:, :, :], over(col[:, 3 + j, :]), ALU.is_equal))
                        link(v.tensor_tensor(pick[:, :, :], pick[:, :, :],
                                             srt.small[:, 7, 0:NE].unsqueeze(1).to_broadcast(full), ALU.mult)
                             if j else v.tensor_scalar(srt.small[:, 7, 0:NE], iota[:, 0:NE], -1.0, float(NE),
                                                       ALU.mult, ALU.add))
                        if j == 0:
                            link(v.tensor_tensor(pick[:, :, :], pick[:, :, :],
                                                 srt.small[:, 7, 0:NE].unsqueeze(1).to_broadcast(full), ALU.mult))
                        link(v.tensor_reduce(keys[:, j, :], pick[:, :, :], AX.X, ALU.max))
                        link(v.tensor_scalar(keys[:, j, :], keys[:, j, :], -1.0, float(NE), ALU.mult, ALU.add))
                        if j == 0:
                            link(v.tensor_tensor(pick[:, :, :], number, over(keys[:, 0, :]), ALU.is_equal))
                            link(v.scalar_tensor_tensor(prob[:, :, :], pick[:, :, :], -2.0, prob[:, :, :],
                                                        ALU.mult, ALU.add))
                    link(v.tensor_tensor(col[:, 5, :], col[:, 3, :], col[:, 4, :], ALU.add))
                    link(v.reciprocal(col[:, 6, :], col[:, 5, :]))
                    for j in range(2):
                        link(v.tensor_tensor(wts[:, j, :], col[:, 3 + j, :], col[:, 6, :], ALU.mult))
                        link(v.scalar_tensor_tensor(keys[:, j, :], padrow[:, :], float(2 * NE), keys[:, j, :],
                                                    ALU.mult, ALU.add))
                    dve.wait_ge(zset, 2)
                    srt.vector(dve, link, keys[:, :, :].rearrange("p j t -> p (j t)"), texp[:, :], wheref[:, :])
                    v.tensor_copy(tokslot[:, :], wheref[:, :]).then_inc(tok_ready, 1)

                @block.scalar
                def _(act):
                    act.sem_inc(xn_copy_free, 1)

                    def keep(i):
                        act.wait_ge(dn.normed, i + 1)
                        hold(act, "act")
                        nc.scalar.activation(XN[:, bass.ds(i * CH, CH), :], dn.xn[:, :, :], ACT.Copy).then_inc(xncopied, 1)
                        act.wait_ge(xncopied, i + 1)
                        act.sem_inc(xn_copy_free, 1)
                    dn.run_act(act, extra=keep)
                    act.wait_ge(shifted, 1)
                    nc.scalar.activation(prob[:, :, :], prob[:, :, :], ACT.Exp).then_inc(exped, 1)

                @block.tensor
                def _(pe):
                    pe.wait_ge(gloaded, 32)
                    dn.run_pe(pe, gw)
                    srt.tensor(pe)

            end_phase()

            with ExitStack() as cc:
                xs = sb("xs", [P, DEPTH, D], c=cc)
                xsT = sb("xsT", [P, 2, KD, P], c=cc)
                w1s = sb("w1s", [P, DEPTH, KD, FH], c=cc)
                w2s = sb("w2s", [P, DEPTH, KD, FH], c=cc)
                w3s = sb("w3s", [P, DEPTH, FH // P, D], c=cc)
                gate = sb("gate", [P, 2, FH], c=cc)
                hid = sb("hid", [P, 2, FH], c=cc)
                ys = sb("ys", [P, DEPTH, D], c=cc)
                names = ("turned", "xsT_ready", "h1", "h2", "gated", "hidden", "y", "y_copied")
                S = {n: sem("m_" + n) for n in names}
                xland = [sem(f"m_xland{r}") for r in range(DEPTH)]
                wland = [sem(f"m_wland{r}") for r in range(DEPTH)]
                ystored = [sem(f"m_ystored{r}") for r in range(DEPTH)]
                records1 = scatter_sems("rec1b")

                psX, psH1 = dn.psT, dn.psF
                psH2, psY = ps("psH2", [P, 2, 512], cc), (srt.psum, ps("psY2", [P, 512], cc))

                pipeline, locate, back = ring(MT)

                with nc.Block() as block:
                    @block.sync
                    def _(sp):
                        def step(s, dyn):
                            t, q, r = locate(s, dyn, 0)
                            back(sp, S["turned"], t, DEPTH)
                            sp.dma_start(xs[:, r, :], expert_in[bass.ds(t * P, P), :]).then_inc(xland[r], 16)
                            back(sp, S["y"], t, DEPTH)
                            hold(sp, "sp")
                            e = sp.value_load(texp[0:1, bass.ds(t, 1)], min_val=0, max_val=NE - 1)
                            for w, d in ((w1s, a["L0_ffn_w1"]), (w2s, a["L0_ffn_w2"]), (w3s, a["L0_ffn_w3"])):
                                sp.dma_start(w[:, r, :, :], d[bass.ds(e, 1), :, :]
                                             .rearrange("e (j p) n -> p (e j) n", p=P)).then_inc(wland[r], 16)
                        pipeline(sp, 0, 0, step)

                    @block.gpsimd
                    def _(pool):
                        scatter_records(pool, 1, records1, 1, 5)
                        for r in range(DEPTH):
                            pool.wait_ge(ystored[r], 16 * (MT // DEPTH))

                    @block.vector
                    def _(dve):
                        v = nc.vector

                        def step(s, dyn):
                            now, last = locate(s, dyn, 0), locate(s, dyn, -1)
                            if now is not None:
                                t, q, r = now
                                dve.wait_ge(S["gated"], t + 1)
                                dve.wait_ge(S["h2"], t + 1)
                                back(dve, S["y"], t, 2)
                                v.tensor_tensor(hid[:, r % 2, :], gate[:, r % 2, :], psH2[:, r % 2, :], ALU.mult)\
                                    .then_inc(S["hidden"], 1)
                            if last is not None:
                                t, q, r = last
                                dve.wait_ge(S["y"], t + 1)
                                if not isinstance(t, int) or t >= DEPTH:
                                    dve.wait_ge(ystored[r], q * 16)
                                v.tensor_copy(ys[:, r, :], psY[r % 2][:, 0:D]).then_inc(S["y_copied"], 1)
                        pipeline(dve, 0, 1, step)

                    @block.scalar
                    def _(act):
                        def step(s, dyn):
                            nxt, now, last = (locate(s, dyn, d) for d in (1, 0, -1))
                            if nxt is not None:
                                t, q, r = nxt
                                act.wait_ge(S["turned"], t + 1)
                                back(act, S["h2"], t, 2)
                                nc.scalar.activation(xsT[:, r % 2, :, :], psX[:, r % 2, 0:D].rearrange("p (a b) -> p a b", a=KD),
                                                     ACT.Copy).then_inc(S["xsT_ready"], 1)
                            if now is not None:
                                t, q, r = now
                                act.wait_ge(S["h1"], t + 1)
                                back(act, S["hidden"], t, 2)
                                nc.scalar.activation(gate[:, r % 2, :], psH1[:, r % 2, :], ACT.Silu).then_inc(S["gated"], 1)
                            if last is not None:
                                t, q, r = last
                                act.wait_ge(S["y_copied"], t + 1)
                                act.dma_start(expert_out[bass.ds(t * P, P), :], ys[:, r, :]).then_inc(ystored[r], 16)
                        pipeline(act, 1, 1, step)

                    @block.tensor
                    def _(pe):
                        def step(s, dyn):
                            nxt, now, last = (locate(s, dyn, d) for d in (1, 0, -1))
                            if nxt is not None:
                                t, q, r = nxt
                                pe.wait_ge(xland[r], q * 16 + 16)
                                back(pe, S["xsT_ready"], t, 2)
                                for j in range(KD):
                                    ins = pe.transpose(psX[:, r % 2, j * P:(j + 1) * P], xs[:, r, j * P:(j + 1) * P],
                                                       ident[:, :])
                                ins.then_inc(S["turned"], 1)
                            if now is not None:
                                t, q, r = now
                                pe.wait_ge(S["xsT_ready"], t + 1)
                                pe.wait_ge(wland[r], q * 48 + 48)
                                for w, p_, name, freed in ((w1s, psH1, "h1", "gated"), (w2s, psH2, "h2", "hidden")):
                                    back(pe, S[freed], t, 2)
                                    for m in range(FH // P):
                                        for j in range(KD):
                                            ins = pe.matmul(p_[:, r % 2, m * P:(m + 1) * P], w[:, r, j, m * P:(m + 1) * P],
                                                            xsT[:, r % 2, j, :], start=(j == 0), stop=(j == KD - 1))
                                    ins.then_inc(S[name], 1)
                            if last is not None:
                                t, q, r = last
                                pe.wait_ge(S["hidden"], t + 1)
                                back(pe, S["y_copied"], t, 2)
                                for m in range(FH // P):
                                    ins = pe.matmul(psY[r % 2][:, 0:D], hid[:, r % 2, m * P:(m + 1) * P],
                                                    w3s[:, r, m, :], start=(m == 0), stop=(m == FH // P - 1))
                                ins.then_inc(S["y"], 1)
                        pipeline(pe, 1, 1, step)

                end_phase()

    with ExitStack() as c4:
        acc1 = sb("acc1", [P, NT, A1], c=c4)
        relW = sb("relW", [P, 2, D], c=c4)
        with ExitStack() as c:
            rec = sb("rec1", [P, ST, 4], I32, c=c)
            with ExitStack() as cc:
                dn = Dense("ln2", cc, W1)
                wn = sb("wn", [P, KD, W1], c=cc)
                frow = sb("frow1", [P, 2, W1], c=cc)
                psR = ps("psR", [P, 512], cc)
                token_rows = sb("token_rows", [P, 2, NT, D], c=cc)
                token_land, token_have, mixed = [sem("tok_l0"), sem("tok_l1")], sem("tok_have"), sem("tok_mixed")
                wloaded, wready, chain = sem("w4_loaded"), sem("w4_ready"), sem("chain4")
                rel_p = sem("rel_product")
                fready, fstored = sem("f4_ready"), [sem("f4st0"), sem("f4st1")]

                with nc.Block() as block:
                    @block.sync
                    def _(sp):
                        sp.dma_start(wn[:, :, 0:D], a["L1_gnn_weight_neighbor"].rearrange("(j p) n -> p j n", p=P))\
                            .then_inc(wloaded, 16)
                        with sp.Fori(0, NCH) as i:
                            for k in range(CH):
                                sp.wait_ge(fready, i * CH + k + 1)
                                sp.dma_start(table1[bass.ds((i * CH + k) * P, P), :], frow[:, k % 2, :])\
                                    .then_inc(fstored[k % 2], 16)
                        sp.wait_ge(fstored[0], 16 * 3 * NCH)
                        sp.wait_ge(fstored[1], 16 * 2 * NCH)

                    @block.gpsimd
                    def _(pool):
                        for i in range(NCH + 1):
                            for j in range(2 if i < NCH else 0):
                                for t in range(i * CH, (i + 1) * CH):
                                    at = j * NT + t
                                    pool.indirect_dma_start(
                                        out=token_rows[:, j, t, :], out_offset=None, in_=expert_out,
                                        in_offset=bass.IndirectOffsetOnAxis(ap=tokslot[:, at:at + 1], axis=0))\
                                        .then_inc(token_land[i % 2], 16)
                            if i:
                                pool.wait_ge(token_land[(i - 1) % 2], 32 * CH * ((i + 1) // 2))
                                pool.sem_inc(token_have, 1)

                    @block.vector
                    def _(dve):
                        v = nc.vector
                        ch = Chain(dve, chain)
                        link = ch.link
                        dve.sem_inc(dn.product_free, 1)
                        dve.wait_ge(wloaded, 16)
                        for j in range(KD):
                            for e in range(2):
                                link(v.tensor_copy(wn[:, j, D + e:D + e + 1], wcol[:, e * KD + j:e * KD + j + 1]))
                        dve.sem_inc(wready, 1)
                        dve.wait_ge(rel_p, 1)
                        link(v.tensor_copy(relW[:, 0, :], psR[:, 0:D]))
                        link(v.tensor_copy(relW[0:R - P, 1, :], psR[0:R - P, D:2 * D]))

                        def mix(i):
                            dve.wait_ge(token_have, i + 1)
                            xc = X[:, bass.ds(i * CH, CH), :]
                            for j in range(2):
                                wt = wts[:, j, bass.ds(i * CH, CH)].unsqueeze(2).to_broadcast([P, CH, D])
                                row = token_rows[:, j, bass.ds(i * CH, CH), :]
                                v.tensor_tensor(row, row, wt, ALU.mult).then_inc(mixed, 1)
                            for j in range(2):
                                dve.wait_ge(mixed, i * 4 + (2 + j))
                                v.tensor_tensor(xc, xc, token_rows[:, j, bass.ds(i * CH, CH), :], ALU.add)\
                                    .then_inc(mixed, 1)
                            dve.wait_ge(mixed, i * 4 + 4)

                        def projections(i):
                            mix(i)
                            dn.vector(dve, ch, i)
                            for k in range(CH):
                                dve.wait_ge(dn.product, i * CH + k + 1)
                                if not (isinstance(i, int) and k < 2):
                                    dve.wait_ge(fstored[k % 2], (i * (3 - k % 2) + k // 2) * 16)
                                v.tensor_copy(frow[:, k % 2, :], dn.psF[:, k % 2, 0:W1]).then_inc(fready, 1)
                                dve.wait_ge(fready, i * CH + k + 1)
                                dve.sem_inc(dn.product_free, 1)
                        projections(0)
                        with dve.Fori(1, NCH) as i:
                            ch.enter(i, dn.LINKS, 1)
                            projections(i)
                        ch.leave(NCH)

                    @block.scalar
                    def _(act):
                        dn.run_act(act)

                    @block.tensor
                    def _(pe):
                        pe.wait_ge(wloaded, 16)
                        for b, n in ((0, P), (1, R - P)):
                            for j in range(KD):
                                ins = pe.matmul(psR[0:n, b * D:(b + 1) * D], relT[:, j, b * P:b * P + n],
                                                wn[:, j, 0:D], start=(j == 0), stop=(j == KD - 1))
                        ins.then_inc(rel_p, 1)
                        pe.wait_ge(wready, 1)
                        dn.run_pe(pe, wn)

                end_phase()

            inverse = sb("inverse", [P, 2, TPG], c=c)
            steps, tail = sem("l1_steps"), sem("l1_tail")

            def l1_onehots(v, at, rows, S):
                g, q, r = at
                v.tensor_tensor(rows[:, r, :, W1:A1], rec[:, bass.ds(g * TPG, TPG), 2:3].to_broadcast([P, TPG, R]),
                                iota[:, :].unsqueeze(1).to_broadcast([P, TPG, R]), ALU.is_equal)\
                    .then_inc(S["counted"], 1)

            def l1_edge(dve, v, at, rows, psA, sc, S, fetched):
                g, q, r = at
                dve.wait_ge(fetched[r], q * (16 * TPG) + 16 * TPG)
                v.tensor_tensor(sc[:, r % 2, :, :], rows[:, r, :, D:D + 1],
                                rec[:, bass.ds(g * TPG, TPG), 3:4].bitcast(F32), ALU.add).then_inc(steps, 1)

            def l1_pair(dve, v, at, rows, psA, sc, S, fetched):
                g, q, r = at
                s = sc[:, r % 2, :, :]
                dve.wait_ge(S["own_e"], g + 1)
                dve.wait_ge(steps, g + 1)
                v.tensor_tensor(s, s, psA[:, r % 2, 0:TPG].unsqueeze(2), ALU.add).then_inc(S["own_used"], 1)

            def l1_leak(dve, v, at, rows, psA, sc, S, fetched):
                g, q, r = at
                s = sc[:, r % 2, :, :]
                dve.wait_ge(S["own_used"], g + 1)
                v.scalar_tensor_tensor(s, s, 0.01, s, ALU.mult, ALU.max).then_inc(S["score"], 1)

            def l1_exp(act, at, rows, sc, S):
                g, q, r = at
                act.wait_ge(S["score"], g + 1)
                nc.scalar.activation(sc[:, r % 2, :, :], sc[:, r % 2, :, :], ACT.Exp).then_inc(S["weight"], 1)

            def l1_scale(act, at, oh, S):
                g, q, r = at
                act.wait_ge(tail, g * 2 + 2)
                act.wait_ge(S["turned"], g + 1)
                act.wait_ge(S["counted"], g + 1)
                for t in range(TPG):
                    ins = nc.scalar.activation(oh[:, r, t, :], oh[:, r, t, :], ACT.Copy,
                                               scale=inverse[:, r % 2, t:t + 1])
                ins.then_inc(S["payload"], 1)

            def l1_inverse(dve, v, at, rows, sc, S):
                g, q, r = at
                dve.wait_ge(S["weight"], g + 1)
                if not isinstance(g, int) or g >= 2:
                    dve.wait_ge(S["payload"], g - 1)
                v.reciprocal(inverse[:, r % 2, :], sc[:, r % 2, :, 0]).then_inc(tail, 1)

            def l1_share(dve, v, at, rows, sc, S):
                g, q, r = at
                dve.wait_ge(tail, g * 2 + 1)
                v.tensor_tensor(inverse[:, r % 2, :], sc[:, r % 2, :, 0], inverse[:, r % 2, :], ALU.mult)\
                    .then_inc(tail, 1)

            edge_phase(1, c, table1, W1, A1, acc1, rec, D, 2, 1,
                       dict(onehots=l1_onehots, score=(l1_edge, l1_pair, l1_leak), exp=l1_exp,
                            scale=l1_scale, payload=(l1_inverse, l1_share)))

        with ExitStack() as c:
            dn = Dense("ln3", c, 2 * D)
            wl = sb("wl", [P, KD, 2 * D], c=c)
            cnt = sb("cnt", [P, 2, R], c=c)
            cntT = sb("cntT", [P, 2, 2, P], c=c)
            deg = sb("deg", [P, 2, 2], c=c)
            upd = sb("upd", [P, 2, D], c=c)
            sel = sb("sel", [P, 2, D], c=c)
            psC = ps("psC", [P, 2, 512], c)
            psG = ps("psG", [P, 2, 512], c)
            wloaded, chain = sem("w5_loaded"), sem("chain5")
            cready, cturned, ccopied, gsum = sem("c_ready"), sem("c_turned"), sem("c_copied"), sem("g_sum")
            tdone = sem("t_done")

            def ago(c_, k, n=0):
                return c_ * CH + (k if k < 1 else k - 1) + 1

            with nc.Block() as block:
                @block.sync
                def _(sp):
                    sp.dma_start(wl[:, :, 0:D], a["L1_gnn_loop_weight"].rearrange("(j p) n -> p j n", p=P))\
                        .then_inc(wloaded, 16)
                    sp.dma_start(wl[:, :, D:2 * D], a["L1_gnn_evolve_loop_weight"].rearrange("(j p) n -> p j n", p=P))\
                        .then_inc(wloaded, 16)

                @block.vector
                def _(dve):
                    v = nc.vector
                    ch = Chain(dve, chain)
                    link = ch.link
                    dve.sem_inc(dn.product_free, 1)
                    dve.sem_inc(tdone, 1)

                    with dve.Fori(0, NCH) as i:
                        ch.enter(i, dn.LINKS + 8 * CH)
                        dn.vector(dve, ch, i)
                        for k in range(CH):
                            t = i * CH + k
                            b = k % 2
                            row = acc1[:, bass.ds(t, 1), :].rearrange("p a w -> p (a w)")
                            link(v.tensor_scalar(cnt[:, b, :], row[:, W1:A1], 1.0, None, ALU.mult))
                            dve.sem_inc(cready, 1)
                            link(v.tensor_reduce(deg[:, b, 0:1], cnt[:, b, :], AX.X, ALU.add))
                            link(v.tensor_scalar(deg[:, b, 0:1], deg[:, b, 0:1], 0.0, None, ALU.is_gt))
                            link(v.tensor_scalar(deg[:, b, 1:2], deg[:, b, 0:1], -1.0, 1.0, ALU.mult, ALU.add))
                            dve.wait_ge(gsum, t + 1)
                            link(v.tensor_tensor(upd[:, b, :], psG[:, b, 0:D], row[:, 0:D], ALU.add))
                            xt = X[:, bass.ds(t, 1), :].rearrange("p a d -> p (a d)")
                            link(v.scalar_tensor_tensor(xt, upd[:, b, :], 0.0, xt, ALU.max, ALU.add))
                            dve.wait_ge(dn.product, t + 1)
                            link(v.scalar_tensor_tensor(xt, dn.psF[:, b, 0:D], deg[:, b, 0:1], xt, ALU.mult, ALU.add))
                            link(v.scalar_tensor_tensor(xt, dn.psF[:, b, D:2 * D], deg[:, b, 1:2], xt, ALU.mult,
                                                        ALU.add))
                            dve.sem_inc(dn.product_free, 1)
                            dve.sem_inc(tdone, 1)
                    ch.leave(NCH)

                @block.scalar
                def _(act):
                    def counts(i, k):
                        t = i * CH + k
                        act.wait_ge(cturned, t + 1)
                        act.wait_ge(tdone, ago(i, k))
                        nc.scalar.activation(cntT[:, k % 2, 0, :], psC[:, k % 2, 0:P], ACT.Copy).then_inc(ccopied, 1)
                        nc.scalar.activation(cntT[0:R - P, k % 2, 1, :], psC[0:R - P, k % 2, P:2 * P],
                                             ACT.Copy).then_inc(ccopied, 1)
                    dn.run_act(act, tail=counts)

                @block.tensor
                def _(pe):
                    def counts(i, k):
                        t = i * CH + k
                        b = k % 2
                        pe.wait_ge(cready, t + 1)
                        pe.transpose(psC[:, b, 0:P], cnt[:, b, 0:P], ident[:, :])
                        pe.transpose(psC[0:R - P, b, P:2 * P], cnt[:, b, P:R], ident[:, :]).then_inc(cturned, 1)
                        pe.wait_ge(ccopied, t * 2 + 2)
                        pe.matmul(psG[:, b, 0:D], cntT[:, b, 0, :], relW[:, 0, :], start=True, stop=False)
                        pe.matmul(psG[:, b, 0:D], cntT[0:R - P, b, 1, :], relW[0:R - P, 1, :], start=False,
                                  stop=True).then_inc(gsum, 1)
                    pe.wait_ge(wloaded, 32)
                    dn.run_pe(pe, wl, extra=counts)

            end_phase()

    with ExitStack() as c:
        dn = Dense("ln4", c, 1)
        Z = sb("Z", [P, NT, D], c=c)
        zT = sb("zT", [P, KD, NT * P], c=c)
        wrc = sb("wrc", [P, KD, 1], c=c)
        brc = sb("brc", [P, 1], c=c)
        w1 = sb("f_w1", [P, KD, FF], c=c)
        w2 = sb("f_w2", [P, FF // P, D], c=c)
        b1 = sb("f_b1", [P, FF // P], c=c)
        b2 = sb("f_b2", [P, D], c=c)
        score = sb("score", [P, NT], c=c)
        srow = sb("srow", [P, NT * P], c=c)
        above = sb("above", [P, NT * P], mybir.dt.bfloat16, c=c)
        tie = sb("tie", [P, 3, P], c=c)
        rank = sb("rank", [P, 4, NT], c=c)
        HALF = CH * P // 2
        hid = sb("f_hid", [P, FF // P, 2 * HALF], c=c)
        psHid = ps("f_psH", [P, 2, 512], c)
        psY = ps("f_psY", [P, 2, 512], c)
        xland, wloaded, chain, scored, rowland = (sem(n) for n in ("w6_xl", "w6_loaded", "chain6", "scored", "rowland"))
        stored_s, zcopied, zfree, zTc = sem("stored_s"), sem("zcopied"), sem("zfree"), sem("zTc")
        hidp, gelu, yp, yd, hfree = sem("hidp"), sem("gelu"), sem("yp"), sem("yd"), sem("hfree")
        final, outd, ranked = sem("final"), sem("outd"), sem("ranked")
        YF = sb("YF", [P, NT, D], c=c)

        with nc.Block() as block:
            @block.sync
            def _(sp):
                with nc.allow_non_contiguous_dma(reason="one small vector, row j * 128 + p to partition p"):
                    sp.dma_start(wrc[:, :, :], a["L1_ffn_wr"].rearrange("(j p) o -> p j o", p=P)).then_inc(wloaded, 16)
                sp.dma_start(brc[:, :], a["L1_ffn_br"].partition_broadcast(P)).then_inc(wloaded, 16)
                sp.dma_start(w1[:, :, :], a["L1_ffn_w1"].rearrange("(j p) n -> p j n", p=P)).then_inc(xland, 16)
                sp.dma_start(w2[:, :, :], a["L1_ffn_w2"].rearrange("(j p) n -> p j n", p=P)).then_inc(xland, 16)
                with nc.allow_non_contiguous_dma(reason="one small vector, hidden unit j * 128 + p to partition p"):
                    sp.dma_start(b1[:, :], a["L1_ffn_b1"].rearrange("(j p) -> p j", p=P)).then_inc(xland, 16)
                sp.dma_start(b2[:, :], a["L1_ffn_b2"].partition_broadcast(P)).then_inc(xland, 16)
                sp.wait_ge(scored, NT)
                with nc.allow_non_contiguous_dma(reason="the scores, turned once"):
                    sp.dma_start(score_d.rearrange("(t p) o -> p (t o)", p=P), score[:, :]).then_inc(stored_s, 16)
                sp.wait_ge(stored_s, 16)
                sp.dma_start(srow[:, :], score_d.rearrange("n o -> (n o)").partition_broadcast(P)).then_inc(rowland, 16)
                with sp.Fori(0, NCH - 1) as i:
                    sp.wait_ge(final, i + 1)
                    sp.dma_start(out[bass.ds(i * (CH * P), CH * P), :].rearrange("(t p) d -> p t d", p=P),
                                 X[:, bass.ds(i * CH, CH), :]).then_inc(outd, 16)
                sp.wait_ge(final, NCH)
                t0 = (NCH - 1) * CH
                sp.dma_start(out[t0 * P:(NT - 1) * P, :].rearrange("(t p) d -> p t d", p=P), X[:, t0:NT - 1, :])\
                    .then_inc(outd, 16)
                sp.dma_start(out[(NT - 1) * P:N, :], X[0:LAST, NT - 1, :]).then_inc(outd, 16)
                sp.wait_ge(outd, 16 * (NCH + 1))

            @block.vector
            def _(dve):
                v = nc.vector
                ch = Chain(dve, chain)
                link = ch.link
                dve.sem_inc(dn.product_free, 1)
                dve.wait_ge(wloaded, 32)
                with dve.Fori(0, NCH) as i:
                    ch.enter(i, dn.LINKS)
                    dve.wait_ge(zfree, i + 1)
                    dn.vector(dve, ch, i)
                    for k in range(CH):
                        dve.wait_ge(dn.product, i * CH + k + 1)
                        v.tensor_tensor(score[:, bass.ds(i * CH + k, 1)], dn.psF[:, k % 2, 0:1], brc[:, :], ALU.add)\
                            .then_inc(scored, 1)
                        dve.wait_ge(scored, i * CH + k + 1)
                        dve.sem_inc(dn.product_free, 1)
                ch.leave(NCH)
                dve.wait_ge(rowland, 16)
                link(v.memset(rank[:, :, :], 0.0))
                for t in range(NT):
                    own = score[:, t:t + 1]
                    if t:
                        link(v.tensor_scalar(above[:, 0:t * P], srow[:, 0:t * P], own, 0.0, ALU.is_ge, ALU.add,
                                             accum_out=rank[:, 0, t:t + 1]))
                    n = min(P, N - t * P)
                    if t < NT - 1:
                        link(v.tensor_scalar(above[:, (t + 1) * P:N], srow[:, (t + 1) * P:N], own, 0.0, ALU.is_gt,
                                             ALU.add, accum_out=rank[:, 1, t:t + 1]))
                    blk = srow[:, t * P:t * P + n]
                    link(v.tensor_scalar(tie[:, 0, 0:n], blk, own, 0.0, ALU.is_gt, ALU.add,
                                         accum_out=rank[:, 2, t:t + 1]))
                    link(v.tensor_scalar(tie[:, 1, 0:n], blk, own, None, ALU.is_equal))
                    link(v.tensor_tensor(tie[:, 2, 0:n], ones[:, 0:n], before[:, 0:n], ALU.subtract))
                    link(v.tensor_tensor(tie[:, 2, 0:n], tie[:, 2, 0:n], ident[:, 0:n], ALU.subtract))
                    link(v.tensor_tensor_reduce(tie[:, 0, 0:n], tie[:, 1, 0:n], tie[:, 2, 0:n], 1.0, 0.0, ALU.mult,
                                                ALU.add, rank[:, 3, t:t + 1]))
                for j in range(1, 4):
                    link(v.tensor_tensor(rank[:, 0, :], rank[:, 0, :], rank[:, j, :], ALU.add))
                link(v.scalar_tensor_tensor(rank[:, 1, :], rank[:, 0, :], float(SELECTED), score[:, :], ALU.is_lt,
                                            ALU.mult))
                dve.wait_ge(xland, 64)
                with dve.Fori(0, NCH) as i:
                    ch.enter(i, 4)
                    dve.wait_ge(yd, i * CH + CH)
                    full = [P, CH, D]
                    y, xc, z = (m[:, bass.ds(i * CH, CH), :] for m in (YF, X, Z))
                    link(v.tensor_tensor(y, y, b2[:, :].unsqueeze(1).to_broadcast(full), ALU.add))
                    link(v.tensor_tensor(y, y, rank[:, 1, bass.ds(i * CH, CH)].unsqueeze(2).to_broadcast(full),
                                         ALU.mult))
                    link(v.tensor_tensor(z, z, y, ALU.add))
                    link(v.tensor_tensor(xc, xc, z, ALU.add))
                    dve.sem_inc(final, 1)
                ch.leave(NCH)

            @block.scalar
            def _(act):
                act.sem_inc(zfree, 1)

                def keep(i):
                    act.wait_ge(dn.normed, i + 1)
                    hold(act, "act")
                    nc.scalar.activation(Z[:, bass.ds(i * CH, CH), :], dn.xn[:, :, :], ACT.Copy).then_inc(zcopied, 1)
                    act.wait_ge(zcopied, i + 1)
                    act.sem_inc(zfree, 1)

                def keepT(i, k):
                    act.wait_ge(dn.copied, i * CH + k + 1)
                    hold(act, "act")
                    nc.scalar.activation(zT[:, :, bass.ds((i * CH + k) * P, P)], dn.xT[:, k, :, :], ACT.Copy)\
                        .then_inc(zTc, 1)
                dn.run_act(act, extra=keep, tail=keepT)
                act.wait_ge(xland, 64)
                with act.Fori(0, NCH) as i:
                    for m in range(FF // P):
                        for h in range(2):
                            act.wait_ge(hidp, i * (2 * FF // P) + 2 * m + h + 1)
                            if m == 0 and h == 0:
                                act.wait_ge(hfree, i + 1)
                            nc.scalar.activation(hid[:, m, h * HALF:(h + 1) * HALF], psHid[:, h, 0:HALF],
                                                 ACT.Gelu_apprx_tanh, bias=b1[:, m:m + 1]).then_inc(gelu, 1)
                    for k in range(CH):
                        act.wait_ge(yp, i * CH + k + 1)
                        hold(act, "act")
                        nc.scalar.activation(YF[:, bass.ds(i * CH + k, 1), :].rearrange("p a d -> p (a d)"),
                                             psY[:, k % 2, 0:D], ACT.Copy).then_inc(yd, 1)

            @block.tensor
            def _(pe):
                pe.wait_ge(wloaded, 32)
                dn.run_pe(pe, wrc)
                pe.wait_ge(zTc, NT)
                pe.wait_ge(xland, 64)
                pe.sem_inc(hfree, 1)
                NH = 2 * FF // P
                with pe.Fori(0, NCH) as i:
                    for m in range(FF // P):
                        for h in range(2):
                            n = 2 * m + h
                            if n < 2:
                                pe.wait_ge(ranked, i + 1)
                            else:
                                pe.wait_ge(gelu, i * NH + n - 1)
                            for j in range(KD):
                                ins = pe.matmul(psHid[:, h, 0:HALF], w1[:, j, m * P:(m + 1) * P],
                                                zT[:, j, bass.ds(i * (2 * HALF) + h * HALF, HALF)],
                                                start=(j == 0), stop=(j == KD - 1))
                            ins.then_inc(hidp, 1)
                    pe.wait_ge(gelu, i * NH + NH)
                    pe.sem_inc(ranked, 1)
                    for k in range(CH):
                        if k >= 2:
                            pe.wait_ge(yd, i * CH + k - 1)
                        for m in range(FF // P):
                            ins = pe.matmul(psY[:, k % 2, 0:D], hid[:, m, k * P:(k + 1) * P],
                                            w2[:, m, :], start=(m == 0), stop=(m == FF // P - 1))
                        ins.then_inc(yp, 1)
                    pe.wait_ge(yd, i * CH + CH)
                    pe.sem_inc(hfree, 1)

            @block.gpsimd
            def _(pool):
                pool.sem_inc(ranked, 1)
    ctx.close()


_INS = ["x", "src", "dst", "edge_type_200", "edge_weight", "L0_gnn_Ws", "L0_gnn_bs", "L0_gnn_aw", "L0_gnn_ab",
        "L0_ffn_gate_w", "L0_ffn_gate_b", "L0_ffn_w1", "L0_ffn_w2", "L0_ffn_w3", "L1_gnn_rel_emb",
        "L1_gnn_weight_neighbor", "L1_gnn_a", "L1_gnn_W3", "L1_gnn_loop_weight", "L1_gnn_evolve_loop_weight",
        "L1_ffn_attention_mask", "L1_ffn_wr", "L1_ffn_br", "L1_ffn_w1", "L1_ffn_b1", "L1_ffn_w2", "L1_ffn_b2"]


def kernel(**inputs):
    import numpy as _np
    import concourse.bacc as _bacc
    from concourse import mybir as _mybir
    from concourse.bass_utils import run_bass_kernel_spmd as _run

    nc = _bacc.Bacc("TRN2", target_bir_lowering=False, num_devices=1)
    arrays, args = {}, {}
    for name in _INS:
        v = _np.ascontiguousarray(inputs[name])
        arrays[f"in_{name}_dram"] = v
        args[name] = nc.dram_tensor(f"in_{name}_dram", v.shape, _mybir.dt.from_np(v.dtype), kind="ExternalInput").ap()
    out = nc.dram_tensor("out_0_dram", (args["x"].shape[0], args["x"].shape[1]), F32, kind="ExternalOutput").ap()
    build(nc, args, out)
    r = _run(nc, [arrays], core_ids=[0])
    return r.results[0]["out_0_dram"]
```

```python
from contextlib import ExitStack

import numpy as np
import concourse.bass as bass
from concourse import mybir

F32 = mybir.dt.float32
I32 = mybir.dt.int32
BF16 = mybir.dt.bfloat16
ALU = mybir.AluOpType
ACT = mybir.ActivationFunctionType
AX = mybir.AxisListType

P = 128
DEPTH = 4
TPG = 4
TPU = 2


class Chain:

    def __init__(self, eng, sem):
        self.eng, self.sem, self.n, self.i, self.per = eng, sem, 0, None, 0

    def value(self):
        return self.n if self.i is None else self.i * self.per + (self.n - self.start * self.per)

    def link(self, ins):
        ins.then_inc(self.sem, 1)
        self.n += 1
        self.eng.wait_ge(self.sem, self.value())

    def enter(self, i, per, start=0):
        self.i, self.per, self.at, self.start = i, per, self.n, start

    def leave(self, end):
        assert self.n - self.at == self.per, (self.n - self.at, self.per)
        self.n, self.i = self.at + self.per * (end - self.start), None


def build(nc, a, out):
    N, D = a["x"].shape
    E = a["src"].shape[0]
    NT = -(-N // P)
    LAST = N - (NT - 1) * P
    EP = next(p for p in range(P, 0, -1) if E % p == 0)
    EC = E // EP
    H, _, O = a["L0_gnn_Ws"].shape
    R = a["L1_gnn_rel_emb"].shape[0]
    NE, _, FH = a["L0_ffn_w1"].shape
    FF = a["L1_ffn_w1"].shape[1]
    KD = D // P
    UNIT = TPU * P
    UNITS = (E + NT * (UNIT - 1)) // UNIT
    GROUPS = -(-UNITS * TPU // TPG)
    GROUPS = -(-GROUPS // DEPTH) * DEPTH
    ST = GROUPS * TPG
    UNITS = ST // TPU
    MT = (2 * N + NE * (P - 1)) // P
    MT += -MT % DEPTH
    W0 = D + 2 * H
    A0 = D + H
    W1 = D + 2
    A1 = W1 + R
    CH = 5
    NCH = NT // CH
    SELECTED = max(1, N // 2) - 1
    assert NT % CH == 0 and D == 2 * P and H * O == D and R > P

    ctx = ExitStack()

    def dram(name, shape, dt):
        return nc.dram_tensor(name, shape, dt).ap()

    rec_d = [dram(f"records{l}", (P * ST, 4), I32) for l in range(2)]
    table0 = dram("table0", (NT * P, W0), F32)
    table1 = dram("table1", (NT * P, W1), F32)
    expert_in = dram("expert_in", (MT * P, D), F32)
    expert_out = dram("expert_out", (MT * P, D), F32)
    score_d = dram("score_d", (NT * P, 1), F32)

    def sb(name, shape, dt=F32, c=ctx):
        return c.enter_context(nc.sbuf_tensor(name, shape, dt))

    def ps(name, shape, c):
        return c.enter_context(nc.psum_tensor(name, shape, F32))

    phase_sems = []

    def sem(name):
        phase_sems.append(nc.alloc_semaphore(name=name))
        return phase_sems[-1]

    def end_phase():
        nc.clear_and_free_semaphores(list(phase_sems))
        phase_sems.clear()
        nc.all_engine_barrier()

    X = sb("X", [P, NT, D])
    wcol = sb("wcol", [P, 3 * KD])
    relrow = sb("relrow", [P, R])
    relation = sb("relation", [EP, EC])
    by_pe = sb("by_pe", [P, 3, ST])
    relT = sb("relT", [P, KD, R])
    rec_s = [sb(f"rec_s{l}", [EP, EC, 4], I32) for l in range(2)]
    slot = [sb(f"slot{l}", [EP, EC], I32) for l in range(2)]
    wts = sb("wts", [P, 2, NT])
    tokslot = sb("tokslot", [P, 2 * NT], I32)
    unit_tile = [sb(f"unit_tile{l}", [P, UNITS], I32) for l in range(2)]
    ident = sb("ident", [P, P])
    iota = sb("iota", [P, R])
    ones = sb("ones", [P, P])
    before = sb("before", [P, P])
    padrow = sb("padrow", [P, NT])
    eps = sb("eps", [P, 1])
    sixes = sb("sixes", [P, NT, 6])
    norm_of = sb("norm_of", [P, 4, NT])
    turn = {e: ctx.enter_context(nc.semaphore(f"turn_{e}")) for e in ("pool", "dve", "act", "sp")}

    def hold(eng, name):
        eng.sem_inc(turn[name], 1)

    def ring(G, depth):
        assert G % depth == 0

        def pipeline(eng, ahead, behind, step):
            for s in range(-ahead, depth):
                step(s, None)
            with eng.Fori(1, G // depth - 1) as q:
                for r in range(depth):
                    step(None, (q, r))
            for s in range(G - depth, G + behind):
                step(s, None)

        def locate(s, dyn, shift):
            if dyn is None:
                g = s + shift
                return None if g < 0 or g >= G else (g, g // depth, g % depth)
            q, r = dyn
            return q * depth + (r + shift), q + (r + shift) // depth, (r + shift) % depth

        def back(eng, s, g, n, per=1, extra=0):
            if not isinstance(g, int) or g - n >= 0:
                eng.wait_ge(s, (g - n + 1) * per + extra)
        return pipeline, locate, back

    by_tiles = ring(NT, CH)

    def bank(eng, s, at):
        t, q, r = at
        by_tiles[2](eng, s, t, next(n for n in range(1, CH + 1) if (r - n) % CH % 2 == r % 2))

    def halves(t0, n):
        for t in range(n):
            at = bass.ds(t0 + t, 1)
            ins = nc.vector.bn_stats(sixes[:, at, :].rearrange("p a s -> p (a s)"),
                                     X[:, at, :].rearrange("p a d -> p (a d)"))
        return ins

    class Dense:

        def __init__(self, tag, c, width):
            self.width = width
            self.pipeline, self.locate, self.back = by_tiles
            self.xn = sb(tag + "_xn", [P, CH, D], c=c)
            self.xT = sb(tag + "_xT", [P, CH, KD, P], c=c)
            self.psT = ps(tag + "_psT", [P, 2, 512], c)
            self.psF = ps(tag + "_psF", [P, 2, 512], c)
            self.spread, self.std, self.normed, self.turned, self.copied, self.product, self.used = (
                sem(tag + "_" + n) for n in ("spread", "std", "normed", "turned", "copied", "product", "used"))

        LINKS = 7

        def moments(self, dve, link, i, t0, n):
            v = nc.vector
            at = bass.ds(t0, n)
            mean, gap, var, inv = (norm_of[:, j, at] for j in range(4))
            even_mean, even_var, odd_mean, odd_var = (sixes[:, at, j] for j in (1, 2, 4, 5))
            link(v.tensor_tensor(mean, even_mean, odd_mean, ALU.add))
            link(v.tensor_scalar(mean, mean, 0.5, None, ALU.mult))
            link(v.tensor_tensor(gap, even_mean, odd_mean, ALU.subtract))
            link(v.tensor_tensor(gap, gap, gap, ALU.mult))
            link(v.tensor_tensor(var, even_var, odd_var, ALU.add))
            v.scalar_tensor_tensor(var, gap, D / 4.0, var, ALU.mult, ALU.add).then_inc(self.spread, 1)
            dve.wait_ge(self.std, i + 1)
            hold(dve, "dve")
            link(v.reciprocal(inv, var))

        def scalar_std(self, act, i, t0, n):
            act.wait_ge(self.spread, i + 1)
            hold(act, "act")
            var = norm_of[:, 2, bass.ds(t0, n)]
            nc.scalar.activation(var, var, ACT.Sqrt, bias=eps[:, :], scale=1.0 / D).then_inc(self.std, 1)

        def normalised(self, dst, t):
            return nc.vector.tensor_scalar(dst, X[:, bass.ds(t, 1), :].rearrange("p a d -> p (a d)"),
                                           norm_of[:, 0, bass.ds(t, 1)], norm_of[:, 3, bass.ds(t, 1)],
                                           ALU.subtract, ALU.mult)

        def norm(self, dve, at):
            t, q, r = at
            self.back(dve, self.turned, t, CH)
            self.normalised(self.xn[:, r, :], t).then_inc(self.normed, 1)

        def transposes(self, pe, at):
            t, q, r = at
            pe.wait_ge(self.normed, t + 1)
            bank(pe, self.copied, at)
            for j in range(KD):
                ins = pe.transpose(self.psT[:, r % 2, j * P:(j + 1) * P], self.xn[:, r, j * P:(j + 1) * P],
                                   ident[:, :])
            ins.then_inc(self.turned, 1)

        def copy(self, act, at):
            t, q, r = at
            act.wait_ge(self.turned, t + 1)
            self.back(act, self.product, t, CH)
            nc.scalar.activation(self.xT[:, r, :, :],
                                 self.psT[:, r % 2, 0:D].rearrange("p (a b) -> p a b", a=KD),
                                 ACT.Copy).then_inc(self.copied, 1)

        def products(self, pe, at, weight):
            t, q, r = at
            pe.wait_ge(self.copied, t + 1)
            bank(pe, self.used, at)
            for j in range(KD):
                ins = pe.matmul(self.psF[:, r % 2, 0:self.width], self.xT[:, r, j, :],
                                weight[:, j, 0:self.width], start=(j == 0), stop=(j == KD - 1))
            ins.then_inc(self.product, 1)

        def run_pe(self, pe, weight):
            def step(s, dyn):
                nxt, now = (self.locate(s, dyn, d) for d in (1, 0))
                if nxt is not None:
                    self.transposes(pe, nxt)
                if now is not None:
                    self.products(pe, now, weight)
            self.pipeline(pe, 1, 0, step)

        def run_act(self, act):
            self.scalar_std(act, 0, 0, NT)
            self.pipeline(act, 0, 0, lambda s, dyn: self.copy(act, self.locate(s, dyn, 0)))

        def run_dve(self, dve, use):
            def step(s, dyn):
                soon, now = (self.locate(s, dyn, d) for d in (2, 0))
                if soon is not None:
                    self.norm(dve, soon)
                if now is not None:
                    dve.wait_ge(self.product, now[0] + 1)
                    use(now)
            self.pipeline(dve, 2, 0, step)

    class Sort:

        def __init__(self, tag, c, rows, cols, buckets, unit, units, oh=None, run=None, psum=None):
            self.rows, self.cols, self.B, self.unit, self.units = rows, cols, buckets, unit, units
            self.oh = oh if oh is not None else sb(tag + "_oh", [rows, buckets, cols], c=c)
            self.run = run if run is not None else sb(tag + "_run", [rows, buckets, cols], c=c)
            self.tot = sb(tag + "_tot", [rows, buckets], c=c)
            self.small = sb(tag + "_small", [P, 8, buckets], c=c)
            self.smalli = sb(tag + "_smalli", [P, 2, buckets], I32, c=c)
            self.ucount = sb(tag + "_ucount", [P, units], c=c)
            self.psum = psum if psum is not None else ps(tag + "_ps", [P, 512], c)
            self.totals, self.sums = sem(tag + "_totals"), sem(tag + "_sums")

        def tensor(self, pe):
            pe.wait_ge(self.totals, 1)
            pe.matmul(self.psum[0:P, 0:self.B], before[0:self.rows, :], self.tot[:, :], start=True, stop=True)
            pe.matmul(self.psum[0:P, self.B:2 * self.B], ones[0:self.rows, :], self.tot[:, :], start=True,
                      stop=True).then_inc(self.sums, 1)

        def vector(self, dve, link, bucket, tile_of_unit, where, parts, placed):
            B, rows, cols, v = self.B, self.rows, self.cols, nc.vector
            oh, run, s, si = self.oh, self.run, self.small, self.smalli
            full = [rows, B, cols]
            flat = "p b c -> p (b c)"
            link(v.tensor_tensor(oh[:, :, :], bucket.unsqueeze(1).to_broadcast(full),
                                 iota[0:rows, 0:B].unsqueeze(2).to_broadcast(full), ALU.is_equal))
            link(v.tensor_tensor_scan(run[:, :, :].rearrange(flat), oh[:, :, :].rearrange(flat),
                                      oh[:, :, :].rearrange(flat), 0.0, ALU.add, ALU.max))
            link(v.memset(s[0:rows, 5, 0:1], 0.0))
            link(v.tensor_copy(s[0:rows, 5, 1:], run[:, 0:B - 1, cols - 1]))
            v.tensor_tensor(self.tot[:, :], run[:, :, cols - 1], s[0:rows, 5, :], ALU.subtract)\
                .then_inc(self.totals, 1)
            dve.wait_ge(self.sums, 1)
            link(v.tensor_scalar(si[:, 0, :], self.psum[:, B:2 * B], float(self.unit - 1), None, ALU.add))
            link(v.tensor_scalar(si[:, 1, :], si[:, 0, :], self.unit.bit_length() - 1, None,
                                 ALU.arith_shift_right))
            link(v.tensor_copy(s[:, 0, :], si[:, 1, :]))
            link(v.tensor_tensor_scan(s[:, 1, :], s[:, 0, :], s[:, 0, :], 0.0, ALU.add, ALU.max))
            link(v.tensor_tensor(s[:, 2, :], s[:, 1, :], s[:, 0, :], ALU.subtract))
            link(v.scalar_tensor_tensor(s[:, 3, :], s[:, 2, :], float(self.unit), self.psum[:, 0:B],
                                        ALU.mult, ALU.add))
            link(v.tensor_tensor(s[0:rows, 4, :], s[0:rows, 3, :], s[0:rows, 5, :], ALU.subtract))
            for lo, hi in parts:
                for b in range(B):
                    ins = v.scalar_tensor_tensor(run[:, b, lo:hi], run[:, b, lo:hi], s[0:rows, 4, b:b + 1],
                                                 oh[:, b, lo:hi], ALU.add, ALU.mult)
                link(ins)
                link(v.tensor_reduce(where[:, lo:hi], run[:, :, lo:hi].rearrange("p b c -> p c b"), AX.X, ALU.max))
                link(v.tensor_scalar(where[:, lo:hi], where[:, lo:hi], -1.0, 0.0, ALU.add, ALU.max))
                placed(lo, hi)
            view = run[:, :, :].rearrange(flat)[:, 0:B * min(self.units, cols)]
            n = min(self.units, cols)
            for u in range(0, self.units, n):
                m = min(n, self.units - u)
                part = view[:, 0:B * m].rearrange("p (u b) -> p u b", b=B)
                link(v.tensor_tensor(part, self.unumber[0:rows, u:u + m].unsqueeze(2).to_broadcast([rows, m, B]),
                                     s[0:rows, 2, :].unsqueeze(1).to_broadcast([rows, m, B]), ALU.is_ge))
                link(v.tensor_reduce(self.ucount[0:rows, u:u + m], part, AX.X, ALU.add))
            link(v.tensor_scalar(tile_of_unit, self.ucount[0:rows, :], -1.0, None, ALU.add))

    BUFS = 5
    COLS = next(n for n in range(20, 0, -1) if EC % (BUFS * n) == 0)
    TURNS = EC // (BUFS * COLS)
    PE_COLS = BUFS * COLS
    PE0 = EC - PE_COLS
    REL_STEP = 3
    XREL_STEP, XREL_STEPS = 5, DEPTH * 8
    XREL0 = EC - XREL_STEP * XREL_STEPS
    assert REL_STEP * PE_COLS <= XREL0 <= 4 * BUFS * COLS and N < 64 * 256
    stage_slot = sb("stage_slot", [EP, BUFS, COLS], I32)
    stage_rec = sb("stage_rec", [EP, BUFS, COLS, 4], I32)

    def scatter_sems(tag):
        return sem(tag + "_staged"), [sem(f"{tag}_landed{b}") for b in range(BUFS)]

    def scatter_records(pool, l, sems, begin, end, rest=None):
        staged, landed = sems

        def turn(i, first):
            for b in range(BUFS):
                if not first:
                    pool.wait_ge(landed[b], (i - begin) * (16 * COLS))
                    hold(pool, "pool")
                at = (i * BUFS + b) * COLS
                nc.gpsimd.tensor_copy(stage_slot[:, b, :], slot[l][:, bass.ds(at, COLS)]).then_inc(staged, 1)
                nc.gpsimd.tensor_copy(stage_rec[:, b, :, :], rec_s[l][:, bass.ds(at, COLS), :]).then_inc(staged, 1)
                pool.wait_ge(staged, (i - begin) * (2 * BUFS) + 2 * b + 2)
                hold(pool, "pool")
                for k in range(COLS):
                    pool.indirect_dma_start(
                        out=rec_d[l], out_offset=bass.IndirectOffsetOnAxis(ap=stage_slot[:, b, k:k + 1], axis=0),
                        in_=stage_rec[:, b, k, :], in_offset=None).then_inc(landed[b], 16)
        turn(begin, True)
        if rest:
            pool.wait_ge(*rest)
        if end - begin > 1:
            with pool.Fori(begin + 1, end) as i:
                turn(i, False)
        for b in range(BUFS):
            pool.wait_ge(landed[b], 16 * COLS * (end - begin))

    with ExitStack() as c:
        big = [sb(f"sort_{n}", [P, NT, EC], c=c) for n in ("oh", "run")]
        unumber = sb("unumber", [P, UNITS], c=c)
        psS = ps("sort_ps", [P, 512], c)
        sort = [Sort(f"sort{l}", c, EP, EC, NT, UNIT, UNITS, *(b[0:EP, :, :] for b in big), psS) for l in range(2)]
        for s in sort:
            s.unumber = unumber
        raw = sb("raw", [EP, 3, EC], I32, c=c)
        elem = sb("elem", [EP, EC], c=c)
        keyi = sb("keyi", [EP, EC], I32, c=c)
        keyf = sb("keyf", [EP, EC], c=c)
        wheref = sb("wheref", [EP, EC], c=c)
        slot_t = sb("slot_t", [EP, 3, EC], I32, c=c)
        ts = slot_t[:, :, :]
        blank = sb("blank", [P, ST, 4], I32, c=c)

        loaded, xloaded, consts, zeroed = sem("edges_loaded"), sem("x_loaded"), sem("consts"), sem("x_zeroed")
        blanked, blank_ready, ready = sem("blanked"), sem("blank_ready"), [sem("slots0_ready"), sem("slots1_ready")]
        chain = sem("chain1")
        records0 = scatter_sems("rec0")

        dn = Dense("ln0", c, W0)
        after = big[0][:, :, :].rearrange("p t e -> p (t e)")
        w3r = after[:, 0:9 * KD * D].rearrange("p (j n) -> p j n", j=3 * KD)
        arow = after[:, 9 * KD * D:9 * KD * D + 3 * D]
        rel = sb("rel", [P, 2, D], c=c)
        relwb = sb("relwb", [P, KD, P], c=c)
        later = big[1][0:EP, :, :].rearrange("p t e -> p (t e)")

        def carve(at, shape, dt=F32):
            size = int(np.prod(shape)) // (2 if dt == BF16 else 1)
            names = " ".join("abcd"[:len(shape)])
            view = later[:, at:at + size]
            view = view.bitcast(dt) if dt != F32 else view
            return view.rearrange(f"p ({names}) -> p {names}", **dict(zip("abcd", shape))), at + size
        relpick, at = carve(0, (5 * REL_STEP, R))
        col_hot, at = carve(at, (5, ST), BF16)
        row_hot, at = carve(at, (5, P), BF16)
        row_part, at = carve(at, (5, 6, P), BF16)
        pieces = sb("pieces", [EP, 6, PE_COLS], c=c)
        part_t = sb("part_t", [EP, PE_COLS], BF16, c=c)
        place_of = sb("place_of", [EP, 2, PE_COLS], c=c)
        column = sb("column", [P, ST], c=c)
        psP = ps("psP", [P, 3, 512], c)
        marked, scaled, put, put_copied = sem("marked"), sem("scaled"), sem("put"), sem("put_copied")
        rel_loaded, rel_t, rel_c = sem("rel_loaded"), sem("rel_turned"), sem("rel_copied")
        rel_p, rel_scored = sem("rel_product1"), sem("rel_scored")
        wcat = sb("wcat", [P, KD, W0], c=c)
        awb = sb("awb", [P, H, 2 * O + 1], c=c)
        biasrow = sb("biasrow", [P, W0], c=c)
        awprod = sb("awprod", [P, H, O], c=c)
        frow = sb("frow", [P, CH, W0], c=c)
        wloaded, wready, fready, fstored = sem("wloaded"), sem("wready"), sem("fready"), [sem(f"fst{r}") for r in range(CH)]

        ppipeline, plocate, pback = ring(PE_COLS, 5)
        assert XREL0 - REL_STEP * PE_COLS <= 5 * REL_STEP

        with nc.Block() as block:
            @block.sync
            def _(sp):
                flat = "(p c) -> p c"
                sp.dma_start(raw[:, 0, :], a["src"].rearrange(flat, p=EP)).then_inc(loaded, 16)
                sp.dma_start(raw[:, 1, :], a["dst"].rearrange(flat, p=EP)).then_inc(loaded, 16)
                sp.dma_start(raw[:, 2, :], a["edge_type_200"].rearrange(flat, p=EP)).then_inc(loaded, 16)
                sp.dma_start(elem[:, :], a["edge_weight"].rearrange(flat, p=EP)).then_inc(loaded, 16)
                sp.dma_start(X[:, 0:NT - 1, :], a["x"][0:(NT - 1) * P, :].rearrange("(t p) d -> p t d", p=P))\
                    .then_inc(xloaded, 16)
                sp.wait_ge(zeroed, 1)
                sp.dma_start(X[0:LAST, NT - 1, :], a["x"][(NT - 1) * P:N, :]).then_inc(xloaded, 16)
                for j in range(KD):
                    sp.dma_start(wcat[:, j, 0:D].rearrange("p (h o) -> p h o", h=H),
                                 a["L0_gnn_Ws"][:, j * P:(j + 1) * P, :].rearrange("h p o -> p h o"))\
                        .then_inc(wloaded, 16)
                sp.dma_start(awb[:, :, :].rearrange("p h o -> p (h o)"),
                             a["L0_gnn_aw"].rearrange("h o -> (h o)").partition_broadcast(P)).then_inc(wloaded, 16)
                sp.dma_start(biasrow[:, 0:D],
                             a["L0_gnn_bs"].rearrange("h o -> (h o)").partition_broadcast(P)).then_inc(wloaded, 16)
                sp.dma_start(rel[:, 0, :], a["L1_gnn_rel_emb"][0:P, :]).then_inc(rel_loaded, 16)
                sp.dma_start(rel[0:R - P, 1, :], a["L1_gnn_rel_emb"][P:R, :]).then_inc(rel_loaded, 16)
                sp.wait_ge(blank_ready, 1)
                for l in range(2):
                    sp.dma_start(rec_d[l].rearrange("(p t) w -> p (t w)", p=P),
                                 blank[:, :, :].rearrange("p t w -> p (t w)")).then_inc(blanked, 16)
                def store(s, dyn):
                    t, q, r = dn.locate(s, dyn, 0)
                    sp.wait_ge(fready, t + 1)
                    sp.dma_start(table0[bass.ds(t * P, P), :], frow[:, r, :]).then_inc(fstored[r], 16)
                dn.pipeline(sp, 0, 0, store)
                sp.wait_ge(ready[1], 1)
                sp.dma_start(arow, a["L1_gnn_a"].rearrange("n o -> (n o)").partition_broadcast(P))\
                    .then_inc(rel_loaded, 16)
                sp.dma_start(w3r[:, :, :], a["L1_gnn_W3"].rearrange("(j p) n -> p j n", p=P)).then_inc(rel_loaded, 16)
                for r in range(CH):
                    sp.wait_ge(fstored[r], 16 * NCH)

            @block.gpsimd
            def _(pool):
                g = nc.gpsimd
                g.memset(ident[:, :], 0.0).then_inc(consts, 1)
                g.memset(before[:, :], 1.0).then_inc(consts, 1)
                g.memset(ones[:, :], 1.0).then_inc(consts, 1)
                g.memset(eps[:, :], 1e-5).then_inc(consts, 1)
                g.memset(padrow[:, :], 0.0).then_inc(consts, 1)
                g.memset(blank[:, :, :], 0).then_inc(consts, 1)
                g.iota(iota[:, :], [[1, R]], base=0, channel_multiplier=0,
                       allow_small_or_imprecise_dtypes=True).then_inc(consts, 1)
                g.iota(column[:, :], [[1, ST]], base=0, channel_multiplier=0,
                       allow_small_or_imprecise_dtypes=True).then_inc(consts, 1)
                g.iota(unumber[:, :], [[1, UNITS]], base=0, channel_multiplier=0,
                       allow_small_or_imprecise_dtypes=True).then_inc(consts, 1)
                pool.wait_ge(consts, 9)
                g.affine_select(out=ident[:, :], in_=ident[:, :], compare_op=ALU.not_equal, fill=1.0, base=0,
                                pattern=[[-1, P]], channel_multiplier=1).then_inc(consts, 1)
                g.affine_select(out=before[:, :], in_=before[:, :], compare_op=ALU.is_gt, fill=0.0, base=0,
                                pattern=[[1, P]], channel_multiplier=-1).then_inc(consts, 1)
                g.affine_select(out=padrow[:, NT - 1:NT], in_=padrow[:, NT - 1:NT], compare_op=ALU.is_gt, fill=1.0,
                                base=LAST, pattern=[[0, 1]], channel_multiplier=-1).then_inc(consts, 1)
                g.memset(blank[:, :, 0:1], P).then_inc(blank_ready, 1)
                pool.wait_ge(blanked, 32)
                pool.wait_ge(ready[0], 1)
                scatter_records(pool, 0, records0, 0, TURNS - 1, (ready[0], 2))

            @block.vector
            def _(dve):
                ch = Chain(dve, chain)
                link = ch.link
                v = nc.vector
                v.memset(X[:, NT - 1, :], 0.0).then_inc(zeroed, 1)
                dve.wait_ge(consts, 12)
                dve.wait_ge(loaded, 64)

                def place(l):
                    key, other = (0, 1) if l == 0 else (1, 0)
                    link(v.tensor_scalar(rec_s[l][:, :, 0], raw[:, key, :], P - 1, None, ALU.bitwise_and))
                    link(v.tensor_copy(rec_s[l][:, :, 1], raw[:, other, :]))
                    if l == 0:
                        link(v.tensor_copy(rec_s[l][:, :, 2:3].bitcast(F32), elem[:, :].unsqueeze(2)))
                    else:
                        link(v.tensor_copy(rec_s[l][:, :, 2], raw[:, 2, :]))
                    if l == 0:
                        link(v.memset(rec_s[l][:, :, 3], 0))
                    link(v.tensor_scalar(keyi[:, :], raw[:, key, :], 7, None, ALU.arith_shift_right))
                    link(v.tensor_copy(keyf[:, :], keyi[:, :]))

                    def slots(lo, hi):
                        link(v.tensor_copy(ts[:, 0, lo:hi], wheref[:, lo:hi]))
                        link(v.tensor_scalar(ts[:, 1, lo:hi], ts[:, 0, lo:hi], P - 1, None, ALU.bitwise_and))
                        link(v.tensor_scalar(ts[:, 2, lo:hi], ts[:, 0, lo:hi], 7, None, ALU.arith_shift_right))
                        link(v.scalar_tensor_tensor(slot[l][:, lo:hi], ts[:, 1, lo:hi], float(ST), ts[:, 2, lo:hi],
                                                    ALU.mult, ALU.add))
                        dve.sem_inc(ready[l], 1)
                        if l == 0 and hi == EC:
                            link(v.tensor_copy(place_of[:, :, :], ts[:, 1:3, PE0:EC]))
                    turn = BUFS * COLS
                    sort[l].vector(dve, link, keyf[:, :], unit_tile[l][0:EP, :], wheref[:, :],
                                   ((0, turn), (turn, EC)) if l == 0 else ((0, EC),), slots)

                place(0)
                dve.wait_ge(wloaded, 16 * (KD + 2))
                for part, off in ((1, 0), (0, H)):
                    aw = awb[:, :, part * O:(part + 1) * O]
                    for j in range(KD):
                        link(v.tensor_tensor(awprod[:, :, :], wcat[:, j, 0:D].rearrange("p (h o) -> p h o", h=H),
                                             aw, ALU.mult))
                        link(v.tensor_reduce(wcat[:, j, D + off:D + off + H], awprod[:, :, :], AX.X, ALU.add))
                    link(v.tensor_tensor(awprod[:, :, :], biasrow[:, 0:D].rearrange("p (h o) -> p h o", h=H),
                                         aw, ALU.mult))
                    link(v.tensor_reduce(biasrow[:, D + off:D + off + H], awprod[:, :, :], AX.X, ALU.add))
                dve.sem_inc(wready, 1)
                dve.wait_ge(xloaded, 32)

                link(halves(0, NT))
                dn.moments(dve, link, 0, 0, NT)

                def features(at):
                    t, q, r = at
                    if not isinstance(t, int) or t >= CH:
                        dve.wait_ge(fstored[r], q * 16)
                    v.tensor_tensor(frow[:, r, :], dn.psF[:, r % 2, 0:W0], biasrow[:, :], ALU.add)\
                        .then_inc(fready, 1)
                    dve.wait_ge(fready, t + 1)
                    dve.sem_inc(dn.used, 1)
                dn.run_dve(dve, features)
                place(1)
                dve.wait_ge(rel_loaded, 64)
                link(v.tensor_tensor(w3r[:, :, :], w3r[:, :, :],
                                     arow.unsqueeze(1).to_broadcast([P, 3 * KD, 3 * D]), ALU.mult))
                link(v.tensor_reduce(wcol[:, :], w3r[:, :, :], AX.X, ALU.add))
                for j in range(KD):
                    link(v.tensor_scalar(relwb[:, j, :], ones[:, :], wcol[:, 2 * KD + j:2 * KD + j + 1], None,
                                         ALU.mult))
                dve.wait_ge(rel_t, 1)
                v.tensor_copy(relT[:, :, :], dn.psT[:, 0, 0:KD * R].rearrange("p (j r) -> p j r", j=KD))\
                    .then_inc(rel_c, 1)
                dve.wait_ge(rel_p, 1)
                link(v.tensor_copy(relrow[:, :], psS[:, 0:R]))
                link(v.tensor_copy(relation[:, :], raw[:, 2, :]))
                last = rec_s[0][:, PE0:EC, :]
                link(v.tensor_scalar(pieces[:, 0, :], last[:, :, 0], float(-P), None, ALU.add))
                link(v.tensor_scalar(keyi[:, 0:PE_COLS], last[:, :, 1], 63, None, ALU.bitwise_and))
                link(v.tensor_copy(pieces[:, 2, :], keyi[:, 0:PE_COLS]))
                link(v.tensor_tensor(pieces[:, 1, :], last[:, :, 1], pieces[:, 2, :], ALU.subtract))
                rest = elem[:, PE0:EC]
                for f in (3, 4):
                    link(v.tensor_copy(part_t[:, :], rest))
                    link(v.tensor_copy(pieces[:, f, :], part_t[:, :]))
                    link(v.tensor_tensor(pieces[:, 5, :], rest, pieces[:, f, :], ALU.subtract))
                    rest = pieces[:, 5, :]

                def relation_score(at, junk):
                    return v.scalar_tensor_tensor(junk, iota[0:EP, :], relation[:, bass.ds(at, 1)],
                                                  relrow[0:EP, :], ALU.is_equal, ALU.mult,
                                                  accum_out=rec_s[1][:, bass.ds(at, 1), 3].bitcast(F32))

                def mark(s, dyn):
                    t, q, r = plocate(s, dyn, 0)
                    pback(dve, put, t, 5)
                    v.tensor_scalar(col_hot[:, r, :], column[0:EP, :], place_of[:, 1, bass.ds(t, 1)], None,
                                    ALU.is_equal).then_inc(marked, 1)
                    v.tensor_scalar(row_hot[:, r, :], iota[0:EP, 0:P], place_of[:, 0, bass.ds(t, 1)], None,
                                    ALU.is_equal).then_inc(marked, 1)
                    pback(dve, rel_scored, t, 5, per=REL_STEP)
                    for j in range(REL_STEP):
                        relation_score(t * REL_STEP + j, relpick[:, REL_STEP * r + j, :]).then_inc(rel_scored, 1)
                ppipeline(dve, 0, 0, mark)
                dve.wait_ge(rel_scored, REL_STEP * PE_COLS)
                for j in range(XREL0 - REL_STEP * PE_COLS):
                    relation_score(REL_STEP * PE_COLS + j, relpick[:, j, :]).then_inc(rel_scored, 1)
                dve.wait_ge(rel_scored, XREL0)

            @block.scalar
            def _(act):
                dn.run_act(act)

                def scale(s, dyn):
                    t, q, r = plocate(s, dyn, 0)
                    act.wait_ge(marked, t * 2 + 2)
                    pback(act, put, t, 5)
                    hold(act, "act")
                    for f in range(6):
                        ins = nc.scalar.activation(row_part[:, r, f, :], row_hot[:, r, :], ACT.Copy,
                                                   scale=pieces[:, f, bass.ds(t, 1)])
                    ins.then_inc(scaled, 1)
                ppipeline(act, 0, 0, scale)
                act.wait_ge(put, PE_COLS)
                nc.scalar.activation(by_pe[:, :, :], psP[:, :, 0:ST], ACT.Copy).then_inc(put_copied, 1)
                act.wait_ge(put_copied, 1)

            @block.tensor
            def _(pe):
                pe.wait_ge(consts, 12)
                sort[0].tensor(pe)
                pe.wait_ge(wready, 1)
                dn.run_pe(pe, wcat)
                sort[1].tensor(pe)
                pe.wait_ge(rel_loaded, 64)
                for j in range(KD):
                    pe.transpose(dn.psT[:, 0, j * R:j * R + P], rel[:, 0, j * P:(j + 1) * P], ident[:, :])
                    ins = pe.transpose(dn.psT[:, 0, j * R + P:(j + 1) * R], rel[0:R - P, 1, j * P:(j + 1) * P],
                                       ident[0:R - P, 0:R - P])
                ins.then_inc(rel_t, 1)
                pe.wait_ge(rel_c, 1)
                for j in range(KD):
                    ins = pe.matmul(psS[:, 0:R], relwb[:, j, :], relT[:, j, :], start=(j == 0),
                                    stop=(j == KD - 1))
                ins.then_inc(rel_p, 1)

                def put_column(s, dyn):
                    t, q, r = plocate(s, dyn, 0)
                    pe.wait_ge(scaled, t + 1)
                    for f, field in enumerate((0, 1, 1, 2, 2, 2)):
                        first, last = f in (0, 1, 3), f in (0, 2, 5)
                        ins = pe.matmul(psP[:, field, 0:ST], row_part[:, r, f, :], col_hot[:, r, :],
                                        start=(first and dyn is None and t == 0),
                                        stop=(last and dyn is None and t == PE_COLS - 1))
                    ins.then_inc(put, 1)
                ppipeline(pe, 0, 0, put_column)

    end_phase()

    def edge_phase(l, c, table, width, accw, acc, rec, own_off, own_n, heads, post):
        tag = f"e{l}_"
        rows = sb(tag + "rows", [P, DEPTH, TPG, accw if l else width], c=c)
        gidx = sb(tag + "gidx", [P, DEPTH, TPG], I32, c=c)
        oh = sb(tag + "oh", [P, DEPTH, TPG, P], c=c)
        ohT = sb(tag + "ohT", [P, 2, TPG, P], c=c)
        ownv = sb(tag + "ownv", [P, DEPTH, 2, own_n], c=c)
        sc = sb(tag + "sc", [P, 2, TPG, heads], c=c)
        psT = ps(tag + "psT", [P, 2, 512], c)
        psA = ps(tag + "psA", [P, 2, 512], c)
        psO = ps(tag + "psO", [P, 4, 512], c)
        names = ("oh_ready", "turned", "ohT_ready", "own_e", "own_used", "score", "weight", "payload",
                 "summed", "added", "gidx_ready", "counted", "rec_loaded", "rec_whole", "table_done", "acc_zero")
        S = {n: sem(tag + n) for n in names}
        fetched = [sem(tag + f"rows_landed{r}") for r in range(DEPTH)]
        ownland = [sem(tag + f"own_landed{r}") for r in range(DEPTH)]
        chain = sem(tag + "chain")
        pipeline, locate, back = ring(GROUPS, DEPTH)

        with nc.Block() as block:
            @block.sync
            def _(sp):
                sp.dma_start(rec[:, :, :].rearrange("p t w -> p (t w)"),
                             rec_d[l].rearrange("(p t) w -> p (t w)", p=P)).then_inc(S["rec_loaded"], 16)
                if post.get("sync"):
                    post["sync"](sp, S)

                def step(s, dyn):
                    at = locate(s, dyn, 0)
                    if at is None:
                        return
                    g, q, r = at
                    back(sp, S["own_e"], g, DEPTH)
                    hold(sp, "sp")
                    for j in range(2):
                        t = sp.value_load(unit_tile[l][0:1, bass.ds(g * 2 + j, 1)], min_val=0, max_val=NT - 1)
                        sp.dma_start(ownv[:, r, j, :], table[bass.ds(t * P, P), own_off:own_off + own_n])\
                            .then_inc(ownland[r], 16)
                pipeline(sp, 0, 0, step)

            @block.gpsimd
            def _(pool):
                nc.gpsimd.memset(acc[:, NT // 2:, :], 0.0).then_inc(S["acc_zero"], 1)

                def step(s, dyn):
                    at = locate(s, dyn, 0)
                    if at is None:
                        return
                    g, q, r = at
                    back(pool, S["summed"], g, DEPTH)
                    pool.wait_ge(S["gidx_ready"], g + 1)
                    hold(pool, "pool")
                    for t in range(TPG):
                        pool.indirect_dma_start(
                            out=rows[:, r, t, 0:width], out_offset=None, in_=table,
                            in_offset=bass.IndirectOffsetOnAxis(ap=gidx[:, r, t:t + 1], axis=0))\
                            .then_inc(fetched[r], 16)
                pipeline(pool, 0, 0, step)

            @block.vector
            def _(dve):
                v = nc.vector
                v.memset(acc[:, 0:NT // 2, :], 0.0).then_inc(S["acc_zero"], 1)
                dve.wait_ge(S["rec_loaded"], 16)
                link = Chain(dve, chain).link
                if post.get("complete"):
                    post["complete"](dve, link)
                dve.sem_inc(S["rec_whole"], 1)
                dve.wait_ge(S["acc_zero"], 2)
                if post.get("bulk"):
                    post["bulk"](dve, S, link)

                def onehots(at):
                    g, q, r = at
                    back(dve, S["summed"], g, DEPTH)
                    v.tensor_tensor(oh[:, r, :, :], rec[:, bass.ds(g * TPG, TPG), 0:1].to_broadcast([P, TPG, P]),
                                    iota[:, 0:P].unsqueeze(1).to_broadcast([P, TPG, P]), ALU.is_equal)\
                        .then_inc(S["oh_ready"], 1)

                def tiles_of(at):
                    g, q, r = at
                    hold(dve, "dve")
                    return [dve.value_load(unit_tile[l][0:1, bass.ds(g * 2 + j, 1)], min_val=0, max_val=NT - 1)
                            for j in range(2)]

                def add(at, tiles, j):
                    g, q, r = at
                    if j == 0:
                        dve.wait_ge(S["summed"], g + 1)
                    if not (isinstance(g, int) and g == 0 and j == 0):
                        dve.wait_ge(S["added"], g * 2 + j)
                    d = acc[:, bass.ds(tiles[j], 1), :].rearrange("p a w -> p (a w)")
                    v.tensor_tensor(d, d, psO[:, 2 * (r % 2) + j, 0:accw], ALU.add).then_inc(S["added"], 1)

                def step(s, dyn):
                    nxt, now, last = (locate(s, dyn, d) for d in (2, 0, -2))
                    if last is not None:
                        tiles = tiles_of(last)
                    for j in range(3):
                        if now is not None:
                            post["score"][j](dve, v, now, rows, psA, sc, S, fetched)
                        if last is not None and j < 2:
                            add(last, tiles, j)
                    if nxt is not None:
                        onehots(nxt)
                    if now is not None:
                        post["payload"][0](dve, v, now, rows, sc, S)
                    if nxt is not None and post.get("onehots"):
                        post["onehots"](v, nxt, rows, S)
                    if now is not None and len(post["payload"]) > 1:
                        post["payload"][1](dve, v, now, rows, sc, S)
                pipeline(dve, 2, 2, step)

            @block.scalar
            def _(act):
                def indices(at):
                    g, q, r = at
                    if not isinstance(g, int) or g >= DEPTH:
                        act.wait_ge(fetched[r], q * (16 * TPG))
                        hold(act, "act")
                    nc.scalar.activation(gidx[:, r, :], rec[:, bass.ds(g * TPG, TPG), 1], ACT.Copy)\
                        .then_inc(S["gidx_ready"], 1)

                act.wait_ge(S["rec_whole"], 1)

                def step(s, dyn):
                    soon, nxt, now = (locate(s, dyn, d) for d in (3, 1, 0))
                    if now is not None:
                        post["exp"](act, now, rows, sc, S)
                    if nxt is not None:
                        g, q, r = nxt
                        act.wait_ge(S["turned"], g + 1)
                        back(act, S["own_e"], g, 2)
                        nc.scalar.activation(ohT[:, r % 2, :, :].rearrange("p t n -> p (t n)"), psT[:, r % 2, :],
                                             ACT.Copy).then_inc(S["ohT_ready"], 1)
                    if soon is not None:
                        indices(soon)
                    if now is not None and post.get("scale"):
                        post["scale"](act, now, oh, S)
                pipeline(act, 3, 0, step)

            @block.tensor
            def _(pe):
                def step(s, dyn):
                    nxt, now, last = (locate(s, dyn, d) for d in (1, 0, -1))
                    if now is not None:
                        g, q, r = now
                        pe.wait_ge(S["ohT_ready"], g + 1)
                        pe.wait_ge(ownland[r], q * 32 + 32)
                        back(pe, S["own_used"], g, 2)
                        for t in range(TPG):
                            ins = pe.matmul(psA[:, r % 2, t * heads:(t + 1) * heads], ohT[:, r % 2, t, :],
                                            ownv[:, r, t // TPU, own_n - heads:], start=True, stop=True)
                        ins.then_inc(S["own_e"], 1)
                    if nxt is not None:
                        g, q, r = nxt
                        pe.wait_ge(S["oh_ready"], g + 1)
                        back(pe, S["ohT_ready"], g, 2)
                        for t in range(TPG):
                            ins = pe.transpose(psT[:, r % 2, t * P:(t + 1) * P], oh[:, r, t, :], ident[:, :])
                        ins.then_inc(S["turned"], 1)
                    if last is not None:
                        g, q, r = last
                        pe.wait_ge(S["payload"], g + 1)
                        back(pe, S["added"], g, 2, per=2)
                        for t in range(TPG):
                            ins = pe.matmul(psO[:, 2 * (r % 2) + t // TPU, 0:accw], oh[:, r, t, :],
                                            rows[:, r, t, 0:accw], start=(t % TPU == 0), stop=(t % TPU == TPU - 1))
                        ins.then_inc(S["summed"], 1)
                pipeline(pe, 1, 1, step)

        end_phase()

    with ExitStack() as c2:
        acc0 = sb("acc0", [P, NT, A0], c=c2)
        with ExitStack() as c:
            rec = sb("rec0", [P, ST, 4], I32, c=c)
            edge_term = sb("edge_term", [P, ST, H], c=c)
            awe = sb("awe", [P, H, 2 * O + 1], c=c)
            abb = sb("abb", [P, H], c=c)
            s_score = sem("l0_score_steps")

            def l0_sync(sp, S):
                sp.dma_start(awe[:, :, :].rearrange("p h o -> p (h o)"),
                             a["L0_gnn_aw"].rearrange("h o -> (h o)").partition_broadcast(P)).then_inc(S["table_done"], 16)
                sp.dma_start(abb[:, :], a["L0_gnn_ab"].partition_broadcast(P)).then_inc(S["table_done"], 16)

            def l0_complete(dve, link):
                v = nc.vector
                for f in range(2):
                    link(v.tensor_tensor(rec[:, :, f], rec[:, :, f], by_pe[:, f, :], ALU.add))
                weight = rec[:, :, 2:3].bitcast(F32)
                link(v.tensor_tensor(weight, weight, by_pe[:, 2, :].unsqueeze(2), ALU.add))

            def l0_bulk(dve, S, link):
                v = nc.vector
                dve.wait_ge(S["table_done"], 32)
                full = [P, ST, H]
                el = rec[:, :, 2:3].bitcast(F32).to_broadcast(full)
                link(v.tensor_tensor(edge_term[:, :, :], el,
                                     awe[:, :, 2 * O:2 * O + 1].rearrange("p h o -> p o h").to_broadcast(full),
                                     ALU.mult))
                link(v.tensor_tensor(edge_term[:, :, :], edge_term[:, :, :],
                                     abb[:, :].unsqueeze(1).to_broadcast(full), ALU.add))

            def l0_pair(dve, v, at, rows, psA, sc, S, fetched):
                g, q, r = at
                dve.wait_ge(S["own_e"], g + 1)
                dve.wait_ge(fetched[r], q * (16 * TPG) + 16 * TPG)
                v.tensor_tensor(sc[:, r % 2, :, :], psA[:, r % 2, 0:TPG * H].rearrange("p (t h) -> p t h", t=TPG),
                                rows[:, r, :, D:D + H], ALU.add).then_inc(S["own_used"], 1)

            def l0_edge(dve, v, at, rows, psA, sc, S, fetched):
                g, q, r = at
                s = sc[:, r % 2, :, :]
                dve.wait_ge(S["own_used"], g + 1)
                v.tensor_tensor(s, s, edge_term[:, bass.ds(g * TPG, TPG), :], ALU.add).then_inc(s_score, 1)

            def l0_clamp(dve, v, at, rows, psA, sc, S, fetched):
                g, q, r = at
                s = sc[:, r % 2, :, :]
                dve.wait_ge(s_score, g + 1)
                v.tensor_scalar(s, s, -1.0 / 20.0, 0.0, ALU.mult, ALU.min).then_inc(S["score"], 1)

            def l0_exp(act, at, rows, sc, S):
                g, q, r = at
                act.wait_ge(S["score"], g + 1)
                nc.scalar.activation(rows[:, r, :, D:D + H], sc[:, r % 2, :, :], ACT.Exp).then_inc(S["weight"], 1)

            def l0_payload(dve, v, at, rows, sc, S):
                g, q, r = at
                dve.wait_ge(S["weight"], g + 1)
                f = rows[:, r, :, 0:D].rearrange("p t (h o) -> p t h o", h=H)
                v.tensor_tensor(f, f, rows[:, r, :, D:D + H].unsqueeze(3).to_broadcast([P, TPG, H, O]), ALU.mult)\
                    .then_inc(S["payload"], 1)

            edge_phase(0, c, table0, W0, A0, acc0, rec, D + H, H, H,
                       dict(sync=l0_sync, complete=l0_complete, bulk=l0_bulk, score=(l0_pair, l0_edge, l0_clamp), exp=l0_exp,
                            payload=(l0_payload,)))

        with ExitStack() as c:
            dn = Dense("ln1", c, NE)
            XN = sb("XN", [P, NT, D], c=c)
            gw = sb("gw", [P, KD, NE], c=c)
            gb = sb("gb", [P, NE], c=c)
            prob = sb("prob", [P, NT, NE], c=c)
            pick = sb("pick", [P, NT, NE], c=c)
            col = sb("col", [P, 8, NT], c=c)
            keys = sb("keys", [P, 2, NT], c=c)
            wheref = sb("where2", [P, 2 * NT], c=c)
            texp = sb("tile_expert", [P, MT], I32, c=c)
            srt = Sort("sort2", c, P, 2 * NT, NE, P, MT)
            srt.unumber = sb("unumber2", [P, MT], c=c)
            zero = sb("zero", [P, 8, D], c=c)
            chain = sem("chain3")
            gloaded, zfilled, zset = sem("gloaded"), sem("zfilled"), sem("zset")
            kept_rows = sem("kept_rows")
            shifted, exped, tok_ready, dispatched = sem("shifted"), sem("exped"), sem("tok_ready"), sem("dispatched")
            records1 = scatter_sems("rec1a")

            with nc.Block() as block:
                @block.sync
                def _(sp):
                    sp.dma_start(gw[:, :, :], a["L0_ffn_gate_w"].rearrange("(j p) e -> p j e", p=P)).then_inc(gloaded, 16)
                    sp.dma_start(gb[:, :], a["L0_ffn_gate_b"].partition_broadcast(P)).then_inc(gloaded, 16)
                    sp.wait_ge(zset, 1)
                    rest = expert_in.rearrange("(p s) d -> p s d", p=P)
                    for s0 in range(0, MT, 8):
                        n = min(8, MT - s0)
                        sp.dma_start(rest[:, s0:s0 + n, :], zero[:, 0:n, :]).then_inc(zfilled, 16)

                @block.gpsimd
                def _(pool):
                    nc.gpsimd.memset(zero[:, :, :], 0.0).then_inc(zset, 1)
                    nc.gpsimd.iota(srt.unumber[:, :], [[1, MT]], base=0, channel_multiplier=0,
                                   allow_small_or_imprecise_dtypes=True).then_inc(zset, 1)
                    scatter_records(pool, 1, records1, 0, 1)
                    pool.wait_ge(zfilled, 16 * -(-MT // 8))
                    pool.wait_ge(tok_ready, 1)
                    for j in range(2):
                        for t in range(NT):
                            n = LAST if t == NT - 1 else P
                            at = j * NT + t
                            pool.indirect_dma_start(
                                out=expert_in,
                                out_offset=bass.IndirectOffsetOnAxis(ap=tokslot[0:n, at:at + 1], axis=0),
                                in_=XN[0:n, t, :], in_offset=None).then_inc(dispatched, 16)
                    pool.wait_ge(dispatched, 16 * 2 * NT)

                @block.vector
                def _(dve):
                    v = nc.vector
                    ch = Chain(dve, chain)
                    link = ch.link
                    w = acc0[:, :, D:D + H]
                    link(v.tensor_tensor(w, w, padrow[:, :].unsqueeze(2).to_broadcast([P, NT, H]), ALU.add))
                    link(v.reciprocal(w, w))
                    for h in range(H):
                        f = acc0[:, :, h * O:(h + 1) * O]
                        link(v.tensor_tensor(f, f, acc0[:, :, D + h:D + h + 1].to_broadcast([P, NT, O]), ALU.mult))
                    link(v.tensor_tensor(X[:, :, :], X[:, :, :], acc0[:, :, 0:D], ALU.add))
                    dve.wait_ge(gloaded, 32)
                    link(halves(0, NT))
                    dn.moments(dve, link, 0, 0, NT)

                    def logits(at):
                        t, q, r = at
                        v.tensor_tensor(prob[:, bass.ds(t, 1), :].rearrange("p a e -> p (a e)"),
                                        dn.psF[:, r % 2, 0:NE], gb[:, :], ALU.add).then_inc(dn.used, 1)
                        dn.normalised(XN[:, bass.ds(t, 1), :].rearrange("p a d -> p (a d)"), t).then_inc(kept_rows, 1)
                    dn.run_dve(dve, logits)
                    dve.wait_ge(kept_rows, NT)
                    dve.wait_ge(dn.used, NT)
                    full = [P, NT, NE]

                    def over(x):
                        return x.unsqueeze(2).to_broadcast(full)

                    number = iota[:, 0:NE].unsqueeze(1).to_broadcast(full)
                    link(v.tensor_reduce(col[:, 0, :], prob[:, :, :], AX.X, ALU.max))
                    v.tensor_tensor(prob[:, :, :], prob[:, :, :], over(col[:, 0, :]), ALU.subtract).then_inc(shifted, 1)
                    dve.wait_ge(exped, 1)
                    link(v.tensor_reduce(col[:, 1, :], prob[:, :, :], AX.X, ALU.add))
                    link(v.reciprocal(col[:, 2, :], col[:, 1, :]))
                    link(v.tensor_tensor(prob[:, :, :], prob[:, :, :], over(col[:, 2, :]), ALU.mult))
                    backwards = srt.small[:, 7, 0:NE]
                    link(v.tensor_scalar(backwards, iota[:, 0:NE], -1.0, float(NE), ALU.mult, ALU.add))
                    for j in range(2):
                        link(v.tensor_reduce(col[:, 3 + j, :], prob[:, :, :], AX.X, ALU.max))
                        link(v.tensor_tensor(pick[:, :, :], prob[:, :, :], over(col[:, 3 + j, :]), ALU.is_equal))
                        link(v.tensor_tensor(pick[:, :, :], pick[:, :, :],
                                             backwards.unsqueeze(1).to_broadcast(full), ALU.mult))
                        link(v.tensor_reduce(keys[:, j, :], pick[:, :, :], AX.X, ALU.max))
                        link(v.tensor_scalar(keys[:, j, :], keys[:, j, :], -1.0, float(NE), ALU.mult, ALU.add))
                        if j == 0:
                            link(v.tensor_tensor(pick[:, :, :], number, over(keys[:, 0, :]), ALU.is_equal))
                            link(v.scalar_tensor_tensor(prob[:, :, :], pick[:, :, :], -2.0, prob[:, :, :],
                                                        ALU.mult, ALU.add))
                    link(v.tensor_tensor(col[:, 5, :], col[:, 3, :], col[:, 4, :], ALU.add))
                    link(v.reciprocal(col[:, 6, :], col[:, 5, :]))
                    for j in range(2):
                        link(v.tensor_tensor(wts[:, j, :], col[:, 3 + j, :], col[:, 6, :], ALU.mult))
                        link(v.scalar_tensor_tensor(keys[:, j, :], padrow[:, :], float(2 * NE), keys[:, j, :],
                                                    ALU.mult, ALU.add))
                    dve.wait_ge(zset, 2)
                    srt.vector(dve, link, keys[:, :, :].rearrange("p j t -> p (j t)"), texp[:, :], wheref[:, :],
                               ((0, 2 * NT),),
                               lambda lo, hi: v.tensor_copy(tokslot[:, :], wheref[:, :]).then_inc(tok_ready, 1))

                @block.scalar
                def _(act):
                    dn.run_act(act)
                    act.wait_ge(shifted, 1)
                    nc.scalar.activation(prob[:, :, :], prob[:, :, :], ACT.Exp).then_inc(exped, 1)

                @block.tensor
                def _(pe):
                    pe.wait_ge(gloaded, 32)
                    dn.run_pe(pe, gw)
                    srt.tensor(pe)

            end_phase()

            with ExitStack() as cc:
                xs = sb("xs", [P, DEPTH, D], c=cc)
                xsT = sb("xsT", [P, 2, KD, P], c=cc)
                w1s = sb("w1s", [P, DEPTH, KD, FH], c=cc)
                w2s = sb("w2s", [P, DEPTH, KD, FH], c=cc)
                w3s = sb("w3s", [P, DEPTH, FH // P, D], c=cc)
                gate = sb("gate", [P, 2, FH], c=cc)
                hid = sb("hid", [P, 2, FH], c=cc)
                ys = sb("ys", [P, DEPTH, D], c=cc)
                names = ("turned", "xsT_ready", "h1", "h2", "gated", "hidden", "y", "y_copied")
                S = {n: sem("m_" + n) for n in names}
                xland = [sem(f"m_xland{r}") for r in range(DEPTH)]
                wland = [sem(f"m_wland{r}") for r in range(DEPTH)]
                ystored = [sem(f"m_ystored{r}") for r in range(DEPTH)]
                records1 = [scatter_sems("rec1b"), scatter_sems("rec1c")]
                rel_scored = sem("m_rel_scored")
                relpick = XN[0:EP, :, :].rearrange("p t d -> p (t d)")[:, 0:XREL_STEP * R]\
                    .rearrange("p (k r) -> p k r", k=XREL_STEP)

                psX, psH1 = dn.psT, dn.psF
                psH2, psY = ps("psH2", [P, 2, 512], cc), (srt.psum, ps("psY2", [P, 512], cc))

                pipeline, locate, back = ring(MT, DEPTH)

                with nc.Block() as block:
                    @block.sync
                    def _(sp):
                        def step(s, dyn):
                            t, q, r = locate(s, dyn, 0)
                            back(sp, S["turned"], t, DEPTH)
                            sp.dma_start(xs[:, r, :], expert_in[bass.ds(t * P, P), :]).then_inc(xland[r], 16)
                            back(sp, S["y"], t, DEPTH)
                            hold(sp, "sp")
                            e = sp.value_load(texp[0:1, bass.ds(t, 1)], min_val=0, max_val=NE - 1)
                            for w, d in ((w1s, a["L0_ffn_w1"]), (w2s, a["L0_ffn_w2"]), (w3s, a["L0_ffn_w3"])):
                                sp.dma_start(w[:, r, :, :], d[bass.ds(e, 1), :, :]
                                             .rearrange("e (j p) n -> p (e j) n", p=P)).then_inc(wland[r], 16)
                        pipeline(sp, 0, 0, step)

                    @block.gpsimd
                    def _(pool):
                        scatter_records(pool, 1, records1[0], 1, 3)
                        pool.wait_ge(rel_scored, XREL_STEPS)
                        scatter_records(pool, 1, records1[1], 3, TURNS)
                        for r in range(DEPTH):
                            pool.wait_ge(ystored[r], 16 * (MT // DEPTH))

                    @block.vector
                    def _(dve):
                        v = nc.vector

                        def step(s, dyn, relations=False):
                            now, last = locate(s, dyn, 0), locate(s, dyn, -1)
                            if now is not None:
                                t, q, r = now
                                dve.wait_ge(S["gated"], t + 1)
                                dve.wait_ge(S["h2"], t + 1)
                                back(dve, S["y"], t, 2)
                                v.tensor_tensor(hid[:, r % 2, :], gate[:, r % 2, :], psH2[:, r % 2, :], ALU.mult)\
                                    .then_inc(S["hidden"], 1)
                            if last is not None:
                                t, q, r = last
                                dve.wait_ge(S["y"], t + 1)
                                if not isinstance(t, int) or t >= DEPTH:
                                    dve.wait_ge(ystored[r], q * 16)
                                v.tensor_copy(ys[:, r, :], psY[r % 2][:, 0:D]).then_inc(S["y_copied"], 1)
                            if now is not None and relations:
                                t, q, r = now
                                back(dve, rel_scored, t, 1)
                                for j in range(XREL_STEP):
                                    at = t * XREL_STEP + (XREL0 + j)
                                    ins = v.scalar_tensor_tensor(
                                        relpick[:, j, :], iota[0:EP, :], relation[:, bass.ds(at, 1)], relrow[0:EP, :],
                                        ALU.is_equal, ALU.mult, accum_out=rec_s[1][:, bass.ds(at, 1), 3].bitcast(F32))
                                ins.then_inc(rel_scored, 1)
                        for s in range(DEPTH):
                            step(s, None, True)
                        with dve.Fori(1, XREL_STEPS // DEPTH) as q:
                            for r in range(DEPTH):
                                step(None, (q, r), True)
                        with dve.Fori(XREL_STEPS // DEPTH, MT // DEPTH - 1) as q:
                            for r in range(DEPTH):
                                step(None, (q, r))
                        for s in range(MT - DEPTH, MT + 1):
                            step(s, None)

                    @block.scalar
                    def _(act):
                        def step(s, dyn):
                            nxt, now, last = (locate(s, dyn, d) for d in (1, 0, -1))
                            if nxt is not None:
                                t, q, r = nxt
                                act.wait_ge(S["turned"], t + 1)
                                back(act, S["h2"], t, 2)
                                nc.scalar.activation(xsT[:, r % 2, :, :], psX[:, r % 2, 0:D].rearrange("p (a b) -> p a b", a=KD),
                                                     ACT.Copy).then_inc(S["xsT_ready"], 1)
                            if now is not None:
                                t, q, r = now
                                act.wait_ge(S["h1"], t + 1)
                                back(act, S["hidden"], t, 2)
                                nc.scalar.activation(gate[:, r % 2, :], psH1[:, r % 2, :], ACT.Silu).then_inc(S["gated"], 1)
                            if last is not None:
                                t, q, r = last
                                act.wait_ge(S["y_copied"], t + 1)
                                act.dma_start(expert_out[bass.ds(t * P, P), :], ys[:, r, :]).then_inc(ystored[r], 16)
                        pipeline(act, 1, 1, step)

                    @block.tensor
                    def _(pe):
                        def step(s, dyn):
                            nxt, now, last = (locate(s, dyn, d) for d in (1, 0, -1))
                            if nxt is not None:
                                t, q, r = nxt
                                pe.wait_ge(xland[r], q * 16 + 16)
                                back(pe, S["xsT_ready"], t, 2)
                                for j in range(KD):
                                    ins = pe.transpose(psX[:, r % 2, j * P:(j + 1) * P], xs[:, r, j * P:(j + 1) * P],
                                                       ident[:, :])
                                ins.then_inc(S["turned"], 1)
                            if now is not None:
                                t, q, r = now
                                pe.wait_ge(S["xsT_ready"], t + 1)
                                pe.wait_ge(wland[r], q * 48 + 48)
                                for w, p_, name, freed in ((w1s, psH1, "h1", "gated"), (w2s, psH2, "h2", "hidden")):
                                    back(pe, S[freed], t, 2)
                                    for m in range(FH // P):
                                        for j in range(KD):
                                            ins = pe.matmul(p_[:, r % 2, m * P:(m + 1) * P], w[:, r, j, m * P:(m + 1) * P],
                                                            xsT[:, r % 2, j, :], start=(j == 0), stop=(j == KD - 1))
                                    ins.then_inc(S[name], 1)
                            if last is not None:
                                t, q, r = last
                                pe.wait_ge(S["hidden"], t + 1)
                                back(pe, S["y_copied"], t, 2)
                                for m in range(FH // P):
                                    ins = pe.matmul(psY[r % 2][:, 0:D], hid[:, r % 2, m * P:(m + 1) * P],
                                                    w3s[:, r, m, :], start=(m == 0), stop=(m == FH // P - 1))
                                ins.then_inc(S["y"], 1)
                        pipeline(pe, 1, 1, step)

                end_phase()

    with ExitStack() as c4:
        acc1 = sb("acc1", [P, NT, A1], c=c4)
        relW = sb("relW", [P, 2, D], c=c4)
        loops = sb("loops", [P, NT, 2 * D], c=c4)
        with ExitStack() as c:
            rec = sb("rec1", [P, ST, 4], I32, c=c)
            with ExitStack() as cc:
                dn = Dense("ln2", cc, W1)
                wn = sb("wn", [P, KD, W1], c=cc)
                frow = sb("frow1", [P, CH, W1], c=cc)
                psR = ps("psR", [P, 512], cc)
                flat = acc1[:, :, :].rearrange("p t w -> p (t w)")
                token_rows = (flat[:, 0:NT * D].rearrange("p (t d) -> p t d", t=NT),
                              sb("token_rows1", [P, NT, D], c=cc))
                wl = flat[:, NT * D:NT * D + 2 * KD * D].rearrange("p (j n) -> p j n", j=KD)
                psL = ps("psL", [P, 2, 512], cc)
                looped, loop_kept, wl_loaded = sem("looped"), sem("loop_kept"), sem("wl_loaded")
                token_land, token_have, mixed = [sem("tok_l0"), sem("tok_l1")], sem("tok_have"), sem("tok_mixed")
                wloaded, wready, chain = sem("w4_loaded"), sem("w4_ready"), sem("chain4")
                rel_p = sem("rel_product")
                fready, fstored = sem("f4_ready"), [sem(f"f4st{r}") for r in range(CH)]
                moment_steps = sem("moment_steps")

                with nc.Block() as block:
                    @block.sync
                    def _(sp):
                        sp.dma_start(wn[:, :, 0:D], a["L1_gnn_weight_neighbor"].rearrange("(j p) n -> p j n", p=P))\
                            .then_inc(wloaded, 16)
                        for e, w in enumerate(("L1_gnn_loop_weight", "L1_gnn_evolve_loop_weight")):
                            sp.dma_start(wl[:, :, e * D:(e + 1) * D], a[w].rearrange("(j p) n -> p j n", p=P))\
                                .then_inc(wl_loaded, 16)
                        def store(s, dyn):
                            t, q, r = dn.locate(s, dyn, 0)
                            sp.wait_ge(fready, t + 1)
                            sp.dma_start(table1[bass.ds(t * P, P), :], frow[:, r, :]).then_inc(fstored[r], 16)
                        dn.pipeline(sp, 0, 0, store)
                        for r in range(CH):
                            sp.wait_ge(fstored[r], 16 * NCH)

                    @block.gpsimd
                    def _(pool):
                        for i in range(NCH + 1):
                            for j in range(2 if i < NCH else 0):
                                for t in range(i * CH, (i + 1) * CH):
                                    at = j * NT + t
                                    pool.indirect_dma_start(
                                        out=token_rows[j][:, t, :], out_offset=None, in_=expert_out,
                                        in_offset=bass.IndirectOffsetOnAxis(ap=tokslot[:, at:at + 1], axis=0))\
                                        .then_inc(token_land[i % 2], 16)
                            if i:
                                pool.wait_ge(token_land[(i - 1) % 2], 32 * CH * ((i + 1) // 2))
                                pool.sem_inc(token_have, 1)

                    @block.vector
                    def _(dve):
                        v = nc.vector
                        ch = Chain(dve, chain)
                        link = ch.link
                        dve.wait_ge(wloaded, 16)
                        for j in range(KD):
                            for e in range(2):
                                link(v.tensor_copy(wn[:, j, D + e:D + e + 1], wcol[:, e * KD + j:e * KD + j + 1]))
                        dve.sem_inc(wready, 1)
                        dve.wait_ge(rel_p, 1)
                        link(v.tensor_copy(relW[:, 0, :], psR[:, 0:D]))
                        link(v.tensor_copy(relW[0:R - P, 1, :], psR[0:R - P, D:2 * D]))

                        def mix(i):
                            dve.wait_ge(token_have, i + 1)
                            for j in range(2):
                                for k in range(CH):
                                    t = bass.ds(i * CH + k, 1)
                                    xt, row = (m.rearrange("p a d -> p (a d)")
                                               for m in (X[:, t, :], token_rows[j][:, t, :]))
                                    ins = v.scalar_tensor_tensor(xt, row, wts[:, j, t], xt, ALU.mult, ALU.add)
                                ins.then_inc(mixed, 1)
                                dve.wait_ge(mixed, i * 2 + (1 + j))

                        def moments(i):
                            mix(i)
                            hold(dve, "dve")
                            halves(i * CH, CH).then_inc(moment_steps, 1)
                            steps = [1]
                            dve.wait_ge(moment_steps, i * (dn.LINKS) + 1)

                            def link(ins):
                                steps[0] += 1
                                ins.then_inc(moment_steps, 1)
                                dve.wait_ge(moment_steps, i * dn.LINKS + steps[0])
                            dn.moments(dve, link, i, i * CH, CH)
                            assert steps[0] == dn.LINKS

                        def step(s, dyn):
                            soon = dn.locate(s, dyn, 2)
                            if soon is not None:
                                if soon[2] == 0:
                                    moments(soon[1])
                                dn.norm(dve, soon)
                        dn.pipeline(dve, 2, -2, step)

                    @block.scalar
                    def _(act):
                        def step(s, dyn):
                            now, last = (dn.locate(s, dyn, d) for d in (0, -1))
                            if now is not None:
                                t, q, r = now
                                if s == 0:
                                    dn.scalar_std(act, 0, 0, CH)
                                if r == CH - 2 and not (isinstance(q, int) and q == NCH - 1):
                                    dn.scalar_std(act, q + 1, (q + 1) * CH, CH)
                                dn.copy(act, now)
                            if last is not None:
                                t, q, r = last
                                act.wait_ge(dn.product, t + 1)
                                if not isinstance(t, int) or t >= CH:
                                    act.wait_ge(fstored[r], q * 16)
                                nc.scalar.activation(frow[:, r, :], dn.psF[:, r % 2, 0:W1], ACT.Copy)\
                                    .then_inc(fready, 1)
                                act.wait_ge(fready, t + 1)
                                act.sem_inc(dn.used, 1)
                                act.wait_ge(looped, t + 1)
                                hold(act, "act")
                                nc.scalar.activation(loops[:, bass.ds(t, 1), :].rearrange("p a n -> p (a n)"),
                                                     psL[:, r % 2, :], ACT.Copy).then_inc(loop_kept, 1)
                        dn.pipeline(act, 0, 1, step)

                    @block.tensor
                    def _(pe):
                        pe.wait_ge(wloaded, 16)
                        for b, n in ((0, P), (1, R - P)):
                            for j in range(KD):
                                ins = pe.matmul(psR[0:n, b * D:(b + 1) * D], relT[:, j, b * P:b * P + n],
                                                wn[:, j, 0:D], start=(j == 0), stop=(j == KD - 1))
                        ins.then_inc(rel_p, 1)
                        pe.wait_ge(wready, 1)

                        pe.wait_ge(wl_loaded, 32)

                        def step(s, dyn):
                            nxt, now = (dn.locate(s, dyn, d) for d in (1, 0))
                            if nxt is not None:
                                dn.transposes(pe, nxt)
                            if now is not None:
                                t, q, r = now
                                pe.wait_ge(dn.copied, t + 1)
                                bank(pe, loop_kept, now)
                                for j in range(KD):
                                    ins = pe.matmul(psL[:, r % 2, :], dn.xT[:, r, j, :], wl[:, j, :],
                                                    start=(j == 0), stop=(j == KD - 1))
                                ins.then_inc(looped, 1)
                                dn.products(pe, now, wn)
                        dn.pipeline(pe, 1, 0, step)

                end_phase()

            inverse = sb("inverse", [P, 2, TPG], c=c)
            steps, tail = sem("l1_steps"), sem("l1_tail")

            def l1_onehots(v, at, rows, S):
                g, q, r = at
                v.tensor_tensor(rows[:, r, :, W1:A1], rec[:, bass.ds(g * TPG, TPG), 2:3].to_broadcast([P, TPG, R]),
                                iota[:, :].unsqueeze(1).to_broadcast([P, TPG, R]), ALU.is_equal)\
                    .then_inc(S["counted"], 1)

            def l1_edge(dve, v, at, rows, psA, sc, S, fetched):
                g, q, r = at
                dve.wait_ge(fetched[r], q * (16 * TPG) + 16 * TPG)
                v.tensor_tensor(sc[:, r % 2, :, :], rows[:, r, :, D:D + 1],
                                rec[:, bass.ds(g * TPG, TPG), 3:4].bitcast(F32), ALU.add).then_inc(steps, 1)

            def l1_pair(dve, v, at, rows, psA, sc, S, fetched):
                g, q, r = at
                s = sc[:, r % 2, :, :]
                dve.wait_ge(S["own_e"], g + 1)
                dve.wait_ge(steps, g + 1)
                v.tensor_tensor(s, s, psA[:, r % 2, 0:TPG].unsqueeze(2), ALU.add).then_inc(S["own_used"], 1)

            def l1_leak(dve, v, at, rows, psA, sc, S, fetched):
                g, q, r = at
                s = sc[:, r % 2, :, :]
                dve.wait_ge(S["own_used"], g + 1)
                v.scalar_tensor_tensor(s, s, 0.01, s, ALU.mult, ALU.max).then_inc(S["score"], 1)

            def l1_exp(act, at, rows, sc, S):
                g, q, r = at
                act.wait_ge(S["score"], g + 1)
                nc.scalar.activation(sc[:, r % 2, :, :], sc[:, r % 2, :, :], ACT.Exp).then_inc(S["weight"], 1)

            def l1_scale(act, at, oh, S):
                g, q, r = at
                act.wait_ge(tail, g * 2 + 2)
                act.wait_ge(S["turned"], g + 1)
                act.wait_ge(S["counted"], g + 1)
                for t in range(TPG):
                    ins = nc.scalar.activation(oh[:, r, t, :], oh[:, r, t, :], ACT.Copy,
                                               scale=inverse[:, r % 2, t:t + 1])
                ins.then_inc(S["payload"], 1)

            def l1_inverse(dve, v, at, rows, sc, S):
                g, q, r = at
                dve.wait_ge(S["weight"], g + 1)
                if not isinstance(g, int) or g >= 2:
                    dve.wait_ge(S["payload"], g - 1)
                v.reciprocal(inverse[:, r % 2, :], sc[:, r % 2, :, 0]).then_inc(tail, 1)

            def l1_share(dve, v, at, rows, sc, S):
                g, q, r = at
                dve.wait_ge(tail, g * 2 + 1)
                v.tensor_tensor(inverse[:, r % 2, :], sc[:, r % 2, :, 0], inverse[:, r % 2, :], ALU.mult)\
                    .then_inc(tail, 1)

            edge_phase(1, c, table1, W1, A1, acc1, rec, D, 2, 1,
                       dict(onehots=l1_onehots, score=(l1_edge, l1_pair, l1_leak), exp=l1_exp,
                            scale=l1_scale, payload=(l1_inverse, l1_share)))

        with ExitStack() as c:
            cnt = sb("cnt", [P, CH, R], c=c)
            cntT = sb("cntT", [P, CH, 2, P], c=c)
            deg = sb("deg", [P, 2, NT], c=c)
            upd = sb("upd", [P, CH, D], c=c)
            psC = ps("psC", [P, 2, 512], c)
            psG = ps("psG", [P, 2, 512], c)
            chain, updated = sem("chain5"), sem("updated")
            cready, cturned, ccopied, gsum = sem("c_ready"), sem("c_turned"), sem("c_copied"), sem("g_sum")
            added, clamped, looped = sem("u_added"), sem("u_clamped"), sem("u_looped")
            pipeline, locate, back = by_tiles

            with nc.Block() as block:
                @block.vector
                def _(dve):
                    v = nc.vector
                    link = Chain(dve, chain).link
                    link(v.tensor_reduce(deg[:, 0, :], acc1[:, :, W1:A1], AX.X, ALU.add))
                    link(v.tensor_scalar(deg[:, 0, :], deg[:, 0, :], 0.0, None, ALU.is_gt))
                    link(v.tensor_scalar(deg[:, 1, :], deg[:, 0, :], -1.0, 1.0, ALU.mult, ALU.add))

                    def update(s, dyn):
                        t, q, r = locate(s, dyn, 0)
                        b = r % 2
                        at = bass.ds(t, 1)
                        xt, agg, loop, evolve = (m.rearrange("p a w -> p (a w)") for m in (
                            X[:, at, :], acc1[:, at, 0:D], loops[:, at, 0:D], loops[:, at, D:2 * D]))
                        v.scalar_tensor_tensor(xt, loop, deg[:, 0, at], xt, ALU.mult, ALU.add).then_inc(looped, 1)
                        dve.wait_ge(gsum, t + 1)
                        v.tensor_tensor(upd[:, r, :], psG[:, b, 0:D], agg, ALU.add).then_inc(added, 1)
                        dve.wait_ge(looped, t * 2 + 1)
                        v.scalar_tensor_tensor(xt, evolve, deg[:, 1, at], xt, ALU.mult, ALU.add).then_inc(looped, 1)
                        if not isinstance(t, int) or t >= 1:
                            dve.wait_ge(updated, t)
                            hold(dve, "dve")
                            halves(t - 1, 1)
                        dve.wait_ge(added, t + 1)
                        dve.wait_ge(looped, t * 2 + 2)
                        v.scalar_tensor_tensor(xt, upd[:, r, :], 0.0, xt, ALU.max, ALU.add).then_inc(updated, 1)
                    pipeline(dve, 0, 0, update)
                    dve.wait_ge(updated, NT)
                    link(halves(NT - 1, 1))

                @block.scalar
                def _(act):
                    def step(s, dyn):
                        soon, nxt = (locate(s, dyn, d) for d in (2, 1))
                        if nxt is not None:
                            t, q, r = nxt
                            act.wait_ge(cturned, t + 1)
                            back(act, gsum, t, CH)
                            nc.scalar.activation(cntT[:, r, 0, :], psC[:, r % 2, 0:P], ACT.Copy)
                            nc.scalar.activation(cntT[0:R - P, r, 1, :], psC[0:R - P, r % 2, P:2 * P], ACT.Copy)\
                                .then_inc(ccopied, 1)
                        if soon is not None:
                            t, q, r = soon
                            back(act, cturned, t, CH)
                            hold(act, "act")
                            nc.scalar.activation(cnt[:, r, :],
                                                 acc1[:, bass.ds(t, 1), W1:A1].rearrange("p a w -> p (a w)"),
                                                 ACT.Copy).then_inc(cready, 1)
                    pipeline(act, 2, 0, step)

                @block.tensor
                def _(pe):
                    def step(s, dyn):
                        nxt, now = (locate(s, dyn, d) for d in (1, 0))
                        if nxt is not None:
                            t, q, r = nxt
                            pe.wait_ge(cready, t + 1)
                            bank(pe, ccopied, nxt)
                            pe.transpose(psC[:, r % 2, 0:P], cnt[:, r, 0:P], ident[:, :])
                            pe.transpose(psC[0:R - P, r % 2, P:2 * P], cnt[:, r, P:R], ident[:, :])\
                                .then_inc(cturned, 1)
                        if now is not None:
                            t, q, r = now
                            pe.wait_ge(ccopied, t + 1)
                            bank(pe, added, now)
                            pe.matmul(psG[:, r % 2, 0:D], cntT[:, r, 0, :], relW[:, 0, :], start=True, stop=False)
                            pe.matmul(psG[:, r % 2, 0:D], cntT[0:R - P, r, 1, :], relW[0:R - P, 1, :], start=False,
                                      stop=True).then_inc(gsum, 1)
                    pipeline(pe, 1, 0, step)

            end_phase()

    with ExitStack() as c:
        dn = Dense("ln4", c, 1)
        Z = sb("Z", [P, NT, D], c=c)
        zT = sb("zT", [P, KD, NT * P], c=c)
        wrc = sb("wrc", [P, KD, 1], c=c)
        brc = sb("brc", [P, 1], c=c)
        w1 = sb("f_w1", [P, KD, FF], c=c)
        w2 = sb("f_w2", [P, FF // P, D], c=c)
        b1 = sb("f_b1", [P, FF // P], c=c)
        b2 = sb("f_b2", [P, D], c=c)
        score = sb("score", [P, NT], c=c)
        srow = sb("srow", [P, NT * P], c=c)
        above = sb("above", [P, NT * P], mybir.dt.bfloat16, c=c)
        tie = sb("tie", [P, P], c=c)
        earlier = sb("earlier", [P, P], c=c)
        rank = sb("rank", [P, 3, NT], c=c)
        HALF = CH * P // 2
        hid = sb("f_hid", [P, FF // P, 2 * HALF], c=c)
        psHid = ps("f_psH", [P, 2, 512], c)
        psY = ps("f_psY", [P, 2, 512], c)
        xland, wloaded, chain, rowland, kept_rows = (sem(n) for n in ("w6_xl", "w6_loaded", "chain6", "rowland", "kept_rows6"))
        stored_s, zTc = sem("stored_s"), sem("zTc")
        hidp, gelu, yp, yd, hfree = sem("hidp"), sem("gelu"), sem("yp"), sem("yd"), sem("hfree")
        final, outd, chunk_free = sem("final"), sem("outd"), sem("chunk_free")
        residual, biased = sem("residual"), sem("biased")
        NH = 2 * FF // P
        assert NH + CH >= NT - CH
        YF = sb("YF", [P, NT, D], c=c)

        with nc.Block() as block:
            @block.sync
            def _(sp):
                with nc.allow_non_contiguous_dma(reason="one small vector, row j * 128 + p to partition p"):
                    sp.dma_start(wrc[:, :, :], a["L1_ffn_wr"].rearrange("(j p) o -> p j o", p=P)).then_inc(wloaded, 16)
                sp.dma_start(brc[:, :], a["L1_ffn_br"].partition_broadcast(P)).then_inc(wloaded, 16)
                sp.dma_start(w1[:, :, :], a["L1_ffn_w1"].rearrange("(j p) n -> p j n", p=P)).then_inc(xland, 16)
                sp.dma_start(w2[:, :, :], a["L1_ffn_w2"].rearrange("(j p) n -> p j n", p=P)).then_inc(xland, 16)
                with nc.allow_non_contiguous_dma(reason="one small vector, hidden unit j * 128 + p to partition p"):
                    sp.dma_start(b1[:, :], a["L1_ffn_b1"].rearrange("(j p) -> p j", p=P)).then_inc(xland, 16)
                sp.dma_start(b2[:, :], a["L1_ffn_b2"].partition_broadcast(P)).then_inc(xland, 16)
                sp.wait_ge(dn.used, NT)
                with nc.allow_non_contiguous_dma(reason="the scores, turned once"):
                    sp.dma_start(score_d.rearrange("(t p) o -> p (t o)", p=P), score[:, :]).then_inc(stored_s, 16)
                sp.wait_ge(stored_s, 16)
                sp.dma_start(srow[:, :], score_d.rearrange("n o -> (n o)").partition_broadcast(P)).then_inc(rowland, 16)
                with sp.Fori(0, NCH - 1) as i:
                    sp.wait_ge(final, i + 1)
                    sp.dma_start(out[bass.ds(i * (CH * P), CH * P), :].rearrange("(t p) d -> p t d", p=P),
                                 X[:, bass.ds(i * CH, CH), :]).then_inc(outd, 16)
                sp.wait_ge(final, NCH)
                t0 = (NCH - 1) * CH
                sp.dma_start(out[t0 * P:(NT - 1) * P, :].rearrange("(t p) d -> p t d", p=P), X[:, t0:NT - 1, :])\
                    .then_inc(outd, 16)
                sp.dma_start(out[(NT - 1) * P:N, :], X[0:LAST, NT - 1, :]).then_inc(outd, 16)
                sp.wait_ge(outd, 16 * (NCH + 1))

            @block.vector
            def _(dve):
                v = nc.vector
                ch = Chain(dve, chain)
                link = ch.link
                dve.wait_ge(wloaded, 32)
                dn.moments(dve, link, 0, 0, NT)

                def scores(at):
                    t, q, r = at
                    v.tensor_tensor(score[:, bass.ds(t, 1)], dn.psF[:, r % 2, 0:1], brc[:, :], ALU.add)\
                        .then_inc(dn.used, 1)
                    dn.normalised(Z[:, bass.ds(t, 1), :].rearrange("p a d -> p (a d)"), t).then_inc(kept_rows, 1)
                dn.run_dve(dve, scores)
                dve.wait_ge(kept_rows, NT)
                dve.wait_ge(rowland, 16)
                link(v.memset(rank[:, :, :], 0.0))
                link(v.tensor_tensor(earlier[:, :], ones[:, :], before[:, :], ALU.subtract))
                link(v.tensor_tensor(earlier[:, :], earlier[:, :], ident[:, :], ALU.subtract))
                for t in range(NT):
                    own = score[:, t:t + 1]
                    if t:
                        v.tensor_scalar(above[:, 0:t * P], srow[:, 0:t * P], own, 0.0, ALU.is_ge, ALU.add,
                                        accum_out=rank[:, 0, t:t + 1])
                    v.tensor_scalar(above[:, t * P:N], srow[:, t * P:N], own, 0.0, ALU.is_gt, ALU.add,
                                    accum_out=rank[:, 1, t:t + 1])
                    n = min(P, N - t * P)
                    link(v.scalar_tensor_tensor(tie[:, 0:n], srow[:, t * P:t * P + n], own, earlier[:, 0:n],
                                                ALU.is_equal, ALU.mult, accum_out=rank[:, 2, t:t + 1]))
                for j in range(1, 3):
                    link(v.tensor_tensor(rank[:, 0, :], rank[:, 0, :], rank[:, j, :], ALU.add))
                link(v.scalar_tensor_tensor(rank[:, 1, :], rank[:, 0, :], float(SELECTED), score[:, :], ALU.is_lt,
                                            ALU.mult))
                dve.wait_ge(residual, 1)
                with dve.Fori(0, NCH) as i:
                    dve.wait_ge(biased, i + 1)
                    for k in range(CH):
                        t = bass.ds(i * CH + k, 1)
                        xt, y = (m[:, t, :].rearrange("p a d -> p (a d)") for m in (X, YF))
                        ins = v.scalar_tensor_tensor(xt, y, rank[:, 1, t], xt, ALU.mult, ALU.add)
                    ins.then_inc(final, 1)

            @block.scalar
            def _(act):
                dn.scalar_std(act, 0, 0, NT)

                def keep(t):
                    at = t, t // CH, t % CH
                    dn.copy(act, at)
                    act.wait_ge(dn.copied, t + 1)
                    nc.scalar.activation(zT[:, :, t * P:(t + 1) * P], dn.xT[:, at[2], :, :], ACT.Copy)\
                        .then_inc(zTc, 1)

                def chunk(i, beside=lambda n: None):
                    for n in range(NH):
                        m, h = n // 2, n % 2
                        beside(n)
                        act.wait_ge(hidp, i * NH + n + 1)
                        if n == 0:
                            act.wait_ge(hfree, i + 1)
                        nc.scalar.activation(hid[:, m, h * HALF:(h + 1) * HALF], psHid[:, h, 0:HALF],
                                             ACT.Gelu_apprx_tanh, bias=b1[:, m:m + 1]).then_inc(gelu, 1)
                    for k in range(CH):
                        beside(NH + k)
                        act.wait_ge(yp, i * CH + k + 1)
                        hold(act, "act")
                        nc.scalar.activation(YF[:, bass.ds(i * CH + k, 1), :].rearrange("p a d -> p (a d)"),
                                             psY[:, k % 2, 0:D], ACT.Copy).then_inc(yd, 1)

                for t in range(CH):
                    keep(t)
                act.wait_ge(xland, 64)
                chunk(0, lambda n: keep(CH + n) if CH + n < NT else None)
                with act.Fori(1, NCH) as i:
                    chunk(i)

            @block.tensor
            def _(pe):
                pe.wait_ge(wloaded, 32)

                def score_tile(t):
                    if t + 1 < NT:
                        dn.transposes(pe, (t + 1, (t + 1) // CH, (t + 1) % CH))
                    dn.products(pe, (t, t // CH, t % CH), wrc)

                def chunk(i, beside=lambda n: None):
                    for n in range(NH):
                        m, h = n // 2, n % 2
                        if n < 2:
                            pe.wait_ge(chunk_free, i + 1)
                        else:
                            pe.wait_ge(gelu, i * NH + n - 1)
                        for j in range(KD):
                            ins = pe.matmul(psHid[:, h, 0:HALF], w1[:, j, m * P:(m + 1) * P],
                                            zT[:, j, bass.ds(i * (2 * HALF) + h * HALF, HALF)],
                                            start=(j == 0), stop=(j == KD - 1))
                        ins.then_inc(hidp, 1)
                        beside(n)
                    pe.wait_ge(gelu, i * NH + NH)
                    pe.sem_inc(chunk_free, 1)
                    for k in range(CH):
                        if k >= 2:
                            pe.wait_ge(yd, i * CH + k - 1)
                        for m in range(FF // P):
                            ins = pe.matmul(psY[:, k % 2, 0:D], hid[:, m, k * P:(k + 1) * P],
                                            w2[:, m, :], start=(m == 0), stop=(m == FF // P - 1))
                        ins.then_inc(yp, 1)
                        beside(NH + k)
                    pe.wait_ge(yd, i * CH + CH)
                    pe.sem_inc(hfree, 1)

                dn.transposes(pe, (0, 0, 0))
                for t in range(CH):
                    score_tile(t)
                pe.wait_ge(zTc, CH)
                pe.wait_ge(xland, 64)
                pe.sem_inc(hfree, 1)
                chunk(0, lambda n: score_tile(CH + n) if CH + n < NT else None)
                pe.wait_ge(zTc, NT)
                with pe.Fori(1, NCH) as i:
                    chunk(i)

            @block.gpsimd
            def _(pool):
                pool.sem_inc(chunk_free, 1)
                pool.wait_ge(kept_rows, NT)
                nc.gpsimd.tensor_tensor(X[:, :, :], X[:, :, :], Z[:, :, :], ALU.add).then_inc(residual, 1)
                pool.wait_ge(xland, 64)
                with pool.Fori(0, NCH) as i:
                    pool.wait_ge(yd, i * CH + CH)
                    hold(pool, "pool")
                    y = YF[:, bass.ds(i * CH, CH), :]
                    nc.gpsimd.tensor_tensor(y, y, b2[:, :].unsqueeze(1).to_broadcast([P, CH, D]), ALU.add)\
                        .then_inc(biased, 1)
    ctx.close()


_INS = ["x", "src", "dst", "edge_type_200", "edge_weight", "L0_gnn_Ws", "L0_gnn_bs", "L0_gnn_aw", "L0_gnn_ab",
        "L0_ffn_gate_w", "L0_ffn_gate_b", "L0_ffn_w1", "L0_ffn_w2", "L0_ffn_w3", "L1_gnn_rel_emb",
        "L1_gnn_weight_neighbor", "L1_gnn_a", "L1_gnn_W3", "L1_gnn_loop_weight", "L1_gnn_evolve_loop_weight",
        "L1_ffn_attention_mask", "L1_ffn_wr", "L1_ffn_br", "L1_ffn_w1", "L1_ffn_b1", "L1_ffn_w2", "L1_ffn_b2"]


def kernel(**inputs):
    import numpy as _np
    import concourse.bacc as _bacc
    from concourse import mybir as _mybir
    from concourse.bass_utils import run_bass_kernel_spmd as _run

    nc = _bacc.Bacc("TRN2", target_bir_lowering=False, num_devices=1)
    arrays, args = {}, {}
    for name in _INS:
        v = _np.ascontiguousarray(inputs[name])
        arrays[f"in_{name}_dram"] = v
        args[name] = nc.dram_tensor(f"in_{name}_dram", v.shape, _mybir.dt.from_np(v.dtype), kind="ExternalInput").ap()
    out = nc.dram_tensor("out_0_dram", (args["x"].shape[0], args["x"].shape[1]), F32, kind="ExternalOutput").ap()
    build(nc, args, out)
    r = _run(nc, [arrays], core_ids=[0])
    return r.results[0]["out_0_dram"]
```
